# Optimizing a Trainium2 kernel written in Bass

```python
import numpy as np
import jax
import jax.numpy as jnp

def _softmax(x, axis=-1):
    return jax.nn.softmax(x, axis=axis)
def _gelu(x):
    return jax.nn.gelu(x, approximate=True)
def _silu(x):
    return jax.nn.silu(x)
def _sigmoid(x):
    return jax.nn.sigmoid(x)
def _layernorm(x, axis=-1, eps=1e-5):
    m = jnp.mean(x, axis=axis, keepdims=True)
    v = jnp.var(x, axis=axis, keepdims=True)
    return (x - m) / jnp.sqrt(v + eps)
def _scatter_add(tgt, idx, src, axis=0):
    return tgt.at[idx].add(src)
def _segment_sum(src, seg, n):
    return jax.ops.segment_sum(src, seg, n)

kernel_name = 'mk_conv_preact_d2_conv_nhwc512_0394bb'

def setup_inputs(seed: int = 0):
    np.random.seed(seed)
    _w = jnp.asarray
    def _rec_inputs():
        import jax
        import jax.numpy as jnp
        _gk = jax.random.key(seed)
        x = -0.0006537 + 1.001 * jax.random.normal(jax.random.fold_in(_gk, 1), (2, 48, 48, 512), jnp.float32)
        return x
    x = _rec_inputs()
    def _L0_conv_setup():
        import jax, jax.numpy as jnp
        import numpy as np
        DIM = 512
        HEADS = 8
        HEAD_DIM = DIM // HEADS // 2
        KS = 7
        DIL = 1

        def _window_and_pb_start(length, ks):
            nh = ks // 2
            i = jnp.arange(length)
            ni = jnp.clip(i - nh, 0, length - ks)
            pi = nh + jnp.maximum(nh - i, 0) + jnp.where(i + nh >= length, length - i - 1 - nh, 0)
            return (ni, pi)

        def na_attention(qkv_na, rpb):
            B, H, W, _ = qkv_na.shape
            qkv = qkv_na.reshape(B, H, W, 3, HEADS, HEAD_DIM)
            qkv = jnp.transpose(qkv, (3, 0, 4, 1, 2, 5))
            q, k, v = (qkv[0], qkv[1], qkv[2])
            scale = HEAD_DIM ** (-0.5)
            ni, pi = _window_and_pb_start(H, KS)
            nj, pj = _window_and_pb_start(W, KS)
            off = jnp.arange(KS)
            idx_i = ni[:, None] + off[None, :]
            idx_j = nj[:, None] + off[None, :]
            kn = k[:, :, idx_i[:, None, :, None], idx_j[None, :, None, :], :]
            vn = v[:, :, idx_i[:, None, :, None], idx_j[None, :, None, :], :]
            bias_i = pi[:, None] + off[None, :]
            bias_j = pj[:, None] + off[None, :]
            bias = rpb[:, bias_i[:, None, :, None], bias_j[None, :, None, :]]
            attn = jnp.einsum('bhijd,bhijkld->bhijkl', q * scale, kn) + bias[None]
            a = attn.reshape(B, HEADS, H, W, KS * KS)
            a = jax.nn.softmax(a, axis=-1).reshape(B, HEADS, H, W, KS, KS)
            out = jnp.einsum('bhijkl,bhijkld->bhijd', a, vn)
            return jnp.transpose(out, (0, 2, 3, 1, 4)).reshape(B, H, W, HEADS * HEAD_DIM)

        def self_attention(qkv_self):
            B, H, W, _ = qkv_self.shape
            N = H * W
            qkv = qkv_self.reshape(B, N, 3, HEADS, HEAD_DIM)
            qkv = jnp.transpose(qkv, (2, 0, 3, 1, 4))
            q, k, v = (qkv[0], qkv[1], qkv[2])
            scale = HEAD_DIM ** (-0.5)
            scores = jnp.einsum('bhnd,bhmd->bhnm', q * scale, k)
            a = jax.nn.softmax(scores, axis=-1)
            out = jnp.einsum('bhnm,bhmd->bhnd', a, v)
            out = jnp.transpose(out, (0, 2, 1, 3)).reshape(B, H, W, HEADS * HEAD_DIM)
            return out
        key = jax.random.key(seed)
        ks = jax.random.split(key, 6)
        B, H, W = (2, 48, 48)
        x = jax.random.normal(ks[0], (B, H, W, DIM), dtype=jnp.float32)
        W_qkv = jax.random.normal(ks[1], (DIM, 3 * DIM), dtype=jnp.float32) * DIM ** (-0.5)
        b_qkv = jax.random.normal(ks[2], (3 * DIM,), dtype=jnp.float32) * 0.02
        rpb = jax.random.normal(ks[3], (HEADS, 2 * KS - 1, 2 * KS - 1), dtype=jnp.float32) * 0.02
        W_proj = jax.random.normal(ks[4], (DIM, DIM), dtype=jnp.float32) * DIM ** (-0.5)
        b_proj = jax.random.normal(ks[5], (DIM,), dtype=jnp.float32) * 0.02
        return {'x': x, 'W_qkv': W_qkv, 'b_qkv': b_qkv, 'rpb': rpb, 'W_proj': W_proj, 'b_proj': b_proj}
    _L0_conv_all = _L0_conv_setup()
    _L0_conv_in = {k: v for k, v in _L0_conv_all.items() if k in ('W_qkv', 'b_qkv', 'rpb', 'W_proj', 'b_proj', )}
    del _L0_conv_all

    def _L1_conv_setup():
        import jax, jax.numpy as jnp
        import numpy as np
        import math
        H = 8
        MAX_POS = 48
        MAX_PART = 16

        def _rel_bias(table, L, max_len):
            b = table[max_len - L:max_len + L - 1]
            idx = jnp.arange(L)
            rel = idx[None, :] - idx[:, None] + (L - 1)
            return jnp.transpose(b[rel], (2, 0, 1))
        key = jax.random.key(seed)
        ks = jax.random.split(key, 7)
        B, N, T, C = (16, 16, 48, 512)
        s = 0.02
        return {'x': jax.random.normal(ks[0], (B, N, T, C), jnp.float32), 'Wq': jax.random.normal(ks[1], (C, C), jnp.float32) * s, 'Wk': jax.random.normal(ks[2], (C, C), jnp.float32) * s, 'Wv': jax.random.normal(ks[3], (C, C), jnp.float32) * s, 'Wo': jax.random.normal(ks[4], (C, C), jnp.float32) * s, 'rel_pos_bias': jax.random.normal(ks[5], (2 * MAX_POS - 1, H), jnp.float32) * s, 'particle_rel_pos_bias': jax.random.normal(ks[6], (2 * MAX_PART - 1, H), jnp.float32) * s}
    _L1_conv_all = _L1_conv_setup()
    _L1_conv_in = {k: v for k, v in _L1_conv_all.items() if k in ('Wq', 'Wk', 'Wv', 'Wo', 'rel_pos_bias', 'particle_rel_pos_bias', )}
    del _L1_conv_all

    return {
        "x": x,
        "L0_conv_W_qkv": _L0_conv_in["W_qkv"],
        "L0_conv_b_qkv": _L0_conv_in["b_qkv"],
        "L0_conv_rpb": _L0_conv_in["rpb"],
        "L0_conv_W_proj": _L0_conv_in["W_proj"],
        "L0_conv_b_proj": _L0_conv_in["b_proj"],
        "L1_conv_Wq": _L1_conv_in["Wq"],
        "L1_conv_Wk": _L1_conv_in["Wk"],
        "L1_conv_Wv": _L1_conv_in["Wv"],
        "L1_conv_Wo": _L1_conv_in["Wo"],
        "L1_conv_rel_pos_bias": _L1_conv_in["rel_pos_bias"],
        "L1_conv_particle_rel_pos_bias": _L1_conv_in["particle_rel_pos_bias"],
    }

def reference(x, L0_conv_W_qkv, L0_conv_b_qkv, L0_conv_rpb, L0_conv_W_proj, L0_conv_b_proj, L1_conv_Wq, L1_conv_Wk, L1_conv_Wv, L1_conv_Wo, L1_conv_rel_pos_bias, L1_conv_particle_rel_pos_bias):
    import jax
    import jax.numpy as jnp
    def _L0_conv_ref(x, W_qkv, b_qkv, rpb, W_proj, b_proj):
        import jax, jax.numpy as jnp
        import numpy as np
        DIM = 512
        HEADS = 8
        HEAD_DIM = DIM // HEADS // 2
        KS = 7
        DIL = 1

        def _window_and_pb_start(length, ks):
            nh = ks // 2
            i = jnp.arange(length)
            ni = jnp.clip(i - nh, 0, length - ks)
            pi = nh + jnp.maximum(nh - i, 0) + jnp.where(i + nh >= length, length - i - 1 - nh, 0)
            return (ni, pi)

        def na_attention(qkv_na, rpb):
            B, H, W, _ = qkv_na.shape
            qkv = qkv_na.reshape(B, H, W, 3, HEADS, HEAD_DIM)
            qkv = jnp.transpose(qkv, (3, 0, 4, 1, 2, 5))
            q, k, v = (qkv[0], qkv[1], qkv[2])
            scale = HEAD_DIM ** (-0.5)
            ni, pi = _window_and_pb_start(H, KS)
            nj, pj = _window_and_pb_start(W, KS)
            off = jnp.arange(KS)
            idx_i = ni[:, None] + off[None, :]
            idx_j = nj[:, None] + off[None, :]
            kn = k[:, :, idx_i[:, None, :, None], idx_j[None, :, None, :], :]
            vn = v[:, :, idx_i[:, None, :, None], idx_j[None, :, None, :], :]
            bias_i = pi[:, None] + off[None, :]
            bias_j = pj[:, None] + off[None, :]
            bias = rpb[:, bias_i[:, None, :, None], bias_j[None, :, None, :]]
            attn = jnp.einsum('bhijd,bhijkld->bhijkl', q * scale, kn) + bias[None]
            a = attn.reshape(B, HEADS, H, W, KS * KS)
            a = jax.nn.softmax(a, axis=-1).reshape(B, HEADS, H, W, KS, KS)
            out = jnp.einsum('bhijkl,bhijkld->bhijd', a, vn)
            return jnp.transpose(out, (0, 2, 3, 1, 4)).reshape(B, H, W, HEADS * HEAD_DIM)

        def self_attention(qkv_self):
            B, H, W, _ = qkv_self.shape
            N = H * W
            qkv = qkv_self.reshape(B, N, 3, HEADS, HEAD_DIM)
            qkv = jnp.transpose(qkv, (2, 0, 3, 1, 4))
            q, k, v = (qkv[0], qkv[1], qkv[2])
            scale = HEAD_DIM ** (-0.5)
            scores = jnp.einsum('bhnd,bhmd->bhnm', q * scale, k)
            a = jax.nn.softmax(scores, axis=-1)
            out = jnp.einsum('bhnm,bhmd->bhnd', a, v)
            out = jnp.transpose(out, (0, 2, 1, 3)).reshape(B, H, W, HEADS * HEAD_DIM)
            return out
        B, H, W, C = x.shape
        qkv = x @ W_qkv + b_qkv
        qkv_na, qkv_self = (qkv[..., :3 * C // 2], qkv[..., 3 * C // 2:])
        x_na = na_attention(qkv_na, rpb)
        x_self = self_attention(qkv_self)
        out = jnp.concatenate([x_na, x_self], axis=-1) @ W_proj + b_proj
        return out

    def _L1_conv_ref(x, Wq, Wk, Wv, Wo, rel_pos_bias, particle_rel_pos_bias):
        import jax, jax.numpy as jnp
        import numpy as np
        import math
        H = 8
        MAX_POS = 48
        MAX_PART = 16

        def _rel_bias(table, L, max_len):
            b = table[max_len - L:max_len + L - 1]
            idx = jnp.arange(L)
            rel = idx[None, :] - idx[:, None] + (L - 1)
            return jnp.transpose(b[rel], (2, 0, 1))
        B, N, T, C = x.shape
        hd = C // H
        L = N * T
        xf = x.reshape(B, L, C)
        q = (xf @ Wq).reshape(B, L, H, hd).transpose(0, 2, 1, 3)
        k = (xf @ Wk).reshape(B, L, H, hd).transpose(0, 2, 1, 3)
        v = (xf @ Wv).reshape(B, L, H, hd).transpose(0, 2, 1, 3)
        att = jnp.einsum('bhqd,bhkd->bhqk', q, k) * (1.0 / math.sqrt(hd))
        att = att.reshape(B, H, N, T, N, T)
        bias_t = _rel_bias(rel_pos_bias, T, MAX_POS).reshape(1, H, 1, T, 1, T)
        bias_p = _rel_bias(particle_rel_pos_bias, N, MAX_PART).reshape(1, H, N, 1, N, 1)
        att = att + bias_t + bias_p
        causal = jnp.tril(jnp.ones((T, T), dtype=bool))
        att = jnp.where(causal[None, None, None, :, None, :], att, -jnp.inf)
        att = jax.nn.softmax(att.reshape(B, H, L, L), axis=-1)
        y = att @ v
        y = y.transpose(0, 2, 1, 3).reshape(B, L, C) @ Wo
        return y.reshape(B, N, T, C)

    def _gn(v, G=32, eps=1e-5):
        B_, H_, W_, C_ = v.shape
        g = v.reshape(B_, H_, W_, G, C_ // G)
        m = jnp.mean(g, axis=(1, 2, 4), keepdims=True)
        s = jnp.var(g, axis=(1, 2, 4), keepdims=True)
        return ((g - m) / jnp.sqrt(s + eps)).reshape(v.shape)

    def _ln_c(v, eps=1e-6):
        m = jnp.mean(v, axis=-1, keepdims=True)
        s = jnp.var(v, axis=-1, keepdims=True)
        return (v - m) / jnp.sqrt(s + eps)

    def _ln_t(v, eps=1e-5):
        m = jnp.mean(v, axis=-1, keepdims=True)
        s = jnp.var(v, axis=-1, keepdims=True)
        return (v - m) / jnp.sqrt(s + eps)

    def _to_tokens(v):
        B_, H_, W_, C_ = v.shape
        return v.reshape(B_, H_ * W_, C_)
    def _from_tokens(t, like):
        return t.reshape(like.shape)

    x = x + _L0_conv_ref(_gn(x), L0_conv_W_qkv, L0_conv_b_qkv, L0_conv_rpb, L0_conv_W_proj, L0_conv_b_proj)
    x = x + _L1_conv_ref(_gn(x), L1_conv_Wq, L1_conv_Wk, L1_conv_Wv, L1_conv_Wo, L1_conv_rel_pos_bias, L1_conv_particle_rel_pos_bias)
    return x


_drawn_inputs = setup_inputs


def setup_inputs(seed=0):
    import zlib

    import numpy as np

    out = dict(_drawn_inputs(seed))
    spreads = {}
    factors = {'L0_conv_rpb': 8.0,
     'L0_conv_b_proj': 2.749,
     'L1_conv_Wq': 8.0,
     'L1_conv_Wk': 8.0,
     'L1_conv_Wv': 4.591,
     'L1_conv_Wo': 4.702,
     'L1_conv_rel_pos_bias': 8.0,
     'L1_conv_particle_rel_pos_bias': 8.0}
    for name, (base, spread) in spreads.items():
        noise = np.random.default_rng([zlib.crc32(name.encode()), seed]).standard_normal(out[name].shape)
        drawn = base * np.exp(spread * noise) if base else spread * noise
        out[name] = jnp.asarray(drawn.astype(out[name].dtype))
    for name, factor in factors.items():
        out[name] = (out[name] * factor).astype(out[name].dtype)
    return out
```

```python
from contextlib import ExitStack

import numpy as np
import concourse.bass as bass
from concourse import mybir

F32 = mybir.dt.float32
F32R = mybir.dt.float32r
ALU = mybir.AluOpType
ACT = mybir.ActivationFunctionType
AX = mybir.AxisListType

B = 2
HW = 48
T = HW * HW
C = 512
P = 128
KC = C // P
NT = T // P
CH = 384
NCH = T // CH
EPS = 1e-5
BIG = 1e30

D0 = 32
H0 = P // D0
G0 = 2
SCALE0 = float(D0) ** -0.5
KS = 7
QR, QW = 8, 16
BR, BW = 4, 22
BAND = BR * BW
NB = HW // BR
CW = HW // QW
COL0 = [0, 13, 26]
QT_NA = NT
RPB = 2 * KS - 1
PADR, PADC = 23, 43
OFFR, OFFC = 5, 15
TTW = 16 * 28
RUN = 15 * PADC + 28
RUNP = 16 * PADC

D1 = 64
H1 = P // D1
G1 = 4
HEADS1 = 8
SCALE1 = float(D1) ** -0.5
NU = HW + 3
KGW = NU * HW

NG = 2 * G0 + G1
CREDIT = 8
RING = 4


def chunks_of(keys):
    return [(c, min(512, keys - c)) for c in range(0, keys, 512)]


SELF_CHUNKS = chunks_of(T)
NC0 = len(SELF_CHUNKS)


def causal_keys(i):
    return ((P * (i + 1) - 1) // HW + 1) * HW


L1_CHUNKS = [chunks_of(causal_keys(i)) for i in range(NT)]
L1_PER_HEAD = sum(len(c) for c in L1_CHUNKS)

EVA0 = (0, 2)
EVC, EVC_TOTAL = {}, {"a": 0, "d": 0}
for _n in range(H1 * NT):
    for _c in range(len(L1_CHUNKS[_n % NT])):
        _who = "a" if len(EVC) % 5 in (0, 2) else "d"
        EVC[_n, _c] = (_who, len(EVC) % 2)
        EVC_TOTAL[_who] += 1


def na_tiles():
    out = []
    for cw in range(CW):
        for rt in range(HW // QR):
            lo = max(QR * rt - BR, 0) // BR
            hi = min(QR * rt + QR + BR, HW) // BR
            cls = 0 if rt == 0 else 2 if rt == HW // QR - 1 else 1
            out.append((rt * CW + cw, cw, cls, lo, hi - lo))
    return out


NA_TILES = na_tiles()
NA_TABLES = []
NA_TABLE_OF = []
for _n, (_t, _cw, _cls, _lo, _nb) in enumerate(NA_TILES):
    if not NA_TABLES or NA_TABLES[-1][:2] != (_cw, _cls):
        NA_TABLES.append((_cw, _cls, _nb, _n))
    NA_TABLE_OF.append(len(NA_TABLES) - 1)
NTAB = len(NA_TABLES)
V_RING = T // (KC * BAND)
TAB_RING = 3


def build(nc, a):
    ctx = ExitStack()
    with ctx:
        def sb(name, shape, dt=F32):
            return ctx.enter_context(nc.sbuf_tensor(name, shape, dt))

        def sem(name):
            return ctx.enter_context(nc.semaphore(name))

        def overlay(*choices):
            made, largest = [], max(choices, key=lambda c: sum(int(np.prod(s[1][1:])) for s in c))
            for c in choices:
                if c is not largest:
                    with ExitStack() as scope:
                        made += [scope.enter_context(nc.sbuf_tensor(n, s, d)) for n, s, d in c]
            made += [sb(n, s, d) for n, s, d in largest]
            return {t.name: t for t in made}

        def dram(name, shape):
            return nc.dram_tensor(name, shape, F32).ap()

        res_d = dram("res_d", (P, KC, T))
        rpb_d = dram("rpb_d", (8, PADR, PADC))
        tt_d = dram("tt_d", (8, P, TTW))
        part_d = dram("part_d", (8, 2 * HW - 1))

        XN = sb("XN", [P, KC, T])
        YT = sb("YT", [P, NT, C])
        QH, QL = sb("QH", [P, T], F32R), sb("QL", [P, T], F32R)
        KH, KL = sb("KH", [P, T], F32R), sb("KL", [P, T], F32R)
        o = overlay([("KST", [P, 2, T], F32R), ("QS", [P, 2, T], F32R)],
                    [("yT", [P, 2, KC, CH], F32)])
        KST, QS, yT = o["KST"], o["QS"], o["yT"]
        o = overlay([("Vb", [P, CW * NB, P], F32)],
                    [("V", [P, NT, P], F32), ("KG1", [P, KGW], F32R)],
                    [("res", [P, 2, CH], F32)])
        Vb, V, KG1, res = o["Vb"], o["V"], o["KG1"], o["res"]
        o = overlay([("KG0", [P, KGW], F32R)],
                    [("TT", [P, 2, 16, 28], F32), ("tmpt", [P, 16, 28], F32),
                     ("tab", [P, TAB_RING, 16, BW], F32)])
        KG0, TT, tmpt, tab = o["KG0"], o["TT"], o["tmpt"], o["tab"]
        KG = [KG0, KG1]
        Wg = sb("Wg", [P, KC, 3 * P])
        Wo = sb("Wo", [P, KC, C])
        Pb = sb("Pb", [P, T])
        PT = sb("PT", [P, 2, 512])
        ident = sb("ident", [P, P])
        avg = sb("avg", [P, P])
        qoh = sb("qoh", [P, 3, P], F32R)
        PS = sb("PS", [P, 8, HW])
        TS = sb("TS", [P, 8, NU])
        rowm = sb("rowm", [P, 3, 16])
        colm = sb("colm", [P, 3, BW])
        bqkv = sb("bqkv", [P, 2 * G0, 3])
        bproj = sb("bproj", [P, KC])
        epst = sb("epst", [P, 1])
        st = sb("st", [P, NCH, 6])
        mv = sb("mv", [P, KC, 2])
        gm = sb("gm", [P, KC])
        dv = sb("dv", [P, KC])
        sd = sb("sd", [P, KC])
        rstd = sb("rstd", [P, KC])
        cmax = sb("cmax", [P, 8])
        nmax = sb("nmax", [P, RING])
        rsum = sb("rsum", [P, RING, 8])
        den = sb("den", [P, 2])
        rden = sb("rden", [P, RING])
        bsel = sb("bsel", [P, 3])

        SC = ctx.enter_context(nc.psum_tensor("SC", [P, 5 * 512], F32))
        TP = ctx.enter_context(nc.psum_tensor("TP", [P, 2, 512], F32))
        OV = ctx.enter_context(nc.psum_tensor("OV", [P, 512], F32))
        OV_NA = [OV[:, 0:D0], SC[:, 4 * 512:4 * 512 + D0]]

        s_bar = sem("s_bar")
        s_held = sem("s_held")
        s_const = sem("s_const")
        s_dram = sem("s_dram")
        s_set = sem("s_set")
        s_setp = sem("s_setp")
        s_x = sem("s_x")
        s_xt = sem("s_xt")
        s_xe = sem("s_xe")
        s_save = sem("s_save")
        s_st = sem("s_st")
        s_bn = sem("s_bn")
        s_sqr = sem("s_sqr")
        s_vd = sem("s_vd")
        s_bs = sem("s_bs")
        s_gp = sem("s_gp")
        s_sq = sem("s_sq")
        s_w = sem("s_w")
        s_ws = sem("s_ws")
        s_wo = sem("s_wo")
        s_pq = sem("s_pq")
        s_hi = sem("s_hi")
        s_lo = sem("s_lo")
        s_vw = sem("s_vw")
        s_pv = sem("s_pv")
        s_pe = sem("s_pe")
        s_stk = [sem(f"s_stk{i}") for i in range(2)]
        n_tt = [sem(f"n_tt{i}") for i in range(2)]
        n_tmp = sem("n_tmp")
        n_tab = sem("n_tab")
        n_sc = sem("n_sc")
        n_ad = sem("n_ad")
        n_nm = sem("n_nm")
        n_ex = sem("n_ex")
        n_tp = sem("n_tp")
        n_ev = sem("n_ev")
        n_pv = sem("n_pv")
        n_rd = sem("n_rd")
        n_nr = sem("n_nr")
        dense = {}
        for k in "fc":
            dense[k] = {n: sem(f"{k}_{n}") for n in
                        ("q0",
                         "q1",
                         "sc",
                         "cm",
                         "nm",
                         "ex",
                         "tp",
                         "eva",
                         "evd",
                         "pv",
                         "dn",
                         "rd",
                         "nr")}
        c_kg = sem("c_kg")
        s_op = sem("s_op")
        s_oy = sem("s_oy")
        s_om = sem("s_om")
        s_or = [sem(f"s_or{i}") for i in range(2)]
        s_oa = sem("s_oa")
        s_ft = sem("s_ft")
        s_fe = sem("s_fe")
        s_out = sem("s_out")

        block = ctx.enter_context(nc.Block())

        ENGINES = 5
        PH = 2 + 2 * G0 + 2 * G0 + 2 + 2 * G1 + 2

        def hold(eng, semaphore, value):
            eng.wait_ge(semaphore, value)
            eng.sem_inc(s_held, 1)

        def phase_end(eng, n):
            eng.drain().then_inc(s_bar, 1)
            hold(eng, s_bar, ENGINES * n)

        def run_phases(eng, setup, load, norm, proj, na, selfa, causal, outp, final):
            setup()
            phase_end(eng, 1)
            with eng.Fori(0, B) as b:
                ph = b * PH + 1
                load(b)
                phase_end(eng, ph + 1)
                norm(b, 0)
                phase_end(eng, ph + 2)
                with eng.Fori(0, G0) as g:
                    proj("na", b, g)
                    phase_end(eng, ph + g * 2 + 3)
                    na(b, g)
                    phase_end(eng, ph + g * 2 + 4)
                with eng.Fori(0, G0) as g:
                    proj("self", b, g)
                    phase_end(eng, ph + g * 2 + (3 + 2 * G0))
                    selfa(b, g)
                    phase_end(eng, ph + g * 2 + (4 + 2 * G0))
                outp(b, 0)
                phase_end(eng, ph + (3 + 4 * G0))
                norm(b, 1)
                phase_end(eng, ph + (4 + 4 * G0))
                with eng.Fori(0, G1) as g:
                    proj("causal", b, g)
                    phase_end(eng, ph + g * 2 + (5 + 4 * G0))
                    causal(b, g)
                    phase_end(eng, ph + g * 2 + (6 + 4 * G0))
                outp(b, 1)
                phase_end(eng, ph + (5 + 4 * G0 + 2 * G1))
                final(b)
                phase_end(eng, ph + (6 + 4 * G0 + 2 * G1))

        def nothing(*_):
            pass

        def group_index(kind, b, g):
            return b * NG + g + {"na": 0, "self": G0, "causal": 2 * G0}[kind]

        def v_banks(kind):
            n = CW * NB if kind == "na" else NT
            return [(t, min(4, n - t)) for t in range(0, n, 4)]

        V_IMG = G0 * len(v_banks("na")) + (G0 + G1) * len(v_banks("self"))

        def band_tokens(t):
            return Pb[:, (t % V_RING) * KC * BAND:(t % V_RING + 1) * KC * BAND].rearrange(
                "p (k n) -> p k n", k=KC)

        def v_base(kind, b, g):
            per = len(v_banks(kind))
            return b * V_IMG + g * per + {"na": 0, "self": G0 * len(v_banks("na")),
                                          "causal": G0 * (len(v_banks("na")) + per)}[kind]

        STK_NA, STK_SELF, STK_C = 8 * 16, 4 * 16, 4 * 16
        STK_IMG = G0 * H0 // 2 * (STK_NA + STK_SELF) + G1 * H1 // 2 * STK_C

        def stk_base(kind, b, g):
            return b * STK_IMG + {
                "na": g * (H0 // 2 * STK_NA),
                "self": g * (H0 // 2 * STK_SELF) + G0 * H0 // 2 * STK_NA,
                "causal": g * (H1 // 2 * STK_C) + G0 * H0 // 2 * (STK_NA + STK_SELF)}[kind]

        @block.sync
        def _(sp):
            def setup():
                consts = [(ident, a["ident"]), (avg, a["avg"]), (rowm, a["rowm"]), (colm, a["colm"]),
                          (bqkv, a["bqkv"]), (bproj, a["bproj"])]
                for dst, src in consts:
                    sp.dma_start(dst.ap(), src).then_inc(s_const, 16)
                sp.dma_start(YT[:, 0, 0:3 * P], a["qoh"]).then_inc(s_const, 16)
                sp.dma_start(YT[:, 1, 0:P], a["rev"]).then_inc(s_const, 16)
                sp.dma_start(YT[:, 2, 0:NU], a["tmask"]).then_inc(s_const, 16)
                n = a["relp"].shape[1]
                sp.dma_start(YT[0:8, 14, 0:n], a["relp"]).then_inc(s_const, 16)
                sp.wait_ge(s_set, 1)
                sp.dma_start(rpb_d, XN[0:8, 0, 0:PADR * PADC].rearrange("h (r c) -> h r c", c=PADC))\
                    .then_inc(s_dram, 16)
                sp.wait_ge(s_dram, 16)
                sp.dma_start(rpb_d[:, OFFR:OFFR + RPB, OFFC:OFFC + RPB], a["rpb"]).then_inc(s_dram, 16)
                sp.wait_ge(s_set, 2)
                sp.dma_start(part_d, YT[0:8, 14, 0:2 * HW - 1]).then_inc(s_dram, 16)
                sp.wait_ge(s_dram, 48)
                for h in range(8):
                    src = bass.AP(rpb_d.tensor, h * PADR * PADC, [[PADC, QR], [1, QW], [1, RUN]])
                    sp.dma_start(XN[:, 1 + h // 3, (h % 3) * RUNP:(h % 3) * RUNP + RUN], src).then_inc(s_dram, 16)
                for base in (0, 64):
                    src = bass.AP(part_d.tensor, 0, [[1, HW], [2 * HW - 1, 8], [1, HW]])
                    sp.dma_start(YT[base:base + HW, 15, 0:8 * HW].rearrange("p (h n) -> p h n", h=8), src)\
                        .then_inc(s_dram, 16)
                    for r in range(4):
                        u = 3 - r
                        dst = YT[base + HW + r:base + HW + r + 1, 3, 0:8 * NU].rearrange(
                            "p (h n) -> p h n", h=8)[:, :, u:NU]
                        sp.dma_start(dst, a["relt"][:, 0:NU - u].rearrange("(o h) n -> o h n", o=1))\
                            .then_inc(s_dram, 16)
                sp.wait_ge(s_set, 4)
                for h in range(8):
                    sp.dma_start(tt_d[h], YT[:, 4 + h, 0:TTW]).then_inc(s_dram, 16)
                sp.wait_ge(s_dram, 16 * (3 + 8 + 10 + 8))

            def load(b):
                for part in range(3):
                    w = NT // 3
                    src = a["x"][bass.ds(b, 1), part * w * P:(part + 1) * w * P, :].rearrange(
                        "o (t p) c -> p (o t) c", p=P)
                    sp.dma_start(YT[:, part * w:(part + 1) * w, :], src).then_inc(s_x, 16)
                hold(sp, s_x, b * 48 + 48)

            def norm(b, layer):
                sp.dma_start(res_d, XN.ap()).then_inc(s_save, 16)
                sp.dma_start(Wo.ap(), a["wo"][layer]).then_inc(s_wo, 16)
                hold(sp, s_save, b * 32 + 16 * (layer + 1))
                hold(sp, s_wo, b * 32 + 16 * (layer + 1))

            def proj(kind, b, g):
                off = {"na": 0, "self": G0, "causal": 2 * G0}[kind]
                sp.dma_start(Wg.ap(), a["wgrp"][bass.ds(g + off, 1)].rearrange("o p k n -> p (o k) n"))\
                    .then_inc(s_w, 16)
                hold(sp, s_w, group_index(kind, b, g) * 16 + 16)

            def stack(j, slot, with_q):
                r = slice(D0 * j, D0 * j + D0)
                for i, src in enumerate((KH, KL, KH, KL)):
                    sp.dma_start(KST[D0 * i:D0 * i + D0, slot, :].bitcast(F32), src[r, :].bitcast(F32))\
                        .then_inc(s_stk[slot], 16)
                if with_q:
                    for i, src in enumerate((QH, QH, QL, QL)):
                        sp.dma_start(QS[D0 * i:D0 * i + D0, slot, :].bitcast(F32), src[r, :].bitcast(F32))\
                            .then_inc(s_stk[slot], 16)

            def stacks_end(kind, b, g, each):
                for slot in range(2):
                    hold(sp, s_stk[slot], stk_base(kind, b, g) + each)

            def na(b, g):
                n0 = b * (G0 * H0 * NT) + g * (H0 * NT)
                h0 = b * (G0 * H0) + g * H0
                for j in range(H0):
                    if j >= 2:
                        hold(sp, n_sc, n0 + NT * (j - 1))
                        hold(sp, n_tab, (h0 + (j - 1)) * NTAB)
                    stack(j, j % 2, True)
                    sp.dma_start(TT[:, j % 2], tt_d[bass.ds(g * H0 + j, 1)].rearrange(
                        "o p (r c) -> p (o r) c", c=28)).then_inc(n_tt[j % 2], 16)
                stacks_end("na", b, g, H0 // 2 * STK_NA)
                for slot in range(2):
                    hold(sp, n_tt[slot], (b * G0 + g + 1) * (H0 // 2 * 16))

            def selfa(b, g):
                s = dense["f"]
                t0 = (b * G0 + g) * (H0 * NT)

                def queries(j, i, waits=True):
                    r = slice(D0 * j, D0 * j + D0)
                    for e in range(2):
                        if waits:
                            hold(sp, s["sc"], (t0 + i * 2 + (NT * j + e - 1)) * NC0)
                        for k, src in enumerate((QH, QH, QL, QL)):
                            sp.dma_start(QS[D0 * k:D0 * k + D0, 0, e * P:(e + 1) * P].bitcast(F32),
                                         src[r, bass.ds(i * 2 * P + e * P, P)].bitcast(F32))\
                                .then_inc(s[f"q{e}"], 16)

                queries(0, 0, waits=False)
                stack(0, 0, False)
                for j in range(H0):
                    if j:
                        queries(j, 0)
                    queries(j, 1)
                    if j + 1 < H0:
                        stack(j + 1, (j + 1) % 2, False)
                    with sp.Fori(2, NT // 2) as i:
                        queries(j, i)
                stacks_end("self", b, g, H0 // 2 * STK_SELF)
                for e in range(2):
                    hold(sp, s[f"q{e}"], (t0 + H0 * NT) * 32)

            def causal(b, g):
                for j in range(H1):
                    r = slice(D1 * j, D1 * j + D1)
                    for i, src in enumerate((KH, KL)):
                        sp.dma_start(KST[D1 * i:D1 * i + D1, j, :].bitcast(F32), src[r, :].bitcast(F32))\
                            .then_inc(s_stk[j], 16)
                    for i in range(2):
                        sp.dma_start(QS[D1 * i:D1 * i + D1, j, :].bitcast(F32), QH[r, :].bitcast(F32))\
                            .then_inc(s_stk[j], 16)
                stacks_end("causal", b, g, H1 // 2 * STK_C)

            def outp(b, layer):
                n0 = b * (2 * NCH * KC) + layer * NCH * KC
                for c in range(NCH):
                    for m in range(KC):
                        n = c * KC + m
                        hold(sp, s_oa, n0 + (CREDIT + n - 1))
                        sp.dma_start(res[:, n % 2, :], res_d[:, m, c * CH:(c + 1) * CH])\
                            .then_inc(s_or[n % 2], 16)
                for slot in range(2):
                    hold(sp, s_or[slot], (n0 + NCH * KC) * 8)

            def final(b):
                for part in range(3):
                    w = NT // 3
                    hold(sp, s_fe, b * NT + (part + 1) * w)
                    dst = a["out"][bass.ds(b, 1), part * w * P:(part + 1) * w * P, :].rearrange(
                        "o (t p) c -> p (o t) c", p=P)
                    sp.dma_start(dst, YT[:, part * w:(part + 1) * w, :]).then_inc(s_out, 16)
                hold(sp, s_out, b * 48 + 48)

            run_phases(sp, setup, load, norm, proj, na, selfa, causal, outp, final)

        @block.tensor
        def _(pe):
            def mm(*args, **kw):
                return nc.tensor.matmul(*args, skip_group_check=True, **kw)

            def setup():
                pe.wait_ge(s_const, 16 * 10)
                pe.wait_ge(s_dram, 16 * (3 + 8 + 10))
                for n in range(2):
                    for i in range(4):
                        h = 4 * n + i
                        table = XN[:, 1 + h // 3, (h % 3) * RUNP:(h % 3 + 1) * RUNP].rearrange(
                            "p (r c) -> p r c", c=PADC)[:, :, 0:28]
                        mm(SC[:, i * 512:i * 512 + TTW], YT[:, 1, 0:P], table, start=True, stop=True)\
                            .then_inc(s_setp, 1)
                    if n == 0:
                        pe.wait_ge(s_set, 3)

            def load(b):
                pe.wait_ge(s_x, b * 48 + 48)
                for t in range(NT):
                    pe.wait_ge(s_xe, b * NT + (CREDIT + t - 1))
                    for k in range(KC):
                        last = nc.tensor.transpose(TP[:, t % 2, k * P:(k + 1) * P],
                                                   YT[:, t, k * P:(k + 1) * P], ident[:, :])
                    last.then_inc(s_xt, 1)

            def norm(b, layer):
                d0 = b * 2 + layer
                pe.wait_ge(s_st, d0 * 6 + 1)
                mm(SC[:, 0:KC], avg[:, :], mv[:, :, 0], start=True, stop=True).then_inc(s_gp, 1)
                pe.wait_ge(s_st, d0 * 6 + 4)
                mm(SC[:, 512:512 + KC], avg[:, :], dv[:, :], start=True, stop=True).then_inc(s_gp, 1)

            def proj(kind, b, g):
                gi = group_index(kind, b, g)
                pe.wait_ge(s_w, gi * 16 + 16)
                for c in range(NCH):
                    for m in (1, 0):
                        n = 2 * c + (1 - m)
                        if n == 1:
                            pe.wait_ge(s_ws, gi + 1)
                        if n >= 3:
                            pe.wait_ge(s_lo, gi * (2 * NCH) + (n - 2))
                        for k in range(KC):
                            last = mm(SC[:, (n % 3) * 512:(n % 3) * 512 + CH], Wg[:, k, m * P:(m + 1) * P],
                                      XN[:, k, c * CH:(c + 1) * CH], start=(k == 0), stop=(k == KC - 1))
                        last.then_inc(s_pq, 1)
                v0 = v_base(kind, b, g)
                for n, (t0, w) in enumerate(v_banks(kind)):
                    if n >= 2:
                        pe.wait_ge(s_pe, v0 + (n - 1))
                    bank = SC[:, (3 + n % 2) * 512:(4 + n % 2) * 512]
                    for i in range(w):
                        t = t0 + i
                        if kind == "na":
                            pe.wait_ge(s_vw, (b * G0 + g) * (CW * NB) + (t + 1))
                        for k in range(KC):
                            if kind == "na":
                                tok = band_tokens(t)[:, k, :]
                                rows = BAND
                            else:
                                tok = XN[:, k, t * P:(t + 1) * P]
                                rows = P
                            last = mm(bank[0:rows, i * P:(i + 1) * P], tok, Wg[:, k, 2 * P:3 * P],
                                      start=(k == 0 and i == 0), stop=(k == KC - 1))
                    last.then_inc(s_pv, 1)

            def na(b, g):
                n0 = b * (G0 * H0 * NT) + g * (H0 * NT)
                with pe.Fori(0, H0 // 2) as hp:
                    m0 = n0 + hp * (2 * NT)
                    total = 2 * NT

                    def scores(n, base=0):
                        slot, (t, cw, cls, lo, nb) = (n // NT) % 2, NA_TILES[n % NT]
                        if n % NT == 0:
                            pe.wait_ge(s_stk[slot], stk_base("na", b, g) + hp * STK_NA + STK_NA)
                        pe.wait_ge(n_ad, m0 + (CREDIT + n - RING + 1))
                        keys = KST[:, slot, :].rearrange("p (r c) -> p r c", c=HW)[
                            :, lo * BR:(lo + nb) * BR, COL0[cw]:COL0[cw] + BW]
                        bank = SC[:, (n % RING) * 512:(n % RING) * 512 + nb * BAND]
                        mm(bank, QS[:, slot, t * P:(t + 1) * P], keys, start=True, stop=True)\
                            .then_inc(n_sc, 1)

                    def pv(n):
                        t, cw, cls, lo, nb = NA_TILES[n % NT]
                        pe.wait_ge(n_ev, m0 + (n + 1))
                        pe.wait_ge(n_nr, m0 + (CREDIT + n - 1))
                        for k in range(nb):
                            last = mm(OV_NA[n % 2], PT[0:BAND, n % 2, k * P:(k + 1) * P],
                                      Vb[0:BAND, cw * NB + lo + k, bass.ds(hp * (2 * D0) + (n // NT) * D0, D0)],
                                      start=(k == 0), stop=(k == nb - 1))
                        last.then_inc(n_pv, 1)

                    for n in range(2):
                        scores(n)
                    for n in range(total):
                        if n + 2 < total:
                            scores(n + 2)
                        pe.wait_ge(n_ex, m0 + (n + 1))
                        nb = NA_TILES[n % NT][4]
                        for k in range(nb):
                            last = nc.tensor.transpose(TP[0:BAND, n % 2, k * P:(k + 1) * P],
                                                       Pb[:, (n % 4) * 512 + k * BAND:(n % 4) * 512 + (k + 1) * BAND],
                                                       ident[:, :])
                        last.then_inc(n_tp, 1)
                        if n >= 1:
                            pv(n - 1)
                    pv(total - 1)

            def transposes(chunk, slot, s, at):
                k0, w = chunk
                for k in range(0, w, P):
                    r = min(P, w - k)
                    last = nc.tensor.transpose(TP[0:r, slot, k:k + P], Pb[:, k0 + k:k0 + k + r], ident[:, :])
                last.then_inc(s["tp"], 1)

            def selfa(b, g):
                s = dense["f"]
                t0 = (b * G0 + g) * (H0 * NT)
                k0 = stk_base("self", b, g)

                def scores(t, head, e, c):
                    if c == 0:
                        pe.wait_ge(s[f"q{e}"], (t0 + t - e) * 32 + 64)
                        for slot in range(2):
                            pe.wait_ge(s_stk[slot], k0 + (head + 1 + (1 - slot)) // 2 * STK_SELF)
                    o, w = SELF_CHUNKS[c]
                    ins = mm(SC[:, o:o + w], QS[:, 0, e * P:(e + 1) * P], KST.ap().rearrange(
                        "p s t -> p (s t)")[:, bass.ds((head % 2) * T + o, w)], start=True, stop=True)
                    ins.then_inc(s["sc"], 1)

                def pv(t, head, e, c, n_a, n_d):
                    if c == 0:
                        pe.wait_ge(s["nr"], t0 + t + CREDIT)
                    if c in EVA0:
                        pe.wait_ge(s["eva"], n_a)
                    else:
                        pe.wait_ge(s["evd"], n_d)
                    o, w = SELF_CHUNKS[c]
                    for k in range(0, w, P):
                        last = mm(OV[:, 0:D0], PT[:, (e * NC0 + c) % 2, k:k + P],
                                  V[:, (o + k) // P, bass.ds(head * D0, D0)],
                                  start=(o + k == 0), stop=(o + k == T - P))
                    if c == NC0 - 1:
                        last.then_inc(s["pv"], 1)

                def counts(t, c):
                    na_ = sum(1 for x in EVA0 if x <= c)
                    return (t0 + t) * len(EVA0) + na_, (t0 + t) * (NC0 - len(EVA0)) + (c + 1 - na_)

                def pair(i, first, last):
                    for e in range(2):
                        t = i * 2 + e
                        head = t // NT
                        for c in range(NC0):
                            pe.wait_ge(s["ex"], (t0 + t) * NC0 + (c + 1))
                            transposes(SELF_CHUNKS[c], (e * NC0 + c) % 2, s, None)
                            if not (last and e == 1):
                                scores(t + 1, (t + 1) // NT, 1 - e, c)
                            if c > 0:
                                pv(t, head, e, c - 1, *counts(t, c - 1))
                            elif not (first and e == 0):
                                pv(t - 1, (t - 1) // NT, 1 - e, NC0 - 1, *counts(t - 1, NC0 - 1))

                pairs = H0 * NT // 2
                for c in range(NC0):
                    scores(0, 0, 0, c)
                pair(0, True, False)
                with pe.Fori(1, pairs - 1) as i:
                    pair(i, False, False)
                pair(pairs - 1, False, True)
                t = H0 * NT - 1
                pv(t, H0 - 1, 1, NC0 - 1, *counts(t, NC0 - 1))

            def causal(b, g):
                s = dense["c"]
                gi = b * G1 + g
                tiles = [(j, i) for j in range(H1) for i in range(NT)]
                sc0 = gi * (H1 * L1_PER_HEAD)
                t0 = gi * (H1 * NT)
                ex = 0
                ev = {"a": 0, "d": 0}

                def scores(n, c):
                    j, i = tiles[n]
                    o, w = L1_CHUNKS[i][c]
                    if i == 0 and c == 0:
                        pe.wait_ge(s_stk[j], stk_base("causal", b, g) + STK_C)
                        pe.wait_ge(c_kg, gi * H1 + (j + 1))
                    r = slice(D1 * j, D1 * j + D1)
                    q = slice(i * P, (i + 1) * P)
                    bank = SC[:, o:o + w]
                    u = (HW - 1 - i * P // HW) * HW + o
                    mm(bank, QS[:, j, q], KST[:, j, o:o + w], start=True, stop=False)
                    mm(bank, QL[r, q], KH[r, o:o + w], start=False, stop=False)
                    mm(bank, qoh[:, i % 3, :], KG[j][:, u:u + w], start=False, stop=True)\
                        .then_inc(s["sc"], 1)

                def pv(n, c):
                    j, i = tiles[n]
                    if c == 0 :
                        pe.wait_ge(s["nr"], t0 + (n + CREDIT))
                    who, slot = EVC[n, c]
                    ev[who] += 1
                    pe.wait_ge(s["ev" + who], gi * EVC_TOTAL[who] + ev[who])
                    o, w = L1_CHUNKS[i][c]
                    for k in range(0, w, P):
                        rows = min(P, w - k)
                        end = o + k + rows == causal_keys(i)
                        last = mm(OV[:, 0:D1], PT[0:rows, slot, k:k + P],
                                  V[0:rows, (o + k) // P, j * D1:(j + 1) * D1], start=(o + k == 0), stop=end)
                    if end:
                        last.then_inc(s["pv"], 1)

                behind = None
                for c in range(len(L1_CHUNKS[0])):
                    scores(0, c)
                for n, (j, i) in enumerate(tiles):
                    here = len(L1_CHUNKS[i])
                    ahead = len(L1_CHUNKS[tiles[n + 1][1]]) if n + 1 < len(tiles) else 0
                    for c in range(max(here, ahead)):
                        if c < here:
                            ex += 1
                            pe.wait_ge(s["ex"], sc0 + ex)
                            transposes(L1_CHUNKS[i][c], EVC[n, c][1], s, None)
                        if c < ahead:
                            scores(n + 1, c)
                        if c < here:
                            if behind is not None:
                                pv(*behind)
                            behind = (n, c)
                pv(*behind)

            def outp(b, layer):
                n0 = b * (2 * NCH) + layer * NCH
                pe.wait_ge(s_wo, b * 32 + 16 * (layer + 1))
                for c in range(NCH):
                    for t in range(3):
                        n = 3 * c + t
                        if n >= 2:
                            pe.wait_ge(s_oy, n0 * 3 + (n - 1))
                        for k in range(KC):
                            last = nc.tensor.transpose(TP[:, n % 2, k * P:(k + 1) * P],
                                                       YT[:, n, k * P:(k + 1) * P], ident[:, :])
                        last.then_inc(s_op, 1)
                    if c > 0:
                        products(b, layer, c - 1)
                products(b, layer, NCH - 1)

            def products(b, layer, c):
                n0 = b * (2 * NCH) + layer * NCH
                pe.wait_ge(s_oy, n0 * 3 + 3 * (c + 1))
                for m in range(KC):
                    n = c * KC + m
                    if n >= 4:
                        pe.wait_ge(s_oa, n0 * KC + (CREDIT + n - 3))
                    for k in range(KC):
                        last = mm(SC[:, (n % 4) * 512:(n % 4) * 512 + CH], Wo[:, k, m * P:(m + 1) * P],
                                  yT[:, c % 2, k, :], start=(k == 0), stop=(k == KC - 1))
                    last.then_inc(s_om, 1)

            def final(b):
                for t in range(NT):
                    if t >= 2:
                        pe.wait_ge(s_fe, b * NT + (t - 1))
                    for k in range(KC):
                        last = nc.tensor.transpose(TP[:, t % 2, k * P:(k + 1) * P],
                                                   XN[:, k, t * P:(t + 1) * P], ident[:, :])
                    last.then_inc(s_ft, 1)

            run_phases(pe, setup, load, norm, proj, na, selfa, causal, outp, final)

        @block.scalar
        def _(act):
            def setup():
                act.sem_inc(s_xe, CREDIT)
                for s in dense.values():
                    act.sem_inc(s["nr"], CREDIT)
                    act.sem_inc(s["dn"], CREDIT)
                act.sem_inc(n_ad, CREDIT)
                act.sem_inc(n_nr, CREDIT)
                act.sem_inc(s_oa, CREDIT)

            def load(b):
                for t in range(0, NT, 2):
                    act.wait_ge(s_xt, b * NT + (t + 1))
                    if t:
                        act.wait_ge(s_xe, b * NT + (CREDIT + t))
                    nc.scalar.activation(XN[:, :, t * P:(t + 1) * P],
                                         TP[:, t % 2, :].rearrange("p (k n) -> p k n", k=KC),
                                         ACT.Copy).then_inc(s_xe, 1)

            def norm(b, layer):
                d0 = b * 2 + layer
                act.wait_ge(s_st, d0 * 6 + 5)
                nc.scalar.activation(sd[:, :], dv[:, :], ACT.Sqrt, bias=epst[:, 0:1]).then_inc(s_sq, 1)

            def proj(kind, b, g):
                gi = group_index(kind, b, g)
                for n in range(2 * NCH):
                    c, m = n // 2, 1 - n % 2
                    act.wait_ge(s_pq, gi * (2 * NCH) + (n + 1))
                    src = SC[:, (n % 3) * 512:(n % 3) * 512 + CH]
                    dst = (QH, KH)[m][:, c * CH:(c + 1) * CH]
                    if kind == "causal":
                        nc.scalar.activation(dst, src, ACT.Copy).then_inc(s_hi, 1)
                        continue
                    row = {"na": 0, "self": G0}[kind]
                    bias = bsel[:, m:m + 1]
                    if n == 0:
                        nc.scalar.activation(bsel[:, :], bqkv[:, bass.ds(g + row, 1), :].rearrange(
                            "p o n -> p (o n)"), ACT.Copy).then_inc(s_bs, 1)
                        act.wait_ge(s_bs, (b * (2 * G0) + g + (row + 1)))
                    if kind == "na" and m == 0:
                        dst = dst.rearrange("p (w r c) -> p w r c", w=CW, c=QW)
                        src = src.rearrange("p (r w c) -> p w r c", w=CW, c=QW)
                    nc.scalar.activation(dst, src, ACT.Identity, bias=bias).then_inc(s_hi, 1)
                v0 = v_base(kind, b, g)
                for n, (t0, w) in enumerate(v_banks(kind)):
                    if n % 2:
                        continue
                    act.wait_ge(s_pv, v0 + (n + 1))
                    if n:
                        act.wait_ge(s_pe, v0 + n)
                    rows, dst = (BAND, Vb) if kind == "na" else (P, V)
                    nc.scalar.activation(dst[0:rows, t0:t0 + w, :], SC[0:rows, (3 + n % 2) * 512:
                                         (3 + n % 2) * 512 + w * P].rearrange("p (t n) -> p t n", n=P),
                                         ACT.Copy).then_inc(s_pe, 1)

            def na(b, g):
                n0 = b * (G0 * H0 * NT) + g * (H0 * NT)
                with act.Fori(0, H0 // 2) as hp:
                    m0 = n0 + hp * (2 * NT)

                    def copy(n):
                        nb = NA_TILES[n % NT][4]
                        act.wait_ge(n_tp, m0 + (n + 1))
                        nc.scalar.activation(PT[0:BAND, n % 2, 0:nb * P], TP[0:BAND, n % 2, 0:nb * P],
                                             ACT.Copy).then_inc(n_ev, 1)

                    for n in range(2 * NT):
                        w = NA_TILES[n % NT][4] * BAND
                        act.wait_ge(n_nm, m0 + (n + 1))
                        p = Pb[:, (n % 4) * 512:(n % 4) * 512 + w]
                        nc.scalar.activation(p, p, ACT.Exp, bias=nmax[:, n % RING:n % RING + 1],
                                             accum_out=rsum[:, n % RING, 0:1]).then_inc(n_ex, 1)
                        if n:
                            copy(n - 1)
                    copy(2 * NT - 1)

            def selfa(b, g):
                s = dense["f"]
                t0 = (b * G0 + g) * (H0 * NT)
                with act.Fori(0, H0 * NT // 2) as i:
                    for e in range(2):
                        t = t0 + i * 2 + e
                        act.wait_ge(s["nm"], t + 1)
                        act.wait_ge(s["dn"], t + (CREDIT - 1))
                        for c in range(NC0 + 1):
                            if c < NC0:
                                o, w = SELF_CHUNKS[c]
                                nc.scalar.activation(Pb[:, o:o + w], SC[:, o:o + w], ACT.Exp,
                                                     bias=nmax[:, e:e + 1],
                                                     accum_out=rsum[:, e, c:c + 1]).then_inc(s["ex"], 1)
                            k = c - 1
                            if k in EVA0:
                                act.wait_ge(s["tp"], t * NC0 + (k + 1))
                                o, w = SELF_CHUNKS[k]
                                sl = (e * NC0 + k) % 2
                                nc.scalar.activation(PT[:, sl, 0:w], TP[:, sl, 0:w], ACT.Copy)\
                                    .then_inc(s["eva"], 1)

            def causal(b, g):
                s = dense["c"]
                gi = b * G1 + g
                tp0 = gi * (H1 * L1_PER_HEAD)
                t0 = gi * (H1 * NT)
                tp = 0
                pending = None

                def copy(n, c, count):
                    who, slot = EVC[n, c]
                    if who == "a":
                        w = -(-L1_CHUNKS[n % NT][c][1] // P) * P
                        act.wait_ge(s["tp"], tp0 + count)
                        nc.scalar.activation(PT[:, slot, 0:w], TP[:, slot, 0:w], ACT.Copy)\
                            .then_inc(s["eva"], 1)

                for n in range(H1 * NT):
                    i = n % NT
                    act.wait_ge(s["nm"], t0 + (n + 1))
                    act.wait_ge(s["dn"], t0 + (n + CREDIT - 1))
                    for c, (o, w) in enumerate(L1_CHUNKS[i]):
                        nc.scalar.activation(Pb[:, o:o + w], SC[:, o:o + w], ACT.Exp,
                                             bias=nmax[:, n % 2:n % 2 + 1],
                                             accum_out=rsum[:, n % 2, c:c + 1]).then_inc(s["ex"], 1)
                        if c:
                            copy(n, c - 1, tp + c)
                    tp += len(L1_CHUNKS[i])
                    copy(n, len(L1_CHUNKS[i]) - 1, tp)

            def outp(b, layer):
                n0 = b * (2 * NCH) + layer * NCH
                for c in range(NCH):
                    for t in range(3):
                        n = 3 * c + t
                        act.wait_ge(s_op, n0 * 3 + (n + 1))
                        if t == 0 and c >= 2:
                            act.wait_ge(s_om, n0 * KC + KC * (c - 1))
                        src = TP[:, n % 2, :].rearrange("p (k n) -> p k n", k=KC)
                        dst = yT[:, c % 2, :, t * P:(t + 1) * P]
                        if layer == 0:
                            for k in range(KC):
                                if k < G0:
                                    d_ = yT[:, c % 2, k, :].rearrange("p (r w c) -> p w r c", w=CW, c=QW)[:, t]
                                    s_ = src[:, k, :].rearrange("p (r c) -> p r c", c=QW)
                                else:
                                    d_, s_ = dst[:, k, :], src[:, k, :]
                                ins = nc.scalar.activation(d_, s_, ACT.Identity, bias=bqkv[:, k, 2:3])
                            ins.then_inc(s_oy, 1)
                        else:
                            nc.scalar.activation(dst, src, ACT.Copy).then_inc(s_oy, 1)

            def final(b):
                for t in range(0, NT, 2):
                    act.wait_ge(s_ft, b * NT + (t + 1))
                    if t:
                        act.wait_ge(s_fe, b * NT + t)
                    nc.scalar.activation(YT[:, t, :], TP[:, t % 2, :], ACT.Copy).then_inc(s_fe, 1)

            run_phases(act, setup, load, norm, proj, na, selfa, causal, outp, final)

        @block.vector
        def _(dve):
            def setup():
                nc.vector.memset(epst[:, :], EPS)
                nc.vector.memset(YT[:, 3, :], 0.0)
                nc.vector.memset(YT[:, 15, :], 0.0)
                nc.vector.memset(XN.ap(), 0.0).then_inc(s_set, 1)
                dve.wait_ge(s_const, 16 * 10)
                n = a["relp"].shape[1]
                nc.vector.tensor_copy(YT[0:8, 14, n:2 * HW - 1],
                                      YT[0:8, 14, n - 1:n].to_broadcast([8, 2 * HW - 1 - n])).then_inc(s_set, 1)
                nc.vector.tensor_scalar(bqkv[:, :, 0], bqkv[:, :, 0], SCALE0, None, ALU.mult)
                nc.vector.tensor_copy(qoh.ap(), YT[:, 0, 0:3 * P].rearrange("p (n q) -> p n q", n=3))
                for n in range(2):
                    dve.wait_ge(s_setp, 4 * (n + 1))
                    for i in range(4):
                        ins = nc.vector.tensor_copy(YT[:, 4 + 4 * n + i, 0:TTW], SC[:, i * 512:i * 512 + TTW])
                    ins.then_inc(s_set, 1)
                dve.wait_ge(s_dram, 16 * (3 + 8 + 10))
                ts = YT[:, 3, 0:8 * NU].rearrange("p (h n) -> p h n", h=8)
                ps = YT[:, 15, 0:8 * HW].rearrange("p (h n) -> p h n", h=8)
                mask = YT[:, 2, 0:NU].rearrange("p (o n) -> p o n", o=1).to_broadcast([P, 8, NU])
                nc.vector.tensor_tensor(ts, ts, mask, ALU.add).then_inc(s_vd, 1)
                dve.wait_ge(s_vd, 1)
                n = 1
                for dst, src, width in ((PS, ps, HW), (TS, ts, NU)):
                    part = QL[:, 0:8 * width].rearrange("p (h n) -> p h n", h=8)
                    nc.vector.tensor_copy(part, src).then_inc(s_vd, 1)
                    dve.wait_ge(s_vd, n + 1)
                    nc.vector.tensor_copy(dst[0:64], part[0:64].bitcast(F32))
                    nc.vector.tensor_tensor(dst[64:P], src[64:P], part[64:P].bitcast(F32), ALU.subtract)\
                        .then_inc(s_vd, 1)
                    dve.wait_ge(s_vd, n + 2)
                    n += 2

            def load(b):
                for t in range(1, NT, 2):
                    dve.wait_ge(s_xt, b * NT + (t + 1))
                    dve.wait_ge(s_xe, b * NT + (CREDIT + t))
                    nc.vector.tensor_copy(XN[:, :, t * P:(t + 1) * P],
                                          TP[:, t % 2, :].rearrange("p (k n) -> p k n", k=KC)).then_inc(s_xe, 1)

            def norm(b, layer):
                d0 = b * 2 + layer
                for k in range(KC):
                    for c in range(NCH):
                        ins = nc.vector.bn_stats(st[:, c, :], XN[:, k, c * CH:(c + 1) * CH])
                    ins.then_inc(s_bn, 1)
                    hold(dve, s_bn, d0 * (2 * KC) + (2 * k + 1))
                    nc.vector.bn_aggr(mv[:, k, :], st.ap()).then_inc(s_bn, 1)
                    hold(dve, s_bn, d0 * (2 * KC) + (2 * k + 2))
                dve.engine_nop().then_inc(s_st, 1)
                dve.wait_ge(s_gp, d0 * 2 + 1)
                nc.vector.tensor_copy(gm[:, :], SC[:, 0:KC]).then_inc(s_st, 1)
                dve.wait_ge(s_st, d0 * 6 + 2)
                nc.vector.tensor_tensor(dv[:, :], mv[:, :, 0], gm[:, :], ALU.subtract).then_inc(s_st, 1)
                dve.wait_ge(s_st, d0 * 6 + 3)
                nc.vector.tensor_tensor(sd[:, :], dv[:, :], dv[:, :], ALU.mult).then_inc(s_sqr, 1)
                dve.wait_ge(s_sqr, d0 + 1)
                nc.vector.tensor_tensor(dv[:, :], sd[:, :], mv[:, :, 1], ALU.add).then_inc(s_st, 1)
                dve.wait_ge(s_gp, d0 * 2 + 2)
                nc.vector.tensor_copy(dv[:, :], SC[:, 512:512 + KC]).then_inc(s_st, 1)
                dve.wait_ge(s_sq, d0 + 1)
                nc.vector.reciprocal(rstd[:, :], sd[:, :]).then_inc(s_st, 1)
                dve.wait_ge(s_st, d0 * 6 + 6)
                dve.wait_ge(s_save, d0 * 16 + 16)
                for k in range(KC):
                    nc.vector.tensor_scalar(XN[:, k, :], XN[:, k, :], gm[:, k:k + 1], rstd[:, k:k + 1],
                                            ALU.subtract, ALU.mult)

            def proj(kind, b, g):
                gi = group_index(kind, b, g)
                for n in range(2 * NCH):
                    c, m = n // 2, 1 - n % 2
                    dve.wait_ge(s_hi, gi * (2 * NCH) + (n + 1))
                    src = SC[:, (n % 3) * 512:(n % 3) * 512 + CH]
                    hi = (QH, KH)[m][:, c * CH:(c + 1) * CH]
                    lo = (QL, KL)[m][:, c * CH:(c + 1) * CH]
                    if kind == "na" and m == 0:
                        src = src.rearrange("p (r w c) -> p w r c", w=CW, c=QW)
                        hi = hi.rearrange("p (w r c) -> p w r c", w=CW, c=QW)
                        lo = lo.rearrange("p (w r c) -> p w r c", w=CW, c=QW)
                    if kind == "causal":
                        ins = nc.vector.tensor_tensor(lo, src, hi.bitcast(F32), ALU.subtract)
                    else:
                        parts = [(lo, src, hi)] if kind != "na" or m else [
                            (lo[:, w], src[:, w], hi[:, w]) for w in range(CW)]
                        for lo_, src_, hi_ in parts:
                            ins = nc.vector.scalar_tensor_tensor(
                                out=lo_, in0=src_, scalar=bsel[:, m:m + 1], in1=hi_.bitcast(F32),
                                op0=ALU.add, op1=ALU.subtract)
                    ins.then_inc(s_lo, 1)
                v0 = v_base(kind, b, g)
                for n, (t0, w) in enumerate(v_banks(kind)):
                    if n % 2 == 0:
                        continue
                    dve.wait_ge(s_pv, v0 + (n + 1))
                    dve.wait_ge(s_pe, v0 + n)
                    rows, dst = (BAND, Vb) if kind == "na" else (P, V)
                    nc.vector.tensor_copy(dst[0:rows, t0:t0 + w, :], SC[0:rows, (3 + n % 2) * 512:
                                          (3 + n % 2) * 512 + w * P].rearrange("p (t n) -> p t n", n=P))\
                        .then_inc(s_pe, 1)

            def na(b, g):
                n0 = b * (G0 * H0 * NT) + g * (H0 * NT)
                with dve.Fori(0, H0 // 2) as hp:
                    m0 = n0 + hp * (2 * NT)
                    k0 = (b * (G0 * H0) + g * H0 + hp * 2) * NTAB

                    def norm_out(n):
                        e, t = n % RING, NA_TILES[n % NT][0]
                        dve.wait_ge(n_pv, m0 + (n + 1))
                        nc.vector.reciprocal(rden[:, e:e + 1], rsum[:, e, 0:1]).then_inc(n_rd, 1)
                        dve.wait_ge(n_rd, m0 + (n + 1))
                        nc.vector.tensor_scalar(
                            YT[:, t, bass.ds(g * P + hp * (2 * D0) + (n // NT) * D0, D0)],
                            OV_NA[n % 2], rden[:, e:e + 1], None, ALU.mult).then_inc(n_nr, 1)

                    for n in range(2 * NT):
                        t, cw, cls, lo, nb = NA_TILES[n % NT]
                        tb = (n // NT) * NTAB + NA_TABLE_OF[n % NT]
                        if n >= 3:
                            norm_out(n - 3)
                        dve.wait_ge(n_sc, m0 + (n + 1))
                        hold(dve, n_tab, k0 + (tb + 1))
                        w = nb * BAND
                        nc.vector.tensor_tensor_reduce(
                            out=Pb[:, (n % 4) * 512:(n % 4) * 512 + w].rearrange("p (r c) -> p r c", c=BW),
                            in0=SC[:, (n % RING) * 512:(n % RING) * 512 + w].rearrange("p (r c) -> p r c", c=BW),
                            in1=tab[:, tb % TAB_RING, 0:nb * BR, :], scale=1.0, scalar=-3e38,
                            op0=ALU.add, op1=ALU.max, accum_out=cmax[:, n % 2:n % 2 + 1]).then_inc(n_ad, 1)
                        dve.wait_ge(n_ad, m0 + (CREDIT + n + 1))
                        nc.vector.tensor_scalar(nmax[:, n % RING:n % RING + 1], cmax[:, n % 2:n % 2 + 1], -1.0, None,
                                                ALU.mult).then_inc(n_nm, 1)
                    for n in range(2 * NT - 3, 2 * NT):
                        norm_out(n)

            def negate_max(s, e, chunks, count):
                dve.wait_ge(s["cm"], count)
                nc.vector.tensor_reduce(nmax[:, e:e + 1], cmax[:, 0:chunks], AX.X, ALU.max, negate=True)\
                    .then_inc(s["nm"], 1)

            def finish(s, e, chunks, count, exps, d, out):
                dve.wait_ge(s["ex"], exps)
                nc.vector.tensor_reduce(den[:, e:e + 1], rsum[:, e, 0:chunks], AX.X, ALU.add)\
                    .then_inc(s["dn"], 1)
                dve.wait_ge(s["dn"], count + CREDIT)
                nc.vector.reciprocal(rden[:, e:e + 1], den[:, e:e + 1]).then_inc(s["rd"], 1)
                dve.wait_ge(s["rd"], count)
                dve.wait_ge(s["pv"], count)
                nc.vector.tensor_scalar(out, OV[:, 0:d], rden[:, e:e + 1], None, ALU.mult)\
                    .then_inc(s["nr"], 1)

            def selfa(b, g):
                s = dense["f"]
                t0 = (b * G0 + g) * (H0 * NT)

                def chunk_max(t, c):
                    o, w = SELF_CHUNKS[c]
                    dve.wait_ge(s["sc"], (t0 + t) * NC0 + (c + 1))
                    nc.vector.tensor_reduce(cmax[:, c:c + 1], SC[:, o:o + w], AX.X, ALU.max)\
                        .then_inc(s["cm"], 1)

                def copy(t, e, c):
                    if c in EVA0:
                        return
                    o, w = SELF_CHUNKS[c]
                    sl = (e * NC0 + c) % 2
                    dve.wait_ge(s["tp"], (t0 + t) * NC0 + (c + 1))
                    nc.vector.tensor_copy(PT[:, sl, 0:w], TP[:, sl, 0:w]).then_inc(s["evd"], 1)

                def out_of(t, e):
                    head = t // NT
                    finish(s, e, NC0, t0 + t + 1, (t0 + t) * NC0 + NC0, D0,
                           YT[:, bass.ds(t % NT, 1), bass.ds(head * D0 + g * P + G0 * P, D0)].rearrange(
                               "p o c -> p (o c)"))

                def pair(i, first, last):
                    for e in range(2):
                        t = i * 2 + e
                        ahead = not (last and e == 1)
                        for c in range(NC0):
                            copy(t, e, c)
                            if ahead:
                                chunk_max(t + 1, c)
                            if c == 0 and not (first and e == 0):
                                out_of(t - 1, 1 - e)
                        if ahead:
                            negate_max(s, 1 - e, NC0, (t0 + t) * NC0 + 2 * NC0)

                for c in range(NC0):
                    chunk_max(0, c)
                negate_max(s, 0, NC0, t0 * NC0 + NC0)
                pairs = H0 * NT // 2
                pair(0, True, False)
                with dve.Fori(1, pairs - 1) as i:
                    pair(i, False, False)
                pair(pairs - 1, False, True)
                out_of(H0 * NT - 1, 1)

            def causal(b, g):
                s = dense["c"]
                gi = b * G1 + g
                sc0 = gi * (H1 * L1_PER_HEAD)
                t0 = gi * (H1 * NT)
                for j in range(H1):
                    ps = PS[:, bass.ds(g * H1 + j, 1), :].to_broadcast([P, NU, HW])
                    ts = TS[:, bass.ds(g * H1 + j, 1), :].rearrange("p o u -> p u o").to_broadcast([P, NU, HW])
                    nc.vector.tensor_tensor(KG[j].ap().rearrange("p (u n) -> p u n", n=HW), ps, ts, ALU.add)\
                        .then_inc(c_kg, 1)
                sc = [0]

                def chunk_max(n, c):
                    o, w = L1_CHUNKS[n % NT][c]
                    sc[0] += 1
                    dve.wait_ge(s["sc"], sc0 + sc[0])
                    nc.vector.tensor_reduce(cmax[:, c:c + 1], SC[:, o:o + w], AX.X, ALU.max)\
                        .then_inc(s["cm"], 1)

                def out_of(n):
                    i, j = n % NT, n // NT
                    exps = j * L1_PER_HEAD + sum(len(L1_CHUNKS[x]) for x in range(i + 1))
                    finish(s, n % 2, len(L1_CHUNKS[i]), t0 + (n + 1), sc0 + exps, D1,
                           YT[:, i, bass.ds(g * P + j * D1, D1)])

                chunk_max(0, 0)
                negate_max(s, 0, 1, sc0 + sc[0])
                tp = 0
                for n in range(H1 * NT):
                    here = len(L1_CHUNKS[n % NT])
                    ahead = len(L1_CHUNKS[(n + 1) % NT]) if n + 1 < H1 * NT else 0
                    for c in range(max(here, ahead)):
                        if c < here:
                            tp += 1
                            who, slot = EVC[n, c]
                            if who == "d":
                                w = -(-L1_CHUNKS[n % NT][c][1] // P) * P
                                dve.wait_ge(s["tp"], sc0 + tp)
                                nc.vector.tensor_copy(PT[:, slot, 0:w], TP[:, slot, 0:w]).then_inc(s["evd"], 1)
                        if c < ahead:
                            chunk_max(n + 1, c)
                        if c == 0 and n:
                            out_of(n - 1)
                    if ahead:
                        negate_max(s, (n + 1) % 2, ahead, sc0 + sc[0])
                out_of(H1 * NT - 1)

            def outp(b, layer):
                n0 = b * (2 * NCH * KC) + layer * NCH * KC
                for c in range(NCH):
                    for m in range(KC):
                        n = c * KC + m
                        dve.wait_ge(s_om, n0 + (n + 1))
                        dve.wait_ge(s_or[n % 2], n0 * 8 + 16 * (n // 2 + 1))
                        dst = XN[:, m, :].rearrange("p (c r) -> p r c", r=HW)[:, c * QR:(c + 1) * QR, :]
                        src = SC[:, (n % 4) * 512:(n % 4) * 512 + CH].rearrange("p (r c) -> p r c", c=HW)
                        add = res[:, n % 2, :].rearrange("p (r c) -> p r c", c=HW)
                        if layer == 0:
                            nc.vector.scalar_tensor_tensor(out=dst, in0=src, scalar=bproj[:, m:m + 1], in1=add,
                                                           op0=ALU.add, op1=ALU.add).then_inc(s_oa, 1)
                        else:
                            nc.vector.tensor_tensor(dst, src, add, ALU.add).then_inc(s_oa, 1)

            def final(b):
                for t in range(1, NT, 2):
                    dve.wait_ge(s_ft, b * NT + (t + 1))
                    dve.wait_ge(s_fe, b * NT + t)
                    nc.vector.tensor_copy(YT[:, t, :], TP[:, t % 2, :]).then_inc(s_fe, 1)

            run_phases(dve, setup, load, norm, proj, na, selfa, causal, outp, final)

        @block.gpsimd
        def _(pool):
            def proj(kind, b, g):
                gi = group_index(kind, b, g)
                hold(pool, s_w, gi * 16 + 16)
                q = Wg[:, :, 0:P]
                scale = SCALE1 if kind == "causal" else SCALE0
                nc.gpsimd.tensor_scalar(q, q, scale, None, ALU.mult).then_inc(s_ws, 1)
                if kind == "na":
                    v0 = v_base(kind, b, g)
                    for t in range(CW * NB):
                        if t >= V_RING:
                            hold(pool, s_pv, v0 + ((t - V_RING) // 4 + 1))
                        cw, rb = t // NB, t % NB
                        grid = XN.ap().rearrange("p k (r c) -> p k r c", c=HW)
                        nc.gpsimd.tensor_copy(
                            band_tokens(t).rearrange("p k (r c) -> p k r c", c=BW),
                            grid[:, :, rb * BR:(rb + 1) * BR, COL0[cw]:COL0[cw] + BW]).then_inc(s_vw, 1)

            def na(b, g):
                h0 = b * (G0 * H0) + g * H0
                n0 = b * (G0 * H0 * NT) + g * (H0 * NT)
                for j in range(H0):
                    hold(pool, n_tt[j % 2], (b * G0 + g) * (H0 // 2 * 16) + (j // 2 + 1) * 16)
                    for x, (cw, cls, nb, n) in enumerate(NA_TABLES):
                        r0 = BR if cls == 0 else 0
                        c0 = 6 - (QW * cw - COL0[cw])
                        k = j * NTAB + x
                        nr = nb * BR
                        if k:
                            hold(pool, n_tab, h0 * NTAB + k)
                        rows = rowm[:, cls, 0:nr].rearrange("p (r o) -> p r o", o=1).to_broadcast([P, nr, BW])
                        nc.gpsimd.tensor_tensor(tmpt[:, 0:nr, 0:BW], TT[:, j % 2, r0:r0 + nr, c0:c0 + BW],
                                                rows, ALU.add).then_inc(n_tmp, 1)
                        hold(pool, n_tmp, h0 * NTAB + (k + 1))
                        if k >= TAB_RING:
                            kk = k - TAB_RING + 1
                            done = (kk // NTAB) * NT + NA_TABLES[kk % NTAB][3]
                            hold(pool, n_ad, n0 + (CREDIT + done))
                        cols = colm[:, cw:cw + 1, :].to_broadcast([P, nr, BW])
                        nc.gpsimd.tensor_tensor(tab[:, k % TAB_RING, 0:nr, :], tmpt[:, 0:nr, 0:BW], cols,
                                                ALU.add).then_inc(n_tab, 1)

            run_phases(pool, nothing, nothing, nothing, proj, na, nothing, nothing, nothing, nothing)


def constants():
    f = np.float32
    c = {"ident": np.eye(P, dtype=f), "rev": np.eye(P, dtype=f)[::-1].copy(),
         "avg": np.kron(np.eye(P // 16, dtype=f), np.full((16, 16), 1 / 16, f))}
    qoh = np.zeros((P, 3, P), f)
    for phase in range(3):
        for p in range(P):
            tok = P * phase + p
            r = tok // HW - P * phase // HW
            for base in (0, 64):
                qoh[base + HW - 1 - tok % HW, phase, p] = 1
                qoh[base + HW + 3 - r, phase, p] = 1
    c["qoh"] = qoh.reshape(P, 3 * P)
    tmask = np.zeros((P, NU), f)
    for r in range(4):
        for base in (0, 64):
            tmask[base + HW + 3 - r, HW - 1 + r + 1:] = -BIG
    c["tmask"] = tmask

    def outside(q, key):
        first = min(max(q - KS // 2, 0), HW - KS)
        return not first <= key < first + KS

    rowm, colm = np.zeros((P, 3, 16), f), np.zeros((P, 3, BW), f)
    for p in range(P):
        for cls, (q0, w0) in enumerate(((0, 0), (QR, QR - BR), (HW - QR, HW - QR - BR))):
            for k in range(16):
                rowm[p, cls, k] = -BIG if outside(q0 + p // QW, w0 + k) else 0
        for cw in range(CW):
            for k in range(BW):
                colm[p, cw, k] = -BIG if outside(QW * cw + p % QW, COL0[cw] + k) else 0
    c["rowm"], c["colm"] = rowm, colm
    return c


def kernel(**inputs):
    import concourse.bacc as bacc
    from concourse.bass_utils import run_bass_kernel_spmd

    arr = {k: np.asarray(v) for k, v in inputs.items()}
    x = arr["x"].reshape(B, T, C)
    wqkv = arr["L0_conv_W_qkv"].reshape(KC, P, 2, 3, 2, P)
    w0 = wqkv.transpose(2, 4, 1, 0, 3, 5).reshape(2 * G0, P, KC, 3 * P)
    w1 = np.stack([arr["L1_conv_Wq"], arr["L1_conv_Wk"], arr["L1_conv_Wv"]]).reshape(3, KC, P, G1, P)
    w1 = w1.transpose(3, 2, 1, 0, 4).reshape(G1, P, KC, 3 * P)
    wo = np.stack([arr["L0_conv_W_proj"], arr["L1_conv_Wo"]]).reshape(2, KC, P, C).transpose(0, 2, 1, 3)
    bqkv = arr["L0_conv_b_qkv"].reshape(2, 3, 2, P).transpose(3, 0, 2, 1).reshape(P, 2 * G0, 3)
    given = {"x": x, "wgrp": np.concatenate([w0, w1]), "wo": wo, "bqkv": bqkv,
             "bproj": arr["L0_conv_b_proj"].reshape(KC, P).T, "rpb": arr["L0_conv_rpb"],
             "relt": arr["L1_conv_rel_pos_bias"].T, "relp": arr["L1_conv_particle_rel_pos_bias"].T,
             **constants()}
    given = {k: np.ascontiguousarray(v) for k, v in given.items()}
    nc = bacc.Bacc("TRN2", target_bir_lowering=False, num_devices=1)
    a = {k: nc.dram_tensor(f"in_{k}", v.shape, F32, kind="ExternalInput").ap() for k, v in given.items()}
    a["out"] = nc.dram_tensor("out", (B, T, C), F32, kind="ExternalOutput").ap()
    build(nc, a)
    r = run_bass_kernel_spmd(nc, [{f"in_{k}": v for k, v in given.items()}], core_ids=[0])
    return np.asarray(r.results[0]["out"]).reshape(B, HW, HW, C)
```

```python
from contextlib import ExitStack

import numpy as np
import concourse.bass as bass
from concourse import mybir

F32 = mybir.dt.float32
F32R = mybir.dt.float32r
ALU = mybir.AluOpType
ACT = mybir.ActivationFunctionType
AX = mybir.AxisListType

B = 2
HW = 48
T = HW * HW
C = 512
P = 128
KC = C // P
NT = T // P
CH = 384
NCH = T // CH
EPS = 1e-5
BIG = 1e30

D0 = 32
H0 = P // D0
G0 = 2
SCALE0 = float(D0) ** -0.5
KS = 7
QR, QW = 8, 16
BR, BW = 4, 22
BAND = BR * BW
NB = HW // BR
CW = HW // QW
COL0 = [0, 13, 26]
QT_NA = NT
RPB = 2 * KS - 1
PADR, PADC = 23, 43
OFFR, OFFC = 5, 15
TTW = 16 * 28
RUN = 15 * PADC + 28
RUNP = 16 * PADC

D1 = 64
H1 = P // D1
G1 = 4
HEADS1 = 8
SCALE1 = float(D1) ** -0.5
NU = HW + 3
KGW = NU * HW

NG = 2 * G0 + G1
CREDIT = 8
RING = 4


def chunks_of(keys):
    return [(c, min(512, keys - c)) for c in range(0, keys, 512)]


SELF_CHUNKS = chunks_of(T)
NC0 = len(SELF_CHUNKS)
UT = CH // P
UNITS = H0 * T // CH
NM = UT * NC0
PAIRS = NT // 2
M_AT = [range(0, 3)] + [range(2 * p + 1, 2 * p + 3) for p in range(1, 7)] + [range(0)] * 2
MT_AT = {3: 0, 6: 1, 8: 2}


def causal_keys(i):
    return ((P * (i + 1) - 1) // HW + 1) * HW


L1_CHUNKS = [chunks_of(causal_keys(i)) for i in range(NT)]
L1_PER_HEAD = sum(len(c) for c in L1_CHUNKS)

EVC, EVC_TOTAL = {}, {"a": 0, "d": 0}
for _n in range(H1 * NT):
    for _c in range(len(L1_CHUNKS[_n % NT])):
        _who = "a" if len(EVC) % 5 in (0, 2) else "d"
        EVC[_n, _c] = (_who, len(EVC) % 2)
        EVC_TOTAL[_who] += 1


def na_tiles():
    out = []
    for cw in range(CW):
        for rt in range(HW // QR):
            lo = max(QR * rt - BR, 0) // BR
            hi = min(QR * rt + QR + BR, HW) // BR
            cls = 0 if rt == 0 else 2 if rt == HW // QR - 1 else 1
            out.append((rt * CW + cw, cw, cls, lo, hi - lo))
    return out


NA_TILES = na_tiles()
NA_TABLES = []
NA_TABLE_OF = []
for _n, (_t, _cw, _cls, _lo, _nb) in enumerate(NA_TILES):
    if not NA_TABLES or NA_TABLES[-1][:2] != (_cw, _cls):
        NA_TABLES.append((_cw, _cls, _nb, _n))
    NA_TABLE_OF.append(len(NA_TABLES) - 1)
NTAB = len(NA_TABLES)
V_RING = T // (KC * BAND)
TAB_RING = 3


def build(nc, a):
    ctx = ExitStack()
    with ctx:
        def sb(name, shape, dt=F32):
            return ctx.enter_context(nc.sbuf_tensor(name, shape, dt))

        def sem(name):
            return ctx.enter_context(nc.semaphore(name))

        def overlay(*choices):
            made, largest = [], max(choices, key=lambda c: sum(int(np.prod(s[1][1:])) for s in c))
            for c in choices:
                if c is not largest:
                    with ExitStack() as scope:
                        made += [scope.enter_context(nc.sbuf_tensor(n, s, d)) for n, s, d in c]
            made += [sb(n, s, d) for n, s, d in largest]
            return {t.name: t for t in made}

        def dram(name, shape):
            return nc.dram_tensor(name, shape, F32).ap()

        res_d = dram("res_d", (P, KC, T))
        rpb_d = dram("rpb_d", (8, PADR, PADC))
        tt_d = dram("tt_d", (8, P, TTW))
        part_d = dram("part_d", (8, 2 * HW - 1))

        XN = sb("XN", [P, KC, T])
        o = overlay([("YT", [P, NT, C], F32)],
                    [("YA", [P, NT, G0 * P], F32), ("YC", [P, G0, T], F32)])
        YT, YA, YC = o["YT"], o["YA"], o["YC"]
        QH, QL = sb("QH", [P, T], F32R), sb("QL", [P, T], F32R)
        KH, KL = sb("KH", [P, T], F32R), sb("KL", [P, T], F32R)
        o = overlay([("KST", [P, 2, T], F32R), ("QS", [P, 2, T], F32R)],
                    [("yT", [P, 2, KC, CH], F32)])
        KST, QS, yT = o["KST"], o["QS"], o["yT"]
        o = overlay([("Vb", [P, CW * NB, P], F32)],
                    [("VX", [P, NT, H0, 2 * D0], F32)],
                    [("V", [P, NT, P], F32), ("KG1", [P, KGW], F32R)],
                    [("res", [P, 2, CH], F32)])
        VX = o["VX"]
        Vb, V, KG1, res = o["Vb"], o["V"], o["KG1"], o["res"]
        o = overlay([("KG0", [P, KGW], F32R)],
                    [("TT", [P, 2, 16, 28], F32), ("tmpt", [P, 16, 28], F32),
                     ("tab", [P, TAB_RING, 16, BW], F32)])
        KG0, TT, tmpt, tab = o["KG0"], o["TT"], o["tmpt"], o["tab"]
        KG = [KG0, KG1]
        Wg = sb("Wg", [P, KC, 3 * P])
        Wo = sb("Wo", [P, KC, C])
        Pb = sb("Pb", [P, T])
        PT = sb("PT", [P, 2, 512])
        ident = sb("ident", [P, P])
        avg = sb("avg", [P, P])
        qoh = sb("qoh", [P, 3, P], F32R)
        PS = sb("PS", [P, 8, HW])
        TS = sb("TS", [P, 8, NU])
        rowm = sb("rowm", [P, 3, 16])
        colm = sb("colm", [P, 3, BW])
        bqkv = sb("bqkv", [P, 2 * G0, 3])
        bproj = sb("bproj", [P, KC])
        epst = sb("epst", [P, 1])
        st = sb("st", [P, NCH, 6])
        mv = sb("mv", [P, KC, 2])
        gm = sb("gm", [P, KC])
        dv = sb("dv", [P, KC])
        sd = sb("sd", [P, KC])
        rstd = sb("rstd", [P, KC])
        cmax = sb("cmax", [P, 8])
        nmax = sb("nmax", [P, RING])
        rsum = sb("rsum", [P, RING, 8])
        den = sb("den", [P, 2])
        um = sb("um", [P, 2])
        MM = sb("MM", [P, 2, D0], F32R)
        rec = sb("rec", [D0, CH])
        rden = sb("rden", [P, RING])
        bsel = sb("bsel", [P, 3])

        SC = ctx.enter_context(nc.psum_tensor("SC", [P, 5 * 512], F32))
        TP = ctx.enter_context(nc.psum_tensor("TP", [P, 2, 512], F32))
        OV = ctx.enter_context(nc.psum_tensor("OV", [P, 512], F32))
        ST = SC[:, 0:4 * 512].rearrange("p (s k n) -> p s k n", s=2, k=2)
        AM = [SC[:, 4 * 512:5 * 512], TP[:, 0, :]]
        MT = TP[0:D0, 1, :]
        OV_NA = [OV[:, 0:P], SC[:, 4 * 512:4 * 512 + P]]

        s_bar = sem("s_bar")
        s_held = sem("s_held")
        s_const = sem("s_const")
        s_dram = sem("s_dram")
        s_set = sem("s_set")
        s_setp = sem("s_setp")
        s_x = sem("s_x")
        s_xt = sem("s_xt")
        s_xe = sem("s_xe")
        s_save = sem("s_save")
        s_st = sem("s_st")
        s_bn = sem("s_bn")
        s_sqr = sem("s_sqr")
        s_vd = sem("s_vd")
        s_bs = sem("s_bs")
        s_gp = sem("s_gp")
        s_sq = sem("s_sq")
        s_w = sem("s_w")
        s_ws = sem("s_ws")
        s_one = sem("s_one")
        s_wo = sem("s_wo")
        s_pq = sem("s_pq")
        s_hi = sem("s_hi")
        s_lo = sem("s_lo")
        s_vw = sem("s_vw")
        s_pv = sem("s_pv")
        s_pe = sem("s_pe")
        s_stk = [sem(f"s_stk{i}") for i in range(2)]
        n_tt = [sem(f"n_tt{i}") for i in range(2)]
        n_tmp = sem("n_tmp")
        n_tab = sem("n_tab")
        n_sc = sem("n_sc")
        n_ad = sem("n_ad")
        n_nm = sem("n_nm")
        n_ex = sem("n_ex")
        n_tp = sem("n_tp")
        n_ev = sem("n_ev")
        n_pv = sem("n_pv")
        n_rd = sem("n_rd")
        n_nr = sem("n_nr")
        f_q = [sem(f"f_q{i}") for i in range(3)]
        f_am = sem("f_am")
        f_cm = sem("f_cm")
        f_um = sem("f_um")
        f_mh = sem("f_mh")
        f_ml = sem("f_ml")
        f_mt = sem("f_mt")
        f_mr = sem("f_mr")
        f_st = sem("f_st")
        f_ex = sem("f_ex")
        f_pv = sem("f_pv")
        f_rd = sem("f_rd")
        f_nr = sem("f_nr")
        dense = {}
        for k in "c":
            dense[k] = {n: sem(f"{k}_{n}") for n in
                        ("sc",
                         "cm",
                         "nm",
                         "ex",
                         "tp",
                         "eva",
                         "evd",
                         "pv",
                         "dn",
                         "rd",
                         "nr")}
        c_kg = sem("c_kg")
        s_op = sem("s_op")
        s_oy = sem("s_oy")
        s_om = sem("s_om")
        s_or = [sem(f"s_or{i}") for i in range(2)]
        s_oa = sem("s_oa")
        s_ft = sem("s_ft")
        s_fe = sem("s_fe")
        s_out = sem("s_out")

        block = ctx.enter_context(nc.Block())

        ENGINES = 5
        PH = 2 + 2 * G0 + 2 * G0 + 2 + 2 * G1 + 2

        def hold(eng, semaphore, value):
            eng.wait_ge(semaphore, value)
            eng.sem_inc(s_held, 1)

        def phase_end(eng, n):
            eng.drain().then_inc(s_bar, 1)
            hold(eng, s_bar, ENGINES * n)

        def run_phases(eng, setup, load, norm, proj, na, selfa, causal, outp, final):
            setup()
            phase_end(eng, 1)
            with eng.Fori(0, B) as b:
                ph = b * PH + 1
                load(b)
                phase_end(eng, ph + 1)
                norm(b, 0)
                phase_end(eng, ph + 2)
                with eng.Fori(0, G0) as g:
                    proj("na", b, g)
                    phase_end(eng, ph + g * 2 + 3)
                    na(b, g)
                    phase_end(eng, ph + g * 2 + 4)
                with eng.Fori(0, G0) as g:
                    proj("self", b, g)
                    phase_end(eng, ph + g * 2 + (3 + 2 * G0))
                    selfa(b, g)
                    phase_end(eng, ph + g * 2 + (4 + 2 * G0))
                outp(b, 0)
                phase_end(eng, ph + (3 + 4 * G0))
                norm(b, 1)
                phase_end(eng, ph + (4 + 4 * G0))
                with eng.Fori(0, G1) as g:
                    proj("causal", b, g)
                    phase_end(eng, ph + g * 2 + (5 + 4 * G0))
                    causal(b, g)
                    phase_end(eng, ph + g * 2 + (6 + 4 * G0))
                outp(b, 1)
                phase_end(eng, ph + (5 + 4 * G0 + 2 * G1))
                final(b)
                phase_end(eng, ph + (6 + 4 * G0 + 2 * G1))

        def nothing(*_):
            pass

        def group_index(kind, b, g):
            return b * NG + g + {"na": 0, "self": G0, "causal": 2 * G0}[kind]

        def v_banks(kind):
            n = CW * NB if kind == "na" else NT
            return [(t, min(4, n - t)) for t in range(0, n, 4)]

        V_IMG = G0 * len(v_banks("na")) + (G0 + G1) * len(v_banks("self"))

        def v_copy(kind, n, t0, w):
            src = SC[:, (3 + n % 2) * 512:(3 + n % 2) * 512 + w * P]
            if kind == "self":
                return VX[:, t0:t0 + w, :, 0:D0], src.rearrange("p (t h n) -> p t h n", h=H0, n=D0)
            src = src.rearrange("p (t n) -> p t n", n=P)
            return (Vb[0:BAND, t0:t0 + w, :], src[0:BAND]) if kind == "na" else (V[:, t0:t0 + w, :], src)

        def band_tokens(t):
            return Pb[:, (t % V_RING) * KC * BAND:(t % V_RING + 1) * KC * BAND].rearrange(
                "p (k n) -> p k n", k=KC)

        def v_base(kind, b, g):
            per = len(v_banks(kind))
            return b * V_IMG + g * per + {"na": 0, "self": G0 * len(v_banks("na")),
                                          "causal": G0 * (len(v_banks("na")) + per)}[kind]

        STK_NA, STK_SELF, STK_C = 8 * 16, 3 * 16, 4 * 16
        STK_IMG = G0 * H0 // 2 * (STK_NA + STK_SELF) + G1 * H1 // 2 * STK_C

        def stk_base(kind, b, g):
            return b * STK_IMG + {
                "na": g * (H0 // 2 * STK_NA),
                "self": g * (H0 // 2 * STK_SELF) + G0 * H0 // 2 * STK_NA,
                "causal": g * (H1 // 2 * STK_C) + G0 * H0 // 2 * (STK_NA + STK_SELF)}[kind]

        @block.sync
        def _(sp):
            def setup():
                consts = [(ident, a["ident"]), (avg, a["avg"]), (rowm, a["rowm"]), (colm, a["colm"]),
                          (bqkv, a["bqkv"]), (bproj, a["bproj"])]
                for dst, src in consts:
                    sp.dma_start(dst.ap(), src).then_inc(s_const, 16)
                sp.dma_start(YT[:, 0, 0:3 * P], a["qoh"]).then_inc(s_const, 16)
                sp.dma_start(YT[:, 1, 0:P], a["rev"]).then_inc(s_const, 16)
                sp.dma_start(YT[:, 2, 0:NU], a["tmask"]).then_inc(s_const, 16)
                n = a["relp"].shape[1]
                sp.dma_start(YT[0:8, 14, 0:n], a["relp"]).then_inc(s_const, 16)
                sp.wait_ge(s_set, 1)
                sp.dma_start(rpb_d, XN[0:8, 0, 0:PADR * PADC].rearrange("h (r c) -> h r c", c=PADC))\
                    .then_inc(s_dram, 16)
                sp.wait_ge(s_dram, 16)
                sp.dma_start(rpb_d[:, OFFR:OFFR + RPB, OFFC:OFFC + RPB], a["rpb"]).then_inc(s_dram, 16)
                sp.wait_ge(s_set, 2)
                sp.dma_start(part_d, YT[0:8, 14, 0:2 * HW - 1]).then_inc(s_dram, 16)
                sp.wait_ge(s_dram, 48)
                for h in range(8):
                    src = bass.AP(rpb_d.tensor, h * PADR * PADC, [[PADC, QR], [1, QW], [1, RUN]])
                    sp.dma_start(XN[:, 1 + h // 3, (h % 3) * RUNP:(h % 3) * RUNP + RUN], src).then_inc(s_dram, 16)
                for base in (0, 64):
                    src = bass.AP(part_d.tensor, 0, [[1, HW], [2 * HW - 1, 8], [1, HW]])
                    sp.dma_start(YT[base:base + HW, 15, 0:8 * HW].rearrange("p (h n) -> p h n", h=8), src)\
                        .then_inc(s_dram, 16)
                    for r in range(4):
                        u = 3 - r
                        dst = YT[base + HW + r:base + HW + r + 1, 3, 0:8 * NU].rearrange(
                            "p (h n) -> p h n", h=8)[:, :, u:NU]
                        sp.dma_start(dst, a["relt"][:, 0:NU - u].rearrange("(o h) n -> o h n", o=1))\
                            .then_inc(s_dram, 16)
                sp.wait_ge(s_set, 4)
                for h in range(8):
                    sp.dma_start(tt_d[h], YT[:, 4 + h, 0:TTW]).then_inc(s_dram, 16)
                sp.wait_ge(s_dram, 16 * (3 + 8 + 10 + 8))

            def load(b):
                for part in range(3):
                    w = NT // 3
                    src = a["x"][bass.ds(b, 1), part * w * P:(part + 1) * w * P, :].rearrange(
                        "o (t p) c -> p (o t) c", p=P)
                    sp.dma_start(YT[:, part * w:(part + 1) * w, :], src).then_inc(s_x, 16)
                hold(sp, s_x, b * 48 + 48)

            def norm(b, layer):
                sp.dma_start(res_d, XN.ap()).then_inc(s_save, 16)
                sp.dma_start(Wo.ap(), a["wo"][layer]).then_inc(s_wo, 16)
                hold(sp, s_save, b * 32 + 16 * (layer + 1))
                hold(sp, s_wo, b * 32 + 16 * (layer + 1))

            def proj(kind, b, g):
                off = {"na": 0, "self": G0, "causal": 2 * G0}[kind]
                sp.dma_start(Wg.ap(), a["wgrp"][bass.ds(g + off, 1)].rearrange("o p k n -> p (o k) n"))\
                    .then_inc(s_w, 16)
                hold(sp, s_w, group_index(kind, b, g) * 16 + 16)

            def stack(j, slot, with_q):
                r = slice(D0 * j, D0 * j + D0)
                for i, src in enumerate((KH, KL, KH, KL)):
                    sp.dma_start(KST[D0 * i:D0 * i + D0, slot, :].bitcast(F32), src[r, :].bitcast(F32))\
                        .then_inc(s_stk[slot], 16)
                if with_q:
                    for i, src in enumerate((QH, QH, QL, QL)):
                        sp.dma_start(QS[D0 * i:D0 * i + D0, slot, :].bitcast(F32), src[r, :].bitcast(F32))\
                            .then_inc(s_stk[slot], 16)

            def stacks_end(kind, b, g, each):
                for slot in range(2):
                    hold(sp, s_stk[slot], stk_base(kind, b, g) + each)

            def na(b, g):
                n0 = b * (G0 * H0 * NT) + g * (H0 * NT)
                h0 = b * (G0 * H0) + g * H0
                for j in range(H0):
                    if j >= 2:
                        hold(sp, n_sc, n0 + NT * (j - 1))
                        hold(sp, n_tab, (h0 + (j - 1)) * NTAB)
                    stack(j, j % 2, True)
                    sp.dma_start(TT[:, j % 2], tt_d[bass.ds(g * H0 + j, 1)].rearrange(
                        "o p (r c) -> p (o r) c", c=28)).then_inc(n_tt[j % 2], 16)
                stacks_end("na", b, g, H0 // 2 * STK_NA)
                for slot in range(2):
                    hold(sp, n_tt[slot], (b * G0 + g + 1) * (H0 // 2 * 16))

            def selfa(b, g):
                u0 = (b * G0 + g) * UNITS

                def keys(j):
                    for i, src in enumerate((KH, KL, KH)):
                        sp.dma_start(KST[D0 * i:D0 * i + D0, j % 2, :].bitcast(F32),
                                     src[D0 * j:D0 * j + D0, :].bitcast(F32)).then_inc(s_stk[j % 2], 16)

                def queries(u):
                    j, c, slot = u // NCH, u % NCH, u % 3
                    for i, src in enumerate((QH, QH, QL)):
                        sp.dma_start(QS[D0 * i:D0 * i + D0, 0, slot * CH:(slot + 1) * CH].bitcast(F32),
                                     src[D0 * j:D0 * j + D0, c * CH:(c + 1) * CH].bitcast(F32))\
                            .then_inc(f_q[slot], 16)

                queries(0)
                keys(0)
                queries(1)
                queries(2)
                keys(1)
                for u in range(3, UNITS):
                    hold(sp, f_st, (u0 + (u - 2)) * PAIRS)
                    queries(u)
                    if u % NCH == 2 and u // NCH + 1 < H0:
                        keys(u // NCH + 1)
                stacks_end("self", b, g, H0 // 2 * STK_SELF)
                for slot in range(3):
                    hold(sp, f_q[slot], (b * G0 + g + 1) * (UNITS // 3 * 48))

            def causal(b, g):
                for j in range(H1):
                    r = slice(D1 * j, D1 * j + D1)
                    for i, src in enumerate((KH, KL)):
                        sp.dma_start(KST[D1 * i:D1 * i + D1, j, :].bitcast(F32), src[r, :].bitcast(F32))\
                            .then_inc(s_stk[j], 16)
                    for i in range(2):
                        sp.dma_start(QS[D1 * i:D1 * i + D1, j, :].bitcast(F32), QH[r, :].bitcast(F32))\
                            .then_inc(s_stk[j], 16)
                stacks_end("causal", b, g, H1 // 2 * STK_C)

            def outp(b, layer):
                n0 = b * (2 * NCH * KC) + layer * NCH * KC
                for c in range(NCH):
                    for m in range(KC):
                        n = c * KC + m
                        hold(sp, s_oa, n0 + (CREDIT + n - 1))
                        sp.dma_start(res[:, n % 2, :], res_d[:, m, c * CH:(c + 1) * CH])\
                            .then_inc(s_or[n % 2], 16)
                for slot in range(2):
                    hold(sp, s_or[slot], (n0 + NCH * KC) * 8)

            def final(b):
                for part in range(3):
                    w = NT // 3
                    hold(sp, s_fe, b * NT + (part + 1) * w)
                    dst = a["out"][bass.ds(b, 1), part * w * P:(part + 1) * w * P, :].rearrange(
                        "o (t p) c -> p (o t) c", p=P)
                    sp.dma_start(dst, YT[:, part * w:(part + 1) * w, :]).then_inc(s_out, 16)
                hold(sp, s_out, b * 48 + 48)

            run_phases(sp, setup, load, norm, proj, na, selfa, causal, outp, final)

        @block.tensor
        def _(pe):
            def mm(*args, **kw):
                return nc.tensor.matmul(*args, skip_group_check=True, **kw)

            def setup():
                pe.wait_ge(s_const, 16 * 10)
                pe.wait_ge(s_dram, 16 * (3 + 8 + 10))
                for n in range(2):
                    for i in range(4):
                        h = 4 * n + i
                        table = XN[:, 1 + h // 3, (h % 3) * RUNP:(h % 3 + 1) * RUNP].rearrange(
                            "p (r c) -> p r c", c=PADC)[:, :, 0:28]
                        mm(SC[:, i * 512:i * 512 + TTW], YT[:, 1, 0:P], table, start=True, stop=True)\
                            .then_inc(s_setp, 1)
                    if n == 0:
                        pe.wait_ge(s_set, 3)

            def load(b):
                pe.wait_ge(s_x, b * 48 + 48)
                for t in range(NT):
                    pe.wait_ge(s_xe, b * NT + (CREDIT + t - 1))
                    for k in range(KC):
                        last = nc.tensor.transpose(TP[:, t % 2, k * P:(k + 1) * P],
                                                   YT[:, t, k * P:(k + 1) * P], ident[:, :])
                    last.then_inc(s_xt, 1)

            def norm(b, layer):
                d0 = b * 2 + layer
                pe.wait_ge(s_st, d0 * 6 + 1)
                mm(SC[:, 0:KC], avg[:, :], mv[:, :, 0], start=True, stop=True).then_inc(s_gp, 1)
                pe.wait_ge(s_st, d0 * 6 + 4)
                mm(SC[:, 512:512 + KC], avg[:, :], dv[:, :], start=True, stop=True).then_inc(s_gp, 1)

            def proj(kind, b, g):
                gi = group_index(kind, b, g)
                pe.wait_ge(s_w, gi * 16 + 16)
                for c in range(NCH):
                    for m in (1, 0):
                        n = 2 * c + (1 - m)
                        if n == 1:
                            pe.wait_ge(s_ws, gi + 1)
                        if n >= 3:
                            pe.wait_ge(s_lo, gi * (2 * NCH) + (n - 2))
                        for k in range(KC):
                            last = mm(SC[:, (n % 3) * 512:(n % 3) * 512 + CH], Wg[:, k, m * P:(m + 1) * P],
                                      XN[:, k, c * CH:(c + 1) * CH], start=(k == 0), stop=(k == KC - 1))
                        last.then_inc(s_pq, 1)
                v0 = v_base(kind, b, g)
                for n, (t0, w) in enumerate(v_banks(kind)):
                    if n >= 2:
                        pe.wait_ge(s_pe, v0 + (n - 1))
                    bank = SC[:, (3 + n % 2) * 512:(4 + n % 2) * 512]
                    for i in range(w):
                        t = t0 + i
                        if kind == "na":
                            pe.wait_ge(s_vw, (b * G0 + g) * (CW * NB) + (t + 1))
                        for k in range(KC):
                            if kind == "na":
                                tok = band_tokens(t)[:, k, :]
                                rows = BAND
                            else:
                                tok = XN[:, k, t * P:(t + 1) * P]
                                rows = P
                            last = mm(bank[0:rows, i * P:(i + 1) * P], tok, Wg[:, k, 2 * P:3 * P],
                                      start=(k == 0 and i == 0), stop=(k == KC - 1))
                    last.then_inc(s_pv, 1)

            def na(b, g):
                n0 = b * (G0 * H0 * NT) + g * (H0 * NT)
                with pe.Fori(0, H0 // 2) as hp:
                    m0 = n0 + hp * (2 * NT)
                    total = 2 * NT

                    def scores(n, base=0):
                        slot, (t, cw, cls, lo, nb) = (n // NT) % 2, NA_TILES[n % NT]
                        if n % NT == 0:
                            pe.wait_ge(s_stk[slot], stk_base("na", b, g) + hp * STK_NA + STK_NA)
                        pe.wait_ge(n_ad, m0 + (CREDIT + n - RING + 1))
                        keys = KST[:, slot, :].rearrange("p (r c) -> p r c", c=HW)[
                            :, lo * BR:(lo + nb) * BR, COL0[cw]:COL0[cw] + BW]
                        bank = SC[:, (n % RING) * 512:(n % RING) * 512 + nb * BAND]
                        mm(bank, QS[:, slot, t * P:(t + 1) * P], keys, start=True, stop=True)\
                            .then_inc(n_sc, 1)

                    def pv(n):
                        t, cw, cls, lo, nb = NA_TILES[n % NT]
                        pe.wait_ge(n_ev, m0 + (n + 1))
                        pe.wait_ge(n_nr, m0 + (CREDIT + n - 1))
                        for k in range(nb):
                            last = mm(OV_NA[n % 2], PT[0:BAND, n % 2, k * P:(k + 1) * P],
                                      Vb[0:BAND, cw * NB + lo + k, :],
                                      start=(k == 0), stop=(k == nb - 1))
                        last.then_inc(n_pv, 1)

                    for n in range(2):
                        scores(n)
                    for n in range(total):
                        if n + 2 < total:
                            scores(n + 2)
                        pe.wait_ge(n_ex, m0 + (n + 1))
                        nb = NA_TILES[n % NT][4]
                        for k in range(nb):
                            last = nc.tensor.transpose(TP[0:BAND, n % 2, k * P:(k + 1) * P],
                                                       Pb[:, (n % 4) * 512 + k * BAND:(n % 4) * 512 + (k + 1) * BAND],
                                                       ident[:, :])
                        last.then_inc(n_tp, 1)
                        if n >= 1:
                            pv(n - 1)
                    pv(total - 1)

            def transposes(chunk, slot, s, at):
                k0, w = chunk
                for k in range(0, w, P):
                    r = min(P, w - k)
                    last = nc.tensor.transpose(TP[0:r, slot, k:k + P], Pb[:, k0 + k:k0 + k + r], ident[:, :])
                last.then_inc(s["tp"], 1)

            def selfa(b, g):
                gi = b * G0 + g
                u0 = gi * UNITS

                def maximum(u, n):
                    slot, j = u % 3, u // NCH
                    if n == 0:
                        pe.wait_ge(f_q[slot], gi * (UNITS // 3 * 48) + (u // 3 + 1) * 48)
                        if u % NCH == 0:
                            pe.wait_ge(s_stk[j % 2], stk_base("self", b, g) + (j // 2 + 1) * STK_SELF)
                    pe.wait_ge(f_cm, (u0 + u) * NM + (CREDIT + n - 1))
                    i, (o, w) = n // NC0, SELF_CHUNKS[n % NC0]
                    q0 = slot * CH + i * P
                    mm(AM[(u * NM + n) % 2][:, 0:w], QS[0:3 * D0, 0, q0:q0 + P],
                       KST[0:3 * D0, j % 2, o:o + w], start=True, stop=True).then_inc(f_am, 1)

                def rows(u, i):
                    pe.wait_ge(f_ml, (u0 + u) * UT + (i + 1))
                    pe.wait_ge(f_mr, (u0 + u) * UT + (CREDIT + i))
                    nc.tensor.transpose(MT[:, i * P:(i + 1) * P], MM[:, (u * UT + i) % 2, :].bitcast(F32),
                                        ident[:, :]).then_inc(f_mt, 1)

                def scores(u, p):
                    slot, j = u % 3, u // NCH
                    n = u * PAIRS + p
                    if p == 0:
                        pe.wait_ge(f_mr, (u0 + u) * UT + (CREDIT + UT))
                    pe.wait_ge(f_ex, u0 * PAIRS + (CREDIT + n - 1))
                    for k in range(2):
                        t = 2 * p + k
                        last = mm(ST[:, n % 2, k, 0:CH], KST[:, j % 2, t * P:(t + 1) * P],
                                  QS[:, 0, slot * CH:(slot + 1) * CH], start=True, stop=True)
                    last.then_inc(f_st, 1)

                def pv(u, p):
                    n = u * PAIRS + p
                    pe.wait_ge(f_ex, u0 * PAIRS + (CREDIT + n + 1))
                    if p == 0:
                        pe.wait_ge(f_nr, u0 + (CREDIT + u))
                    for k in range(2):
                        t = 2 * p + k
                        last = mm(OV[0:2 * D0, 0:CH], VX[:, t, u // NCH, :],
                                  Pb[:, (n % 3) * 2 * CH + k * CH:(n % 3) * 2 * CH + (k + 1) * CH],
                                  start=(t == 0), stop=(t == NT - 1))
                    last.then_inc(f_pv, 1)

                for n in range(NM):
                    maximum(0, n)
                for i in range(UT):
                    rows(0, i)
                for u in range(UNITS):
                    for p in range(PAIRS):
                        scores(u, p)
                        if u + 1 < UNITS:
                            for n in M_AT[p]:
                                maximum(u + 1, n)
                            if p in MT_AT:
                                rows(u + 1, MT_AT[p])
                        if p:
                            pv(u, p - 1)
                        elif u:
                            pv(u - 1, PAIRS - 1)
                pv(UNITS - 1, PAIRS - 1)

            def causal(b, g):
                s = dense["c"]
                gi = b * G1 + g
                tiles = [(j, i) for j in range(H1) for i in range(NT)]
                sc0 = gi * (H1 * L1_PER_HEAD)
                t0 = gi * (H1 * NT)
                ex = 0
                ev = {"a": 0, "d": 0}

                def scores(n, c):
                    j, i = tiles[n]
                    o, w = L1_CHUNKS[i][c]
                    if i == 0 and c == 0:
                        pe.wait_ge(s_stk[j], stk_base("causal", b, g) + STK_C)
                        pe.wait_ge(c_kg, gi * H1 + (j + 1))
                    r = slice(D1 * j, D1 * j + D1)
                    q = slice(i * P, (i + 1) * P)
                    bank = SC[:, o:o + w]
                    u = (HW - 1 - i * P // HW) * HW + o
                    mm(bank, QS[:, j, q], KST[:, j, o:o + w], start=True, stop=False)
                    mm(bank, QL[r, q], KH[r, o:o + w], start=False, stop=False)
                    mm(bank, qoh[:, i % 3, :], KG[j][:, u:u + w], start=False, stop=True)\
                        .then_inc(s["sc"], 1)

                def pv(n, c):
                    j, i = tiles[n]
                    if c == 0 :
                        pe.wait_ge(s["nr"], t0 + (n + CREDIT))
                    who, slot = EVC[n, c]
                    ev[who] += 1
                    pe.wait_ge(s["ev" + who], gi * EVC_TOTAL[who] + ev[who])
                    o, w = L1_CHUNKS[i][c]
                    for k in range(0, w, P):
                        rows = min(P, w - k)
                        end = o + k + rows == causal_keys(i)
                        last = mm(OV[:, 0:P], PT[0:rows, slot, k:k + P], V[0:rows, (o + k) // P, :], start=(o + k == 0), stop=end)
                    if end:
                        last.then_inc(s["pv"], 1)

                behind = None
                for c in range(len(L1_CHUNKS[0])):
                    scores(0, c)
                for n, (j, i) in enumerate(tiles):
                    here = len(L1_CHUNKS[i])
                    ahead = len(L1_CHUNKS[tiles[n + 1][1]]) if n + 1 < len(tiles) else 0
                    for c in range(max(here, ahead)):
                        if c < here:
                            ex += 1
                            pe.wait_ge(s["ex"], sc0 + ex)
                            transposes(L1_CHUNKS[i][c], EVC[n, c][1], s, None)
                        if c < ahead:
                            scores(n + 1, c)
                        if c < here:
                            if behind is not None:
                                pv(*behind)
                            behind = (n, c)
                pv(*behind)

            def outp(b, layer):
                n0 = b * (2 * NCH) + layer * NCH
                pe.wait_ge(s_wo, b * 32 + 16 * (layer + 1))
                for c in range(NCH):
                    for t in range(3):
                        n = 3 * c + t
                        if n >= 2:
                            pe.wait_ge(s_oy, n0 * 3 + (n - 1))
                        for k in range(KC if layer else G0):
                            last = nc.tensor.transpose(TP[:, n % 2, k * P:(k + 1) * P],
                                                       (YT if layer else YA)[:, n, k * P:(k + 1) * P],
                                                       ident[:, :])
                        last.then_inc(s_op, 1)
                    if c > 0:
                        products(b, layer, c - 1)
                products(b, layer, NCH - 1)

            def products(b, layer, c):
                n0 = b * (2 * NCH) + layer * NCH
                pe.wait_ge(s_oy, n0 * 3 + 3 * (c + 1))
                for m in range(KC):
                    n = c * KC + m
                    if n >= 4:
                        pe.wait_ge(s_oa, n0 * KC + (CREDIT + n - 3))
                    for k in range(KC):
                        last = mm(SC[:, (n % 4) * 512:(n % 4) * 512 + CH], Wo[:, k, m * P:(m + 1) * P],
                                  yT[:, c % 2, k, :], start=(k == 0), stop=(k == KC - 1))
                    last.then_inc(s_om, 1)

            def final(b):
                for t in range(NT):
                    if t >= 2:
                        pe.wait_ge(s_fe, b * NT + (t - 1))
                    for k in range(KC):
                        last = nc.tensor.transpose(TP[:, t % 2, k * P:(k + 1) * P],
                                                   XN[:, k, t * P:(t + 1) * P], ident[:, :])
                    last.then_inc(s_ft, 1)

            run_phases(pe, setup, load, norm, proj, na, selfa, causal, outp, final)

        @block.scalar
        def _(act):
            def setup():
                act.sem_inc(s_xe, CREDIT)
                for s in dense.values():
                    act.sem_inc(s["nr"], CREDIT)
                    act.sem_inc(s["dn"], CREDIT)
                for s in (f_cm, f_mt, f_mr, f_ex, f_pv, f_nr):
                    act.sem_inc(s, CREDIT)
                act.sem_inc(n_ad, CREDIT)
                act.sem_inc(n_nr, CREDIT)
                act.sem_inc(s_oa, CREDIT)

            def load(b):
                for t in range(0, NT, 2):
                    act.wait_ge(s_xt, b * NT + (t + 1))
                    if t:
                        act.wait_ge(s_xe, b * NT + (CREDIT + t))
                    nc.scalar.activation(XN[:, :, t * P:(t + 1) * P],
                                         TP[:, t % 2, :].rearrange("p (k n) -> p k n", k=KC),
                                         ACT.Copy).then_inc(s_xe, 1)

            def norm(b, layer):
                d0 = b * 2 + layer
                act.wait_ge(s_st, d0 * 6 + 5)
                nc.scalar.activation(sd[:, :], dv[:, :], ACT.Sqrt, bias=epst[:, 0:1]).then_inc(s_sq, 1)

            def proj(kind, b, g):
                gi = group_index(kind, b, g)
                for n in range(2 * NCH):
                    c, m = n // 2, 1 - n % 2
                    act.wait_ge(s_pq, gi * (2 * NCH) + (n + 1))
                    src = SC[:, (n % 3) * 512:(n % 3) * 512 + CH]
                    dst = (QH, KH)[m][:, c * CH:(c + 1) * CH]
                    if kind == "causal":
                        nc.scalar.activation(dst, src, ACT.Copy).then_inc(s_hi, 1)
                        continue
                    row = {"na": 0, "self": G0}[kind]
                    bias = bsel[:, m:m + 1]
                    if n == 0:
                        nc.scalar.activation(bsel[:, :], bqkv[:, bass.ds(g + row, 1), :].rearrange(
                            "p o n -> p (o n)"), ACT.Copy).then_inc(s_bs, 1)
                        act.wait_ge(s_bs, (b * (2 * G0) + g + (row + 1)))
                    if kind == "na" and m == 0:
                        dst = dst.rearrange("p (w r c) -> p w r c", w=CW, c=QW)
                        src = src.rearrange("p (r w c) -> p w r c", w=CW, c=QW)
                    nc.scalar.activation(dst, src, ACT.Identity, bias=bias).then_inc(s_hi, 1)
                v0 = v_base(kind, b, g)
                for n, (t0, w) in enumerate(v_banks(kind)):
                    if n % 2:
                        continue
                    act.wait_ge(s_pv, v0 + (n + 1))
                    if n:
                        act.wait_ge(s_pe, v0 + n)
                    nc.scalar.activation(*v_copy(kind, n, t0, w), ACT.Copy).then_inc(s_pe, 1)

            def na(b, g):
                n0 = b * (G0 * H0 * NT) + g * (H0 * NT)
                with act.Fori(0, H0 // 2) as hp:
                    m0 = n0 + hp * (2 * NT)

                    def copy(n):
                        nb = NA_TILES[n % NT][4]
                        act.wait_ge(n_tp, m0 + (n + 1))
                        nc.scalar.activation(PT[0:BAND, n % 2, 0:nb * P], TP[0:BAND, n % 2, 0:nb * P],
                                             ACT.Copy).then_inc(n_ev, 1)

                    for n in range(2 * NT):
                        w = NA_TILES[n % NT][4] * BAND
                        act.wait_ge(n_nm, m0 + (n + 1))
                        p = Pb[:, (n % 4) * 512:(n % 4) * 512 + w]
                        nc.scalar.activation(p, p, ACT.Exp, bias=nmax[:, n % RING:n % RING + 1],
                                             accum_out=rsum[:, n % RING, 0:1]).then_inc(n_ex, 1)
                        if n:
                            copy(n - 1)
                    copy(2 * NT - 1)

            def selfa(b, g):
                n0 = (b * G0 + g) * (UNITS * PAIRS)
                for n in range(UNITS * PAIRS):
                    act.wait_ge(f_st, n0 + (n + 1))
                    act.wait_ge(f_pv, n0 + (CREDIT + n - 2))
                    nc.scalar.activation(
                        Pb[:, (n % 3) * 2 * CH:(n % 3 + 1) * 2 * CH].rearrange("p (k n) -> p k n", k=2),
                        ST[:, n % 2, :, 0:CH], ACT.Exp).then_inc(f_ex, 1)

            def causal(b, g):
                s = dense["c"]
                gi = b * G1 + g
                tp0 = gi * (H1 * L1_PER_HEAD)
                t0 = gi * (H1 * NT)
                tp = 0
                pending = None

                def copy(n, c, count):
                    who, slot = EVC[n, c]
                    if who == "a":
                        w = -(-L1_CHUNKS[n % NT][c][1] // P) * P
                        act.wait_ge(s["tp"], tp0 + count)
                        nc.scalar.activation(PT[:, slot, 0:w], TP[:, slot, 0:w], ACT.Copy)\
                            .then_inc(s["eva"], 1)

                for n in range(H1 * NT):
                    i = n % NT
                    act.wait_ge(s["nm"], t0 + (n + 1))
                    act.wait_ge(s["dn"], t0 + (n + CREDIT - 1))
                    for c, (o, w) in enumerate(L1_CHUNKS[i]):
                        nc.scalar.activation(Pb[:, o:o + w], SC[:, o:o + w], ACT.Exp,
                                             bias=nmax[:, n % 2:n % 2 + 1],
                                             accum_out=rsum[:, n % 2, c:c + 1]).then_inc(s["ex"], 1)
                        if c:
                            copy(n, c - 1, tp + c)
                    tp += len(L1_CHUNKS[i])
                    copy(n, len(L1_CHUNKS[i]) - 1, tp)

            def outp(b, layer):
                n0 = b * (2 * NCH) + layer * NCH
                for c in range(NCH):
                    for t in range(3):
                        n = 3 * c + t
                        act.wait_ge(s_op, n0 * 3 + (n + 1))
                        if t == 0 and c >= 2:
                            act.wait_ge(s_om, n0 * KC + KC * (c - 1))
                        src = TP[:, n % 2, :].rearrange("p (k n) -> p k n", k=KC)
                        dst = yT[:, c % 2, :, t * P:(t + 1) * P]
                        if layer == 0:
                            for k in range(G0):
                                d_ = yT[:, c % 2, k, :].rearrange("p (r w c) -> p w r c", w=CW, c=QW)[:, t]
                                s_ = src[:, k, :].rearrange("p (r c) -> p r c", c=QW)
                                ins = nc.scalar.activation(d_, s_, ACT.Identity, bias=bqkv[:, k, 2:3])
                            if t < G0:
                                k = G0 + t
                                ins = nc.scalar.activation(yT[:, c % 2, k, :], YC[:, t, c * CH:(c + 1) * CH],
                                                           ACT.Identity, bias=bqkv[:, k, 2:3])
                            ins.then_inc(s_oy, 1)
                        else:
                            nc.scalar.activation(dst, src, ACT.Copy).then_inc(s_oy, 1)

            def final(b):
                for t in range(0, NT, 2):
                    act.wait_ge(s_ft, b * NT + (t + 1))
                    if t:
                        act.wait_ge(s_fe, b * NT + t)
                    nc.scalar.activation(YT[:, t, :], TP[:, t % 2, :], ACT.Copy).then_inc(s_fe, 1)

            run_phases(act, setup, load, norm, proj, na, selfa, causal, outp, final)

        @block.vector
        def _(dve):
            def setup():
                nc.vector.memset(epst[:, :], EPS)
                nc.vector.memset(YT[:, 3, :], 0.0)
                nc.vector.memset(YT[:, 15, :], 0.0)
                nc.vector.memset(XN.ap(), 0.0).then_inc(s_set, 1)
                dve.wait_ge(s_const, 16 * 10)
                n = a["relp"].shape[1]
                nc.vector.tensor_copy(YT[0:8, 14, n:2 * HW - 1],
                                      YT[0:8, 14, n - 1:n].to_broadcast([8, 2 * HW - 1 - n])).then_inc(s_set, 1)
                nc.vector.tensor_scalar(bqkv[:, :, 0], bqkv[:, :, 0], SCALE0, None, ALU.mult)
                nc.vector.tensor_copy(qoh.ap(), YT[:, 0, 0:3 * P].rearrange("p (n q) -> p n q", n=3))
                for n in range(2):
                    dve.wait_ge(s_setp, 4 * (n + 1))
                    for i in range(4):
                        ins = nc.vector.tensor_copy(YT[:, 4 + 4 * n + i, 0:TTW], SC[:, i * 512:i * 512 + TTW])
                    ins.then_inc(s_set, 1)
                dve.wait_ge(s_dram, 16 * (3 + 8 + 10))
                ts = YT[:, 3, 0:8 * NU].rearrange("p (h n) -> p h n", h=8)
                ps = YT[:, 15, 0:8 * HW].rearrange("p (h n) -> p h n", h=8)
                mask = YT[:, 2, 0:NU].rearrange("p (o n) -> p o n", o=1).to_broadcast([P, 8, NU])
                nc.vector.tensor_tensor(ts, ts, mask, ALU.add).then_inc(s_vd, 1)
                dve.wait_ge(s_vd, 1)
                n = 1
                for dst, src, width in ((PS, ps, HW), (TS, ts, NU)):
                    part = QL[:, 0:8 * width].rearrange("p (h n) -> p h n", h=8)
                    nc.vector.tensor_copy(part, src).then_inc(s_vd, 1)
                    dve.wait_ge(s_vd, n + 1)
                    nc.vector.tensor_copy(dst[0:64], part[0:64].bitcast(F32))
                    nc.vector.tensor_tensor(dst[64:P], src[64:P], part[64:P].bitcast(F32), ALU.subtract)\
                        .then_inc(s_vd, 1)
                    dve.wait_ge(s_vd, n + 2)
                    n += 2

            def load(b):
                for t in range(1, NT, 2):
                    dve.wait_ge(s_xt, b * NT + (t + 1))
                    dve.wait_ge(s_xe, b * NT + (CREDIT + t))
                    nc.vector.tensor_copy(XN[:, :, t * P:(t + 1) * P],
                                          TP[:, t % 2, :].rearrange("p (k n) -> p k n", k=KC)).then_inc(s_xe, 1)

            def norm(b, layer):
                d0 = b * 2 + layer
                for k in range(KC):
                    for c in range(NCH):
                        ins = nc.vector.bn_stats(st[:, c, :], XN[:, k, c * CH:(c + 1) * CH])
                    ins.then_inc(s_bn, 1)
                    hold(dve, s_bn, d0 * (2 * KC) + (2 * k + 1))
                    nc.vector.bn_aggr(mv[:, k, :], st.ap()).then_inc(s_bn, 1)
                    hold(dve, s_bn, d0 * (2 * KC) + (2 * k + 2))
                dve.engine_nop().then_inc(s_st, 1)
                dve.wait_ge(s_gp, d0 * 2 + 1)
                nc.vector.tensor_copy(gm[:, :], SC[:, 0:KC]).then_inc(s_st, 1)
                dve.wait_ge(s_st, d0 * 6 + 2)
                nc.vector.tensor_tensor(dv[:, :], mv[:, :, 0], gm[:, :], ALU.subtract).then_inc(s_st, 1)
                dve.wait_ge(s_st, d0 * 6 + 3)
                nc.vector.tensor_tensor(sd[:, :], dv[:, :], dv[:, :], ALU.mult).then_inc(s_sqr, 1)
                dve.wait_ge(s_sqr, d0 + 1)
                nc.vector.tensor_tensor(dv[:, :], sd[:, :], mv[:, :, 1], ALU.add).then_inc(s_st, 1)
                dve.wait_ge(s_gp, d0 * 2 + 2)
                nc.vector.tensor_copy(dv[:, :], SC[:, 512:512 + KC]).then_inc(s_st, 1)
                dve.wait_ge(s_sq, d0 + 1)
                nc.vector.reciprocal(rstd[:, :], sd[:, :]).then_inc(s_st, 1)
                dve.wait_ge(s_st, d0 * 6 + 6)
                dve.wait_ge(s_save, d0 * 16 + 16)
                for k in range(KC):
                    nc.vector.tensor_scalar(XN[:, k, :], XN[:, k, :], gm[:, k:k + 1], rstd[:, k:k + 1],
                                            ALU.subtract, ALU.mult)

            def proj(kind, b, g):
                gi = group_index(kind, b, g)
                for n in range(2 * NCH):
                    c, m = n // 2, 1 - n % 2
                    dve.wait_ge(s_hi, gi * (2 * NCH) + (n + 1))
                    src = SC[:, (n % 3) * 512:(n % 3) * 512 + CH]
                    hi = (QH, KH)[m][:, c * CH:(c + 1) * CH]
                    lo = (QL, KL)[m][:, c * CH:(c + 1) * CH]
                    if kind == "na" and m == 0:
                        src = src.rearrange("p (r w c) -> p w r c", w=CW, c=QW)
                        hi = hi.rearrange("p (w r c) -> p w r c", w=CW, c=QW)
                        lo = lo.rearrange("p (w r c) -> p w r c", w=CW, c=QW)
                    if kind == "causal":
                        ins = nc.vector.tensor_tensor(lo, src, hi.bitcast(F32), ALU.subtract)
                    else:
                        parts = [(lo, src, hi)] if kind != "na" or m else [
                            (lo[:, w], src[:, w], hi[:, w]) for w in range(CW)]
                        for lo_, src_, hi_ in parts:
                            ins = nc.vector.scalar_tensor_tensor(
                                out=lo_, in0=src_, scalar=bsel[:, m:m + 1], in1=hi_.bitcast(F32),
                                op0=ALU.add, op1=ALU.subtract)
                    ins.then_inc(s_lo, 1)
                v0 = v_base(kind, b, g)
                for n, (t0, w) in enumerate(v_banks(kind)):
                    if n % 2 == 0:
                        continue
                    dve.wait_ge(s_pv, v0 + (n + 1))
                    dve.wait_ge(s_pe, v0 + n)
                    nc.vector.tensor_copy(*v_copy(kind, n, t0, w)).then_inc(s_pe, 1)

            def na(b, g):
                n0 = b * (G0 * H0 * NT) + g * (H0 * NT)
                with dve.Fori(0, H0 // 2) as hp:
                    m0 = n0 + hp * (2 * NT)
                    k0 = (b * (G0 * H0) + g * H0 + hp * 2) * NTAB

                    def norm_out(n):
                        e, t = n % RING, NA_TILES[n % NT][0]
                        dve.wait_ge(n_pv, m0 + (n + 1))
                        nc.vector.reciprocal(rden[:, e:e + 1], rsum[:, e, 0:1]).then_inc(n_rd, 1)
                        dve.wait_ge(n_rd, m0 + (n + 1))
                        nc.vector.tensor_scalar(
                            YA[:, t, bass.ds(g * P + hp * (2 * D0) + (n // NT) * D0, D0)],
                            OV_NA[n % 2][:, bass.ds(hp * (2 * D0) + (n // NT) * D0, D0)], rden[:, e:e + 1], None, ALU.mult).then_inc(n_nr, 1)

                    for n in range(2 * NT):
                        t, cw, cls, lo, nb = NA_TILES[n % NT]
                        tb = (n // NT) * NTAB + NA_TABLE_OF[n % NT]
                        if n >= 3:
                            norm_out(n - 3)
                        dve.wait_ge(n_sc, m0 + (n + 1))
                        hold(dve, n_tab, k0 + (tb + 1))
                        w = nb * BAND
                        nc.vector.tensor_tensor_reduce(
                            out=Pb[:, (n % 4) * 512:(n % 4) * 512 + w].rearrange("p (r c) -> p r c", c=BW),
                            in0=SC[:, (n % RING) * 512:(n % RING) * 512 + w].rearrange("p (r c) -> p r c", c=BW),
                            in1=tab[:, tb % TAB_RING, 0:nb * BR, :], scale=1.0, scalar=-3e38,
                            op0=ALU.add, op1=ALU.max, accum_out=cmax[:, n % 2:n % 2 + 1]).then_inc(n_ad, 1)
                        dve.wait_ge(n_ad, m0 + (CREDIT + n + 1))
                        nc.vector.tensor_scalar(nmax[:, n % RING:n % RING + 1], cmax[:, n % 2:n % 2 + 1], -1.0, None,
                                                ALU.mult).then_inc(n_nm, 1)
                    for n in range(2 * NT - 3, 2 * NT):
                        norm_out(n)

            def negate_max(s, e, chunks, count):
                dve.wait_ge(s["cm"], count)
                nc.vector.tensor_reduce(nmax[:, e:e + 1], cmax[:, 0:chunks], AX.X, ALU.max, negate=True)\
                    .then_inc(s["nm"], 1)

            def finish(s, e, chunks, count, exps, mine, out):
                dve.wait_ge(s["ex"], exps)
                nc.vector.tensor_reduce(den[:, e:e + 1], rsum[:, e, 0:chunks], AX.X, ALU.add)\
                    .then_inc(s["dn"], 1)
                dve.wait_ge(s["dn"], count + CREDIT)
                nc.vector.reciprocal(rden[:, e:e + 1], den[:, e:e + 1]).then_inc(s["rd"], 1)
                dve.wait_ge(s["rd"], count)
                dve.wait_ge(s["pv"], count)
                nc.vector.tensor_scalar(out, OV[:, mine], rden[:, e:e + 1], None, ALU.mult)\
                    .then_inc(s["nr"], 1)

            def selfa(b, g):
                gi = b * G0 + g
                u0 = gi * UNITS
                nc.vector.memset(MM.ap().bitcast(F32), 0.0)

                def maximum(u, n):
                    i, (o, w) = n // NC0, SELF_CHUNKS[n % NC0]
                    dve.wait_ge(f_am, (u0 + u) * NM + (n + 1))
                    nc.vector.tensor_reduce(cmax[:, n % NC0:n % NC0 + 1], AM[(u * NM + n) % 2][:, 0:w],
                                            AX.X, ALU.max).then_inc(f_cm, 1)
                    if n % NC0 < NC0 - 1:
                        return
                    e, t = (u * UT + i) % 2, (u0 + u) * UT + (i + 1)
                    dve.wait_ge(f_cm, (u0 + u) * NM + (CREDIT + n + 1))
                    nc.vector.tensor_reduce(um[:, e:e + 1], cmax[:, 0:NC0], AX.X, ALU.max, negate=True)\
                        .then_inc(f_um, 1)
                    dve.wait_ge(f_um, t)
                    dve.wait_ge(f_mt, t + (CREDIT - 2))
                    nc.vector.tensor_copy(MM[:, e, 0:1], um[:, e:e + 1]).then_inc(f_mh, 1)
                    dve.wait_ge(f_mh, t)
                    nc.vector.tensor_tensor(MM[:, e, 1:2], um[:, e:e + 1], MM[:, e, 0:1].bitcast(F32),
                                            ALU.subtract).then_inc(f_ml, 1)

                def rows(u, i):
                    q0 = (u % 3) * CH + i * P
                    dve.wait_ge(f_mt, (u0 + u) * UT + (CREDIT + i + 1))
                    nc.vector.tensor_copy(QS[3 * D0:4 * D0, 0, q0:q0 + P], MT[:, i * P:(i + 1) * P])\
                        .then_inc(f_mr, 1)

                def out_of(u):
                    j, c = u // NCH, u % NCH
                    dve.wait_ge(f_pv, (u0 + u) * PAIRS + (CREDIT + PAIRS))
                    nc.vector.reciprocal(rec[:, :], OV[D0:2 * D0, 0:CH]).then_inc(f_rd, 1)
                    dve.wait_ge(f_rd, u0 + (u + 1))
                    nc.vector.tensor_tensor(
                        YC[D0 * j:D0 * j + D0, bass.ds(g, 1), c * CH:(c + 1) * CH].rearrange("p o n -> p (o n)"),
                        OV[0:D0, 0:CH], rec[:, :], ALU.mult).then_inc(f_nr, 1)

                for n in range(NM):
                    maximum(0, n)
                for i in range(UT):
                    rows(0, i)
                for u in range(UNITS):
                    for p in range(PAIRS):
                        if u + 1 < UNITS:
                            for n in M_AT[p]:
                                maximum(u + 1, n)
                            if p in MT_AT:
                                rows(u + 1, MT_AT[p])
                        if p == 0 and u:
                            out_of(u - 1)
                out_of(UNITS - 1)

            def causal(b, g):
                s = dense["c"]
                gi = b * G1 + g
                sc0 = gi * (H1 * L1_PER_HEAD)
                t0 = gi * (H1 * NT)
                for j in range(H1):
                    ps = PS[:, bass.ds(g * H1 + j, 1), :].to_broadcast([P, NU, HW])
                    ts = TS[:, bass.ds(g * H1 + j, 1), :].rearrange("p o u -> p u o").to_broadcast([P, NU, HW])
                    nc.vector.tensor_tensor(KG[j].ap().rearrange("p (u n) -> p u n", n=HW), ps, ts, ALU.add)\
                        .then_inc(c_kg, 1)
                sc = [0]

                def chunk_max(n, c):
                    o, w = L1_CHUNKS[n % NT][c]
                    sc[0] += 1
                    dve.wait_ge(s["sc"], sc0 + sc[0])
                    nc.vector.tensor_reduce(cmax[:, c:c + 1], SC[:, o:o + w], AX.X, ALU.max)\
                        .then_inc(s["cm"], 1)

                def out_of(n):
                    i, j = n % NT, n // NT
                    exps = j * L1_PER_HEAD + sum(len(L1_CHUNKS[x]) for x in range(i + 1))
                    finish(s, n % 2, len(L1_CHUNKS[i]), t0 + (n + 1), sc0 + exps, slice(j * D1, (j + 1) * D1),
                           YT[:, i, bass.ds(g * P + j * D1, D1)])

                chunk_max(0, 0)
                negate_max(s, 0, 1, sc0 + sc[0])
                tp = 0
                for n in range(H1 * NT):
                    here = len(L1_CHUNKS[n % NT])
                    ahead = len(L1_CHUNKS[(n + 1) % NT]) if n + 1 < H1 * NT else 0
                    for c in range(max(here, ahead)):
                        if c < here:
                            tp += 1
                            who, slot = EVC[n, c]
                            if who == "d":
                                w = -(-L1_CHUNKS[n % NT][c][1] // P) * P
                                dve.wait_ge(s["tp"], sc0 + tp)
                                nc.vector.tensor_copy(PT[:, slot, 0:w], TP[:, slot, 0:w]).then_inc(s["evd"], 1)
                        if c < ahead:
                            chunk_max(n + 1, c)
                        if c == 0 and n:
                            out_of(n - 1)
                    if ahead:
                        negate_max(s, (n + 1) % 2, ahead, sc0 + sc[0])
                out_of(H1 * NT - 1)

            def outp(b, layer):
                n0 = b * (2 * NCH * KC) + layer * NCH * KC
                for c in range(NCH):
                    for m in range(KC):
                        n = c * KC + m
                        dve.wait_ge(s_om, n0 + (n + 1))
                        dve.wait_ge(s_or[n % 2], n0 * 8 + 16 * (n // 2 + 1))
                        dst = XN[:, m, :].rearrange("p (c r) -> p r c", r=HW)[:, c * QR:(c + 1) * QR, :]
                        src = SC[:, (n % 4) * 512:(n % 4) * 512 + CH].rearrange("p (r c) -> p r c", c=HW)
                        add = res[:, n % 2, :].rearrange("p (r c) -> p r c", c=HW)
                        if layer == 0:
                            nc.vector.scalar_tensor_tensor(out=dst, in0=src, scalar=bproj[:, m:m + 1], in1=add,
                                                           op0=ALU.add, op1=ALU.add).then_inc(s_oa, 1)
                        else:
                            nc.vector.tensor_tensor(dst, src, add, ALU.add).then_inc(s_oa, 1)

            def final(b):
                for t in range(1, NT, 2):
                    dve.wait_ge(s_ft, b * NT + (t + 1))
                    dve.wait_ge(s_fe, b * NT + t)
                    nc.vector.tensor_copy(YT[:, t, :], TP[:, t % 2, :]).then_inc(s_fe, 1)

            run_phases(dve, setup, load, norm, proj, na, selfa, causal, outp, final)

        @block.gpsimd
        def _(pool):
            def proj(kind, b, g):
                gi = group_index(kind, b, g)
                hold(pool, s_w, gi * 16 + 16)
                q = Wg[:, :, 0:P]
                scale = SCALE1 if kind == "causal" else SCALE0
                nc.gpsimd.tensor_scalar(q, q, scale, None, ALU.mult).then_inc(s_ws, 1)
                if kind == "self":
                    o0 = (b * G0 + g) * 3
                    hold(pool, s_ws, gi + 1)
                    nc.gpsimd.memset(VX[:, :, :, D0:2 * D0], 1.0).then_inc(s_one, 1)
                    for slot in range(2):
                        hold(pool, s_one, o0 + (slot + 1))
                        nc.gpsimd.memset(KST[3 * D0:4 * D0, slot, :].bitcast(F32), 1.0).then_inc(s_one, 1)
                if kind == "na":
                    v0 = v_base(kind, b, g)
                    for t in range(CW * NB):
                        if t >= V_RING:
                            hold(pool, s_pv, v0 + ((t - V_RING) // 4 + 1))
                        cw, rb = t // NB, t % NB
                        grid = XN.ap().rearrange("p k (r c) -> p k r c", c=HW)
                        nc.gpsimd.tensor_copy(
                            band_tokens(t).rearrange("p k (r c) -> p k r c", c=BW),
                            grid[:, :, rb * BR:(rb + 1) * BR, COL0[cw]:COL0[cw] + BW]).then_inc(s_vw, 1)

            def na(b, g):
                h0 = b * (G0 * H0) + g * H0
                n0 = b * (G0 * H0 * NT) + g * (H0 * NT)
                for j in range(H0):
                    hold(pool, n_tt[j % 2], (b * G0 + g) * (H0 // 2 * 16) + (j // 2 + 1) * 16)
                    for x, (cw, cls, nb, n) in enumerate(NA_TABLES):
                        r0 = BR if cls == 0 else 0
                        c0 = 6 - (QW * cw - COL0[cw])
                        k = j * NTAB + x
                        nr = nb * BR
                        if k:
                            hold(pool, n_tab, h0 * NTAB + k)
                        rows = rowm[:, cls, 0:nr].rearrange("p (r o) -> p r o", o=1).to_broadcast([P, nr, BW])
                        nc.gpsimd.tensor_tensor(tmpt[:, 0:nr, 0:BW], TT[:, j % 2, r0:r0 + nr, c0:c0 + BW],
                                                rows, ALU.add).then_inc(n_tmp, 1)
                        hold(pool, n_tmp, h0 * NTAB + (k + 1))
                        if k >= TAB_RING:
                            kk = k - TAB_RING + 1
                            done = (kk // NTAB) * NT + NA_TABLES[kk % NTAB][3]
                            hold(pool, n_ad, n0 + (CREDIT + done))
                        cols = colm[:, cw:cw + 1, :].to_broadcast([P, nr, BW])
                        nc.gpsimd.tensor_tensor(tab[:, k % TAB_RING, 0:nr, :], tmpt[:, 0:nr, 0:BW], cols,
                                                ALU.add).then_inc(n_tab, 1)

            run_phases(pool, nothing, nothing, nothing, proj, na, nothing, nothing, nothing, nothing)


def constants():
    f = np.float32
    c = {"ident": np.eye(P, dtype=f), "rev": np.eye(P, dtype=f)[::-1].copy(),
         "avg": np.kron(np.eye(P // 16, dtype=f), np.full((16, 16), 1 / 16, f))}
    qoh = np.zeros((P, 3, P), f)
    for phase in range(3):
        for p in range(P):
            tok = P * phase + p
            r = tok // HW - P * phase // HW
            for base in (0, 64):
                qoh[base + HW - 1 - tok % HW, phase, p] = 1
                qoh[base + HW + 3 - r, phase, p] = 1
    c["qoh"] = qoh.reshape(P, 3 * P)
    tmask = np.zeros((P, NU), f)
    for r in range(4):
        for base in (0, 64):
            tmask[base + HW + 3 - r, HW - 1 + r + 1:] = -BIG
    c["tmask"] = tmask

    def outside(q, key):
        first = min(max(q - KS // 2, 0), HW - KS)
        return not first <= key < first + KS

    rowm, colm = np.zeros((P, 3, 16), f), np.zeros((P, 3, BW), f)
    for p in range(P):
        for cls, (q0, w0) in enumerate(((0, 0), (QR, QR - BR), (HW - QR, HW - QR - BR))):
            for k in range(16):
                rowm[p, cls, k] = -BIG if outside(q0 + p // QW, w0 + k) else 0
        for cw in range(CW):
            for k in range(BW):
                colm[p, cw, k] = -BIG if outside(QW * cw + p % QW, COL0[cw] + k) else 0
    c["rowm"], c["colm"] = rowm, colm
    return c


def kernel(**inputs):
    import concourse.bacc as bacc
    from concourse.bass_utils import run_bass_kernel_spmd

    arr = {k: np.asarray(v) for k, v in inputs.items()}
    x = arr["x"].reshape(B, T, C)
    wqkv = arr["L0_conv_W_qkv"].reshape(KC, P, 2, 3, 2, P)
    w0 = wqkv.transpose(2, 4, 1, 0, 3, 5).reshape(2 * G0, P, KC, 3 * P)
    w1 = np.stack([arr["L1_conv_Wq"], arr["L1_conv_Wk"], arr["L1_conv_Wv"]]).reshape(3, KC, P, G1, P)
    w1 = w1.transpose(3, 2, 1, 0, 4).reshape(G1, P, KC, 3 * P)
    wo = np.stack([arr["L0_conv_W_proj"], arr["L1_conv_Wo"]]).reshape(2, KC, P, C).transpose(0, 2, 1, 3)
    bqkv = arr["L0_conv_b_qkv"].reshape(2, 3, 2, P).transpose(3, 0, 2, 1).reshape(P, 2 * G0, 3)
    given = {"x": x, "wgrp": np.concatenate([w0, w1]), "wo": wo, "bqkv": bqkv,
             "bproj": arr["L0_conv_b_proj"].reshape(KC, P).T, "rpb": arr["L0_conv_rpb"],
             "relt": arr["L1_conv_rel_pos_bias"].T, "relp": arr["L1_conv_particle_rel_pos_bias"].T,
             **constants()}
    given = {k: np.ascontiguousarray(v) for k, v in given.items()}
    nc = bacc.Bacc("TRN2", target_bir_lowering=False, num_devices=1)
    a = {k: nc.dram_tensor(f"in_{k}", v.shape, F32, kind="ExternalInput").ap() for k, v in given.items()}
    a["out"] = nc.dram_tensor("out", (B, T, C), F32, kind="ExternalOutput").ap()
    build(nc, a)
    r = run_bass_kernel_spmd(nc, [{f"in_{k}": v for k, v in given.items()}], core_ids=[0])
    return np.asarray(r.results[0]["out"]).reshape(B, HW, HW, C)
```

```python
from contextlib import ExitStack

import numpy as np
import concourse.bass as bass
from concourse import mybir

F32 = mybir.dt.float32
F32R = mybir.dt.float32r
ALU = mybir.AluOpType
ACT = mybir.ActivationFunctionType
AX = mybir.AxisListType

B = 2
HW = 48
T = HW * HW
C = 512
P = 128
KC = C // P
NT = T // P
CH = 384
NCH = T // CH
EPS = 1e-5
BIG = 1e30

D0 = 32
H0 = P // D0
G0 = 2
SCALE0 = float(D0) ** -0.5
KS = 7
QR, QW = 8, 16
BR, BW = 4, 22
BAND = BR * BW
NB = HW // BR
CW = HW // QW
COL0 = [0, 13, 26]
QT_NA = NT
RPB = 2 * KS - 1
PADR, PADC = 23, 43
OFFR, OFFC = 5, 15
TTW = 16 * 28
RUN = 15 * PADC + 28
RUNP = 16 * PADC

D1 = 64
H1 = P // D1
G1 = 4
HEADS1 = 8
SCALE1 = float(D1) ** -0.5
NU = HW + 3
KGW = NU * HW

NG = 2 * G0 + G1
CREDIT = 8
RING = 4


def chunks_of(keys):
    out, o = [], 0
    while keys - o > 512:
        w = 512
        while keys - o - w < 256:
            w -= P
        out.append((o, w))
        o += w
    return out + [(o, keys - o)]


SELF_CHUNKS = chunks_of(T)
NC0 = len(SELF_CHUNKS)
UT = CH // P
UNITS = H0 * T // CH
NM = UT * NC0
PAIRS = NT // 2
LD = 192
VW = 2 * D0 + 1

BESIDE = [[("max", 0), ("max", 1), ("max", 2)],
          [("max", 3), ("max", 4)],
          [("max", 5), ("max", 6)],
          [("row", 0), ("out", None), ("max", 7)],
          [("max", 8), ("max", 9)],
          [("max", 10), ("max", 11)],
          [("row", 1), ("max", 12), ("max", 13)],
          [("max", 14)],
          [("row", 2)]]


def beside(u, p):
    return [(kind, u - 1 if kind == "out" else u + 1, n) for kind, n in BESIDE[p]
            if (u > 0 if kind == "out" else u + 1 < UNITS)]


AHEAD = [(kind, 0, n) for p in BESIDE for kind, n in p if kind != "out"]
RING_AT = {}
for _item in AHEAD + [i for u in range(UNITS) for p in range(PAIRS) for i in beside(u, p)]\
        + [("out", UNITS - 1, None)]:
    RING_AT[_item] = len(RING_AT)
ITEMS = len(RING_AT)


def causal_keys(i):
    return ((P * (i + 1) - 1) // HW + 1) * HW


L1_CHUNKS = [chunks_of(causal_keys(i)) for i in range(NT)]
L1_PER_HEAD = sum(len(c) for c in L1_CHUNKS)

TILES1 = H1 * NT
CHUNK_AT = {}
for _n in range(TILES1):
    for _c in range(len(L1_CHUNKS[_n % NT])):
        CHUNK_AT[_n, _c] = len(CHUNK_AT)
NK = len(CHUNK_AT)
BANKS = 5
V1W = P + 1


def causal_order():
    at = sorted(CHUNK_AT, key=CHUNK_AT.get)
    last = [k for k in range(NK) if k + 1 == NK or at[k + 1][0] != at[k][0]]
    cost = {"scores": 1.25, "transpose": 0.84, "product": 1.72, "exp": 0.95, "copy": 0.95, "maximum": 1.2}
    engines = {"pe": ("scores", "transpose", "product"), "act": ("exp", "copy"), "dve": ("maximum", "out")}
    latency, small = 220, 350
    end = {kind: [] for kinds in engines.values() for kind in kinds}

    def ready(kind, k):
        n = at[k][0] if kind != "out" else k
        needs = {"scores": [("exp", k - BANKS)],
                 "transpose": [("exp", k), ("copy", k - 2)],
                 "product": [("copy", k), ("out", n - 1 if at[k][1] == 0 else -1)],
                 "exp": [("maximum", last[n]), ("transpose", k - BANKS)],
                 "copy": [("transpose", k), ("product", k - 2)],
                 "maximum": [("scores", k)],
                 "out": [("product", last[n])]}[kind]
        ends = [0]
        for other, i in needs:
            if i >= 0:
                if i >= len(end[other]):
                    return float("inf")
                ends.append(end[other][i] + latency)
        return max(ends)

    clock, order = dict.fromkeys(engines, 0), {e: [] for e in engines}
    for _ in range(6 * NK + TILES1):
        start, _, engine, kind = min(
            (max(clock[e], ready(kind, len(end[kind]))), i, e, kind)
            for e, kinds in engines.items() for i, kind in enumerate(kinds)
            if len(end[kind]) < (TILES1 if kind == "out" else NK))
        k = len(end[kind])
        if kind == "out":
            took = small
        else:
            n, c = at[k]
            took = cost[kind] * L1_CHUNKS[n % NT][c][1] + (small if kind == "maximum" and last[n] == k else 0)
        clock[engine] = start + took
        end[kind].append(start + took)
        order[engine].append((kind, *(at[k] if kind != "out" else (k,))))
    return order


ORDER1 = causal_order()


def na_tiles():
    out = []
    for cw in range(CW):
        for rt in range(HW // QR):
            lo = max(QR * rt - BR, 0) // BR
            hi = min(QR * rt + QR + BR, HW) // BR
            cls = 0 if rt == 0 else 2 if rt == HW // QR - 1 else 1
            out.append((rt * CW + cw, cw, cls, lo, hi - lo))
    return out


NA_TILES = na_tiles()
NA_TABLES = []
NA_TABLE_OF = []
for _n, (_t, _cw, _cls, _lo, _nb) in enumerate(NA_TILES):
    if not NA_TABLES or NA_TABLES[-1][:2] != (_cw, _cls):
        NA_TABLES.append((_cw, _cls, _nb, _n))
    NA_TABLE_OF.append(len(NA_TABLES) - 1)
NTAB = len(NA_TABLES)
TAB_RING = 3


def build(nc, a):
    ctx = ExitStack()
    with ctx:
        def sb(name, shape, dt=F32):
            return ctx.enter_context(nc.sbuf_tensor(name, shape, dt))

        def sem(name):
            return ctx.enter_context(nc.semaphore(name))

        def overlay(*choices):
            made, largest = [], max(choices, key=lambda c: sum(int(np.prod(s[1][1:])) for s in c))
            for c in choices:
                if c is not largest:
                    with ExitStack() as scope:
                        made += [scope.enter_context(nc.sbuf_tensor(n, s, d)) for n, s, d in c]
            made += [sb(n, s, d) for n, s, d in largest]
            return {t.name: t for t in made}

        def dram(name, shape):
            return nc.dram_tensor(name, shape, F32).ap()

        res_d = dram("res_d", (P, KC, T))
        rpb_d = dram("rpb_d", (8, PADR, PADC))
        v_d = dram("v_d", (T, P))
        tt_d = dram("tt_d", (8, P, TTW))
        part_d = dram("part_d", (8, 2 * HW - 1))

        XN = sb("XN", [P, KC, T])
        YT = sb("YT", [P, NT, C])
        o = overlay([("QH", [P, T], F32R)], [("KG1", [P, KGW], F32R)])
        QH, KG1 = o["QH"], o["KG1"]
        QL = sb("QL", [P, T], F32R)
        KH, KL = sb("KH", [P, T], F32R), sb("KL", [P, T], F32R)
        o = overlay([("KST", [P, 2, T], F32R), ("QS", [P, 2, T], F32R)],
                    [("yT", [P, 2, KC, CH], F32)])
        KST, QS, yT = o["KST"], o["QS"], o["yT"]
        o = overlay([("Vb", [P, CW * NB, P], F32)],
                    [("VX", [P, NT, H0, VW], F32R)],
                    [("VC", [P, NT, V1W], F32)],
                    [("res", [P, 2, CH], F32)])
        VX = o["VX"]
        Vb, VC, res = o["Vb"], o["VC"], o["res"]
        o = overlay([("KG0", [P, KGW], F32R)],
                    [("TT", [P, 2, 16, 28], F32), ("tmpt", [P, 16, 28], F32),
                     ("tab", [P, TAB_RING, 16, BW], F32)],
                    [("PHI", [P, 3, 2 * CH], F32R)])
        KG0, TT, tmpt, tab = o["KG0"], o["TT"], o["tmpt"], o["tab"]
        KG = [KG0, KG1]
        PHI, PLO = o["PHI"], QS[:, 1, :].rearrange("p (s n) -> p s n", s=3)
        Wg = sb("Wg", [P, KC, 3 * P])
        Wo = sb("Wo", [P, KC, C])
        Pb = sb("Pb", [P, BANKS * 512])
        PT = sb("PT", [P, 2, 512])
        st = PT[:, 0, 0:KC * NCH * 6].rearrange("p (k c n) -> p k c n", k=KC, n=6)
        ident = sb("ident", [P, P])
        avg = sb("avg", [P, P])
        qoh = sb("qoh", [P, 3, P], F32R)
        PS = sb("PS", [P, 8, HW])
        TS = sb("TS", [P, 8, NU])
        rowm = sb("rowm", [P, 3, 16])
        colm = sb("colm", [P, 3, BW])
        bqkv = sb("bqkv", [P, 2 * G0, 3])
        bproj = sb("bproj", [P, KC])
        epst = sb("epst", [P, 1])
        mv = sb("mv", [P, KC, 2])
        gm = sb("gm", [P, KC])
        dv = sb("dv", [P, KC])
        sd = sb("sd", [P, KC])
        rstd = sb("rstd", [P, KC])
        cmax = sb("cmax", [P, 2 * NC0])
        nmax = sb("nmax", [P, RING])
        rsum = sb("rsum", [P, RING, 1])
        um = sb("um", [P, 2])
        MM = sb("MM", [P, 2, D0], F32R)
        un = sb("un", [P, UT, D0])
        urec = sb("urec", [P, UT])
        rden = sb("rden", [P, RING])
        bsel = sb("bsel", [P, 3])

        SC = ctx.enter_context(nc.psum_tensor("SC", [P, 5 * 512], F32))
        TP = ctx.enter_context(nc.psum_tensor("TP", [P, 2, 512], F32))
        OV = ctx.enter_context(nc.psum_tensor("OV", [P, 512], F32))
        OV_NA = [OV[:, 0:P], SC[:, 4 * 512:4 * 512 + P]]
        ST = SC[:, 0:4 * 512].rearrange("p (s k n) -> p s k n", s=2, k=2)
        AM = [SC[:, 4 * 512:5 * 512], TP[:, 0, :]]
        OU = [OV[0:VW, 0:CH], TP[0:VW, 1, 0:CH]]
        UC = PT[0:VW, :, 0:CH]

        s_bar = sem("s_bar")
        s_held = sem("s_held")
        s_const = sem("s_const")
        s_dram = sem("s_dram")
        s_set = sem("s_set")
        s_setp = sem("s_setp")
        s_x = [sem(f"s_x{i}") for i in range(3)]
        s_xt = sem("s_xt")
        s_xe = sem("s_xe")
        s_save = sem("s_save")
        s_st = sem("s_st")
        s_ls = sem("s_ls")
        s_bn = sem("s_bn")
        s_sqr = sem("s_sqr")
        s_vd = sem("s_vd")
        s_bs = sem("s_bs")
        s_gp = sem("s_gp")
        s_sq = sem("s_sq")
        s_w = sem("s_w")
        s_ws = sem("s_ws")
        s_one = sem("s_one")
        s_wo = sem("s_wo")
        s_pq = sem("s_pq")
        s_hi = sem("s_hi")
        s_lo = sem("s_lo")
        s_vs = sem("s_vs")
        s_vb = sem("s_vb")
        s_pv = sem("s_pv")
        s_pe = sem("s_pe")
        s_vh = sem("s_vh")
        s_stk = [sem(f"s_stk{i}") for i in range(2)]
        n_tt = [sem(f"n_tt{i}") for i in range(2)]
        n_tmp = sem("n_tmp")
        n_tab = sem("n_tab")
        n_sc = sem("n_sc")
        n_ad = sem("n_ad")
        n_nm = sem("n_nm")
        n_ex = sem("n_ex")
        n_tp = sem("n_tp")
        n_ev = sem("n_ev")
        n_pv = sem("n_pv")
        n_rd = sem("n_rd")
        n_nr = sem("n_nr")
        f_q = [sem(f"f_q{i}") for i in range(3)]
        f_am = sem("f_am")
        f_cm = sem("f_cm")
        f_um = sem("f_um")
        f_ml = sem("f_ml")
        f_st = sem("f_st")
        f_ex = sem("f_ex")
        f_eh = sem("f_eh")
        f_ld = sem("f_ld")
        f_lp = sem("f_lp")
        f_pv = sem("f_pv")
        f_uc = sem("f_uc")
        f_nr = sem("f_nr")
        c_sc = sem("c_sc")
        c_cm = sem("c_cm")
        c_nm = sem("c_nm")
        c_ex = sem("c_ex")
        c_tp = sem("c_tp")
        c_ev = sem("c_ev")
        c_pv = sem("c_pv")
        c_rd = sem("c_rd")
        c_nr = sem("c_nr")
        c_kg = [sem(f"c_kg{i}") for i in range(H1)]
        s_op = sem("s_op")
        s_oy = sem("s_oy")
        s_om = sem("s_om")
        s_or = [sem(f"s_or{i}") for i in range(2)]
        s_oa = sem("s_oa")
        s_ft = sem("s_ft")
        s_fe = sem("s_fe")
        s_out = sem("s_out")

        block = ctx.enter_context(nc.Block())

        ENGINES = 5
        PH = 2 + 2 * G0 + 2 * G0 + 2 + 2 * G1 + 2

        SAVES = (3 + KC) * 16

        def hold(eng, semaphore, value):
            eng.wait_ge(semaphore, value)
            eng.sem_inc(s_held, 1)

        def phase_end(eng, n):
            eng.drain().then_inc(s_bar, 1)
            hold(eng, s_bar, ENGINES * n)

        def run_phases(eng, setup, load, norm, proj, na, selfa, causal, outp, final):
            setup()
            phase_end(eng, 1)
            with eng.Fori(0, B) as b:
                ph = b * PH + 1
                load(b)
                phase_end(eng, ph + 1)
                norm(b, 0)
                phase_end(eng, ph + 2)
                with eng.Fori(0, G0) as g:
                    proj("na", b, g)
                    phase_end(eng, ph + g * 2 + 3)
                    na(b, g)
                    phase_end(eng, ph + g * 2 + 4)
                with eng.Fori(0, G0) as g:
                    proj("self", b, g)
                    phase_end(eng, ph + g * 2 + (3 + 2 * G0))
                    selfa(b, g)
                    phase_end(eng, ph + g * 2 + (4 + 2 * G0))
                outp(b, 0)
                phase_end(eng, ph + (3 + 4 * G0))
                norm(b, 1)
                phase_end(eng, ph + (4 + 4 * G0))
                with eng.Fori(0, G1) as g:
                    proj("causal", b, g)
                    phase_end(eng, ph + g * 2 + (5 + 4 * G0))
                    causal(b, g)
                    phase_end(eng, ph + g * 2 + (6 + 4 * G0))
                outp(b, 1)
                phase_end(eng, ph + (5 + 4 * G0 + 2 * G1))
                final(b)
                phase_end(eng, ph + (6 + 4 * G0 + 2 * G1))

        def nothing(*_):
            pass

        def group_index(kind, b, g):
            return b * NG + g + {"na": 0, "self": G0, "causal": 2 * G0}[kind]

        V_BANKS = [(t, min(4, NT - t)) for t in range(0, NT, 4)]
        NV = len(V_BANKS)

        def v_copy(kind, n, t0, w):
            src = SC[:, (3 + n % 2) * 512:(3 + n % 2) * 512 + w * P]
            src = src.rearrange("p (t n) -> p t n", n=P)
            if kind == "na":
                return Pb[:, t0 * P:(t0 + w) * P].rearrange("p (t n) -> p t n", n=P), src
            return VC[:, t0:t0 + w, 0:P], src

        def v_split(n, t0, w):
            src = SC[:, (3 + n % 2) * 512:(3 + n % 2) * 512 + w * P]
            return (VX[:, t0:t0 + w, :, 0:D0], VX[:, t0:t0 + w, :, D0:2 * D0],
                    src.rearrange("p (t h n) -> p t h n", h=H0, n=D0))

        def bias_operand(eng, g, j):
            ps = PS[:, bass.ds(g * H1 + j, 1), :].to_broadcast([P, NU, HW])
            ts = TS[:, bass.ds(g * H1 + j, 1), :].rearrange("p o u -> p u o").to_broadcast([P, NU, HW])
            eng.tensor_tensor(KG[j].ap().rearrange("p (u n) -> p u n", n=HW), ps, ts, ALU.add)\
                .then_inc(c_kg[j], 1)

        STK_NA, STK_SELF, STK_C = 8 * 16, 3 * 16, 4 * 16
        STK_IMG = G0 * H0 // 2 * (STK_NA + STK_SELF) + G1 * H1 // 2 * STK_C

        def stk_base(kind, b, g):
            return b * STK_IMG + {
                "na": g * (H0 // 2 * STK_NA),
                "self": g * (H0 // 2 * STK_SELF) + G0 * H0 // 2 * STK_NA,
                "causal": g * (H1 // 2 * STK_C) + G0 * H0 // 2 * (STK_NA + STK_SELF)}[kind]

        @block.sync
        def _(sp):
            def setup():
                consts = [(ident, a["ident"]), (avg, a["avg"]), (rowm, a["rowm"]), (colm, a["colm"]),
                          (bqkv, a["bqkv"]), (bproj, a["bproj"])]
                for dst, src in consts:
                    sp.dma_start(dst.ap(), src).then_inc(s_const, 16)
                sp.dma_start(YT[:, 0, 0:3 * P], a["qoh"]).then_inc(s_const, 16)
                sp.dma_start(YT[:, 1, 0:P], a["rev"]).then_inc(s_const, 16)
                sp.dma_start(YT[:, 2, 0:NU], a["tmask"]).then_inc(s_const, 16)
                n = a["relp"].shape[1]
                sp.dma_start(YT[0:8, 14, 0:n], a["relp"]).then_inc(s_const, 16)
                sp.wait_ge(s_set, 1)
                sp.dma_start(rpb_d, XN[0:8, 0, 0:PADR * PADC].rearrange("h (r c) -> h r c", c=PADC))\
                    .then_inc(s_dram, 16)
                sp.wait_ge(s_dram, 16)
                sp.dma_start(rpb_d[:, OFFR:OFFR + RPB, OFFC:OFFC + RPB], a["rpb"]).then_inc(s_dram, 16)
                sp.wait_ge(s_set, 2)
                sp.dma_start(part_d, YT[0:8, 14, 0:2 * HW - 1]).then_inc(s_dram, 16)
                sp.wait_ge(s_dram, 48)
                for h in range(8):
                    src = bass.AP(rpb_d.tensor, h * PADR * PADC, [[PADC, QR], [1, QW], [1, RUN]])
                    sp.dma_start(XN[:, 1 + h // 3, (h % 3) * RUNP:(h % 3) * RUNP + RUN], src).then_inc(s_dram, 16)
                for base in (0, 64):
                    src = bass.AP(part_d.tensor, 0, [[1, HW], [2 * HW - 1, 8], [1, HW]])
                    sp.dma_start(YT[base:base + HW, 15, 0:8 * HW].rearrange("p (h n) -> p h n", h=8), src)\
                        .then_inc(s_dram, 16)
                    for r in range(4):
                        u = 3 - r
                        dst = YT[base + HW + r:base + HW + r + 1, 3, 0:8 * NU].rearrange(
                            "p (h n) -> p h n", h=8)[:, :, u:NU]
                        sp.dma_start(dst, a["relt"][:, 0:NU - u].rearrange("(o h) n -> o h n", o=1))\
                            .then_inc(s_dram, 16)
                sp.wait_ge(s_set, 4)
                for h in range(8):
                    sp.dma_start(tt_d[h], YT[:, 4 + h, 0:TTW]).then_inc(s_dram, 16)
                sp.wait_ge(s_dram, 16 * (3 + 8 + 10 + 8))
                weights(0)
                sp.wait_ge(s_w, 16)

            def weights(n):
                sp.dma_start(Wg.ap(), a["wgrp"][bass.ds(n, 1)].rearrange("o p k n -> p (o k) n"))\
                    .then_inc(s_w, 16)

            def load(b):
                for part in range(3):
                    w = NT // 3
                    src = a["x"][bass.ds(b, 1), part * w * P:(part + 1) * w * P, :].rearrange(
                        "o (t p) c -> p (o t) c", p=P)
                    sp.dma_start(YT[:, part * w:(part + 1) * w, :], src).then_inc(s_x[part], 16)
                for part in range(3):
                    hold(sp, s_x[part], b * 16 + 16)
                for part in range(3):
                    hold(sp, s_xe, b * NT + (CREDIT + (part + 1) * w))
                    sp.dma_start(res_d[:, :, part * w * P:(part + 1) * w * P],
                                 XN[:, :, part * w * P:(part + 1) * w * P]).then_inc(s_save, 16)

            def norm(b, layer):
                sp.dma_start(Wo.ap(), a["wo"][layer]).then_inc(s_wo, 16)
                hold(sp, s_save, b * SAVES + (SAVES if layer else 3 * 16))

            def proj(kind, b, g):
                gi = group_index(kind, b, g)
                hold(sp, s_lo, (gi + 1) * (2 * NCH))
                if kind == "self":
                    queries(0)
                    keys(0)
                    queries(1)
                    queries(2)
                    keys(1)
                elif kind == "causal":
                    for j in range(H1):
                        r = slice(D1 * j, D1 * j + D1)
                        for i, src in enumerate((KH, KL)):
                            sp.dma_start(KST[D1 * i:D1 * i + D1, j, :].bitcast(F32), src[r, :].bitcast(F32))\
                                .then_inc(s_stk[j], 16)
                        for i in range(2):
                            sp.dma_start(QS[D1 * i:D1 * i + D1, j, :].bitcast(F32), QH[r, :].bitcast(F32))\
                                .then_inc(s_stk[j], 16)
                else:
                    for j in range(2):
                        stack(j, g * H0 + j)
                    hold(sp, s_pe, (gi + 1) * NV)
                    sp.dma_start(v_d.rearrange("(t p) n -> p t n", p=P),
                                 Pb[:, 0:T].rearrange("p (t n) -> p t n", n=P)).then_inc(s_vs, 16)
                    hold(sp, s_vs, (b * G0 + g + 1) * 16)
                    for cw in range(CW):
                        for r in range(BR):
                            src = bass.AP(v_d.tensor, (r * HW + COL0[cw]) * P,
                                          [[P, BW], [BR * HW * P, NB], [1, P]])
                            sp.dma_start(Vb[r * BW:(r + 1) * BW, cw * NB:(cw + 1) * NB, :], src)\
                                .then_inc(s_vb, 16)

            def stack(j, h):
                r, slot = slice(D0 * j, D0 * j + D0), j % 2
                for i, (q, k) in enumerate(((QH, KH), (QH, KL), (QL, KH), (QL, KL))):
                    sp.dma_start(KST[D0 * i:D0 * i + D0, slot, :].bitcast(F32), k[r, :].bitcast(F32))\
                        .then_inc(s_stk[slot], 16)
                    sp.dma_start(QS[D0 * i:D0 * i + D0, slot, :].bitcast(F32), q[r, :].bitcast(F32))\
                        .then_inc(s_stk[slot], 16)
                sp.dma_start(TT[:, j % 2], tt_d[bass.ds(h, 1)].rearrange(
                    "o p (r c) -> p (o r) c", c=28)).then_inc(n_tt[j % 2], 16)

            def keys(j):
                for i, src in enumerate((KH, KL, KH)):
                    sp.dma_start(KST[D0 * i:D0 * i + D0, j % 2, :].bitcast(F32),
                                 src[D0 * j:D0 * j + D0, :].bitcast(F32)).then_inc(s_stk[j % 2], 16)

            def queries(u):
                j, c, slot = u // NCH, u % NCH, u % 3
                for i, src in enumerate((QH, QH, QL)):
                    sp.dma_start(QS[D0 * i:D0 * i + D0, 0, slot * CH:(slot + 1) * CH].bitcast(F32),
                                 src[D0 * j:D0 * j + D0, c * CH:(c + 1) * CH].bitcast(F32))\
                        .then_inc(f_q[slot], 16)

            def stacks_end(kind, b, g, each):
                for slot in range(2):
                    hold(sp, s_stk[slot], stk_base(kind, b, g) + each)

            def na(b, g):
                n0 = b * (G0 * H0 * NT) + g * (H0 * NT)
                h0 = b * (G0 * H0) + g * H0
                weights(g + 1)
                for j in range(2, H0):
                    hold(sp, n_sc, n0 + NT * (j - 1))
                    hold(sp, n_tab, (h0 + (j - 1)) * NTAB)
                    stack(j, g * H0 + j)
                hold(sp, s_vb, (b * G0 + g + 1) * (CW * BR * 16))
                hold(sp, s_w, group_index("na", b, g) * 16 + 32)
                stacks_end("na", b, g, H0 // 2 * STK_NA)
                for slot in range(2):
                    hold(sp, n_tt[slot], (b * G0 + g + 1) * (H0 // 2 * 16))

            def selfa(b, g):
                u0 = (b * G0 + g) * UNITS
                weights(g + (G0 + 1))
                for u in range(3, UNITS):
                    hold(sp, f_st, (u0 + (u - 2)) * PAIRS)
                    queries(u)
                    if u % NCH == 2 and u // NCH + 1 < H0:
                        keys(u // NCH + 1)
                stacks_end("self", b, g, H0 // 2 * STK_SELF)
                hold(sp, s_w, group_index("self", b, g) * 16 + 32)
                for slot in range(3):
                    hold(sp, f_q[slot], (b * G0 + g + 1) * (UNITS // 3 * 48))

            def causal(b, g):
                weights(g + (2 * G0 + 1))
                stacks_end("causal", b, g, H1 // 2 * STK_C)
                hold(sp, s_w, group_index("causal", b, g) * 16 + 32)

            def outp(b, layer):
                n0 = b * (2 * NCH * KC) + layer * NCH * KC
                for c in range(NCH):
                    for m in range(KC):
                        n = c * KC + m
                        hold(sp, s_oa, n0 + (CREDIT + n - 1))
                        sp.dma_start(res[:, n % 2, :], res_d[:, m, c * CH:(c + 1) * CH])\
                            .then_inc(s_or[n % 2], 16)
                for m in range(KC if layer == 0 else 0):
                    hold(sp, s_oa, n0 + (CREDIT + (NCH - 1) * KC + m + 1))
                    sp.dma_start(res_d[:, m, :], XN[:, m, :]).then_inc(s_save, 16)
                hold(sp, s_wo, b * 32 + 16 * (layer + 1))
                for slot in range(2):
                    hold(sp, s_or[slot], (n0 + NCH * KC) * 8)

            def final(b):
                for part in range(3):
                    w = NT // 3
                    hold(sp, s_fe, b * NT + (part + 1) * w)
                    dst = a["out"][bass.ds(b, 1), part * w * P:(part + 1) * w * P, :].rearrange(
                        "o (t p) c -> p (o t) c", p=P)
                    sp.dma_start(dst, YT[:, part * w:(part + 1) * w, :]).then_inc(s_out, 16)
                hold(sp, s_out, b * 48 + 48)

            run_phases(sp, setup, load, norm, proj, na, selfa, causal, outp, final)

        @block.tensor
        def _(pe):
            def mm(*args, **kw):
                return nc.tensor.matmul(*args, skip_group_check=True, **kw)

            def setup():
                pe.wait_ge(s_const, 16 * 10)
                pe.wait_ge(s_dram, 16 * (3 + 8 + 10))
                for n in range(2):
                    for i in range(4):
                        h = 4 * n + i
                        table = XN[:, 1 + h // 3, (h % 3) * RUNP:(h % 3 + 1) * RUNP].rearrange(
                            "p (r c) -> p r c", c=PADC)[:, :, 0:28]
                        mm(SC[:, i * 512:i * 512 + TTW], YT[:, 1, 0:P], table, start=True, stop=True)\
                            .then_inc(s_setp, 1)
                    if n == 0:
                        pe.wait_ge(s_set, 3)

            def load(b):
                for t in range(NT):
                    if t % (NT // 3) == 0:
                        pe.wait_ge(s_x[t // (NT // 3)], b * 16 + 16)
                    pe.wait_ge(s_xe, b * NT + (CREDIT + t - 1))
                    for k in range(KC):
                        last = nc.tensor.transpose(TP[:, t % 2, k * P:(k + 1) * P],
                                                   YT[:, t, k * P:(k + 1) * P], ident[:, :])
                    last.then_inc(s_xt, 1)

            def norm(b, layer):
                d0 = b * 2 + layer
                pe.wait_ge(s_st, d0 * 6 + 1)
                mm(SC[:, 0:KC], avg[:, :], mv[:, :, 0], start=True, stop=True).then_inc(s_gp, 1)
                pe.wait_ge(s_st, d0 * 6 + 4)
                mm(SC[:, 512:512 + KC], avg[:, :], dv[:, :], start=True, stop=True).then_inc(s_gp, 1)

            def proj(kind, b, g):
                gi = group_index(kind, b, g)
                pe.wait_ge(s_w, gi * 16 + 16)
                for c in range(NCH):
                    for m in (1, 0):
                        n = 2 * c + (1 - m)
                        if n == 1:
                            pe.wait_ge(s_ws, gi + 1)
                        if n >= 3:
                            pe.wait_ge(s_lo, gi * (2 * NCH) + (n - 2))
                        for k in range(KC):
                            last = mm(SC[:, (n % 3) * 512:(n % 3) * 512 + CH], Wg[:, k, m * P:(m + 1) * P],
                                      XN[:, k, c * CH:(c + 1) * CH], start=(k == 0), stop=(k == KC - 1))
                        last.then_inc(s_pq, 1)
                v0 = gi * NV
                for n, (t0, w) in enumerate(V_BANKS):
                    if n >= 2:
                        pe.wait_ge(s_pe, v0 + (n - 1))
                    bank = SC[:, (3 + n % 2) * 512:(4 + n % 2) * 512]
                    for i in range(w):
                        t = t0 + i
                        for k in range(KC):
                            last = mm(bank[:, i * P:(i + 1) * P], XN[:, k, t * P:(t + 1) * P], Wg[:, k, 2 * P:3 * P],
                                      start=(k == 0 and i == 0), stop=(k == KC - 1))
                    last.then_inc(s_pv, 1)

            def na(b, g):
                n0 = b * (G0 * H0 * NT) + g * (H0 * NT)
                with pe.Fori(0, H0 // 2) as hp:
                    m0 = n0 + hp * (2 * NT)
                    total = 2 * NT

                    def scores(n, base=0):
                        slot, (t, cw, cls, lo, nb) = (n // NT) % 2, NA_TILES[n % NT]
                        if n % NT == 0:
                            pe.wait_ge(s_stk[slot], stk_base("na", b, g) + hp * STK_NA + STK_NA)
                        pe.wait_ge(n_ad, m0 + (CREDIT + n - RING + 1))
                        keys = KST[:, slot, :].rearrange("p (r c) -> p r c", c=HW)[
                            :, lo * BR:(lo + nb) * BR, COL0[cw]:COL0[cw] + BW]
                        bank = SC[:, (n % RING) * 512:(n % RING) * 512 + nb * BAND]
                        mm(bank, QS[:, slot, t * P:(t + 1) * P], keys, start=True, stop=True)\
                            .then_inc(n_sc, 1)

                    def pv(n):
                        t, cw, cls, lo, nb = NA_TILES[n % NT]
                        if n == 0:
                            pe.wait_ge(s_vb, (b * G0 + g + 1) * (CW * BR * 16))
                        pe.wait_ge(n_ev, m0 + (n + 1))
                        pe.wait_ge(n_nr, m0 + (CREDIT + n - 1))
                        for k in range(nb):
                            last = mm(OV_NA[n % 2], PT[0:BAND, n % 2, k * P:(k + 1) * P],
                                      Vb[0:BAND, cw * NB + lo + k, :],
                                      start=(k == 0), stop=(k == nb - 1))
                        last.then_inc(n_pv, 1)

                    for n in range(RING - 1):
                        scores(n)
                    for n in range(total):
                        if n + RING - 1 < total:
                            scores(n + RING - 1)
                        pe.wait_ge(n_ex, m0 + (n + 1))
                        nb = NA_TILES[n % NT][4]
                        for k in range(nb):
                            last = nc.tensor.transpose(TP[0:BAND, n % 2, k * P:(k + 1) * P],
                                                       Pb[:, (n % 4) * 512 + k * BAND:(n % 4) * 512 + (k + 1) * BAND],
                                                       ident[:, :])
                        last.then_inc(n_tp, 1)
                        if n >= 1:
                            pv(n - 1)
                    pv(total - 1)

            def transposes(chunk, slot, s, at):
                k0, w = chunk
                for k in range(0, w, P):
                    r = min(P, w - k)
                    last = nc.tensor.transpose(TP[0:r, slot, k:k + P], Pb[:, k0 + k:k0 + k + r], ident[:, :])
                last.then_inc(s["tp"], 1)

            def selfa(b, g):
                gi = b * G0 + g
                u0 = gi * UNITS

                i0 = gi * ITEMS

                def item(kind, u, n):
                    at = RING_AT[kind, u, n]
                    slot, j = u % 3, u // NCH
                    if kind == "max" and n == 0:
                        pe.wait_ge(f_q[slot], gi * (UNITS // 3 * 48) + (u // 3 + 1) * 48)
                        if u % NCH == 0:
                            pe.wait_ge(s_stk[j % 2], stk_base("self", b, g) + (j // 2 + 1) * STK_SELF)
                    if kind == "row":
                        pe.wait_ge(f_ml, (u0 + u) * UT + (n + 1))
                    if kind == "out":
                        pe.wait_ge(f_uc, u0 + (CREDIT + u + 1))
                    pe.wait_ge(f_cm, i0 + (CREDIT + at - 1))
                    bank = AM[at % 2]
                    if kind == "max":
                        i, (o, w) = n // NC0, SELF_CHUNKS[n % NC0]
                        q0 = slot * CH + i * P
                        last = mm(bank[:, 0:w], QS[0:3 * D0, 0, q0:q0 + P],
                                  KST[0:3 * D0, j % 2, o:o + w], start=True, stop=True)
                    elif kind == "row":
                        last = nc.tensor.transpose(bank[0:D0, 0:P], MM[:, (u * UT + n) % 2, :].bitcast(F32),
                                                   ident[:, :])
                    else:
                        for i in range(UT):
                            last = nc.tensor.transpose(bank[:, i * P:i * P + VW],
                                                       UC[:, u % 2, i * P:(i + 1) * P], ident[0:VW, 0:VW])
                    last.then_inc(f_am, 1)

                def scores(u, p):
                    slot, j = u % 3, u // NCH
                    n = u * PAIRS + p
                    if p == 0:
                        pe.wait_ge(f_cm, i0 + (CREDIT + RING_AT["row", u, UT - 1] + 1))
                    pe.wait_ge(f_eh, u0 * PAIRS + (CREDIT + n - 1))
                    for k in range(2):
                        t = 2 * p + k
                        last = mm(ST[:, n % 2, k, 0:CH], KST[:, j % 2, t * P:(t + 1) * P],
                                  QS[:, 0, slot * CH:(slot + 1) * CH], start=True, stop=True)
                    last.then_inc(f_st, 1)

                def pv(n, k):
                    u, p = n // PAIRS, n % PAIRS
                    t = 2 * p + k
                    part = slice(k * CH, (k + 1) * CH)
                    if k == 0:
                        if p == 0:
                            pe.wait_ge(f_uc, u0 + (CREDIT + u - 1))
                        pe.wait_ge(f_eh, u0 * PAIRS + (CREDIT + n + 1))
                        pe.wait_ge(f_ld, u0 * PAIRS + (n + 1))
                    if k or LD < CH:
                        pe.wait_ge(f_lp, u0 * PAIRS + (n + 1))
                    mm(OU[u % 2], VX[:, t, u // NCH, :], PHI[:, n % 3, part], start=(t == 0), stop=False)
                    last = mm(OU[u % 2], VX[:, t, u // NCH, :], PLO[:, n % 3, part],
                              start=False, stop=(t == NT - 1))
                    if k:
                        last.then_inc(f_pv, 1)

                for it in AHEAD:
                    item(*it)
                for n in range(UNITS * PAIRS):
                    u, p = n // PAIRS, n % PAIRS
                    scores(u, p)
                    items = beside(u, p)
                    for k in range(3):
                        if k and n >= 2:
                            pv(n - 2, k - 1)
                        if k < len(items):
                            item(*items[k])
                for n in (UNITS * PAIRS - 2, UNITS * PAIRS - 1):
                    for k in range(2):
                        pv(n, k)
                item("out", UNITS - 1, None)

            def causal(b, g):
                gi = b * G1 + g
                k0, t0 = gi * NK, gi * TILES1

                def scores(n, c):
                    i, j, at = n % NT, n // NT, CHUNK_AT[n, c]
                    o, w = L1_CHUNKS[i][c]
                    if i == 0 and c == 0:
                        pe.wait_ge(s_stk[j], stk_base("causal", b, g) + STK_C)
                        pe.wait_ge(c_kg[j], gi + 1)
                    pe.wait_ge(c_ex, k0 + (CREDIT + at - BANKS + 1))
                    r = slice(D1 * j, D1 * j + D1)
                    q = slice(i * P, (i + 1) * P)
                    bank = SC[:, (at % BANKS) * 512:(at % BANKS) * 512 + w]
                    u = (HW - 1 - i * P // HW) * HW + o
                    mm(bank, QS[:, j, q], KST[:, j, o:o + w], start=True, stop=False)
                    mm(bank, QL[r, q], KH[r, o:o + w], start=False, stop=False)
                    mm(bank, qoh[:, i % 3, :], KG[j][:, u:u + w], start=False, stop=True)\
                        .then_inc(c_sc, 1)

                def transposes(n, c):
                    at, w = CHUNK_AT[n, c], L1_CHUNKS[n % NT][c][1]
                    pe.wait_ge(c_ex, k0 + (CREDIT + at + 1))
                    pe.wait_ge(c_ev, k0 + (CREDIT + at - 1))
                    for k in range(0, w, P):
                        r = min(P, w - k)
                        p = (at % BANKS) * 512 + k
                        last = nc.tensor.transpose(TP[0:r, at % 2, k:k + P], Pb[:, p:p + r], ident[:, :])
                    last.then_inc(c_tp, 1)

                def pv(n, c):
                    i, at = n % NT, CHUNK_AT[n, c]
                    if c == 0:
                        pe.wait_ge(c_nr, t0 + (CREDIT + n))
                    pe.wait_ge(c_ev, k0 + (CREDIT + at + 1))
                    o, w = L1_CHUNKS[i][c]
                    for k in range(0, w, P):
                        rows = min(P, w - k)
                        last = mm(OV[:, 0:V1W], PT[0:rows, at % 2, k:k + P], VC[0:rows, (o + k) // P, :],
                                  start=(o + k == 0), stop=(o + k + rows == causal_keys(i)))
                    last.then_inc(c_pv, 1)

                for kind, n, c in ORDER1["pe"]:
                    {"scores": scores, "transpose": transposes, "product": pv}[kind](n, c)

            def outp(b, layer):
                n0 = b * (2 * NCH) + layer * NCH
                pe.wait_ge(s_wo, b * 32 + 16 * (layer + 1))
                for c in range(NCH):
                    for t in range(3):
                        n = 3 * c + t
                        if n >= 2:
                            pe.wait_ge(s_oy, n0 * 3 + (n - 1))
                        for k in range(KC):
                            last = nc.tensor.transpose(TP[:, n % 2, k * P:(k + 1) * P],
                                                       YT[:, n, k * P:(k + 1) * P],
                                                       ident[:, :])
                        last.then_inc(s_op, 1)
                    if c > 0:
                        products(b, layer, c - 1)
                products(b, layer, NCH - 1)

            def products(b, layer, c):
                n0 = b * (2 * NCH) + layer * NCH
                pe.wait_ge(s_oy, n0 * 3 + 3 * (c + 1))
                for m in range(KC):
                    n = c * KC + m
                    if n >= 4:
                        pe.wait_ge(s_oa, n0 * KC + (CREDIT + n - 3))
                    for k in range(KC):
                        last = mm(SC[:, (n % 4) * 512:(n % 4) * 512 + CH], Wo[:, k, m * P:(m + 1) * P],
                                  yT[:, c % 2, k, :], start=(k == 0), stop=(k == KC - 1))
                    last.then_inc(s_om, 1)

            def final(b):
                for t in range(NT):
                    if t >= 2:
                        pe.wait_ge(s_fe, b * NT + (t - 1))
                    for k in range(KC):
                        last = nc.tensor.transpose(TP[:, t % 2, k * P:(k + 1) * P],
                                                   XN[:, k, t * P:(t + 1) * P], ident[:, :])
                    last.then_inc(s_ft, 1)

            run_phases(pe, setup, load, norm, proj, na, selfa, causal, outp, final)

        @block.scalar
        def _(act):
            def setup():
                act.sem_inc(s_xe, CREDIT)
                for s in (f_cm, f_eh, f_pv, f_uc, c_ex, c_tp, c_ev, c_pv, c_nr):
                    act.sem_inc(s, CREDIT)
                act.sem_inc(n_ad, CREDIT)
                act.sem_inc(n_nr, CREDIT)
                act.sem_inc(s_oa, CREDIT)

            def load(b):
                for t in range(0, NT, 2):
                    act.wait_ge(s_xt, b * NT + (t + 1))
                    if t:
                        act.wait_ge(s_xe, b * NT + (CREDIT + t))
                    nc.scalar.activation(XN[:, :, t * P:(t + 1) * P],
                                         TP[:, t % 2, :].rearrange("p (k n) -> p k n", k=KC),
                                         ACT.Copy).then_inc(s_xe, 1)

            def norm(b, layer):
                d0 = b * 2 + layer
                act.wait_ge(s_st, d0 * 6 + 5)
                nc.scalar.activation(sd[:, :], dv[:, :], ACT.Sqrt, bias=epst[:, 0:1]).then_inc(s_sq, 1)

            def proj(kind, b, g):
                gi = group_index(kind, b, g)
                for n in range(2 * NCH):
                    c, m = n // 2, 1 - n % 2
                    act.wait_ge(s_pq, gi * (2 * NCH) + (n + 1))
                    src = SC[:, (n % 3) * 512:(n % 3) * 512 + CH]
                    dst = (QH, KH)[m][:, c * CH:(c + 1) * CH]
                    if kind == "causal":
                        nc.scalar.activation(dst, src, ACT.Copy).then_inc(s_hi, 1)
                        continue
                    row = {"na": 0, "self": G0}[kind]
                    bias = bsel[:, m:m + 1]
                    if n == 0:
                        nc.scalar.activation(bsel[:, :], bqkv[:, bass.ds(g + row, 1), :].rearrange(
                            "p o n -> p (o n)"), ACT.Copy).then_inc(s_bs, 1)
                        act.wait_ge(s_bs, (b * (2 * G0) + g + (row + 1)))
                    if kind == "na" and m == 0:
                        dst = dst.rearrange("p (w r c) -> p w r c", w=CW, c=QW)
                        src = src.rearrange("p (r w c) -> p w r c", w=CW, c=QW)
                    nc.scalar.activation(dst, src, ACT.Identity, bias=bias).then_inc(s_hi, 1)
                v0 = gi * NV
                for n, (t0, w) in enumerate(V_BANKS):
                    if kind == "self":
                        act.wait_ge(s_pv, v0 + (n + 1))
                        hi, lo, src = v_split(n, t0, w)
                        nc.scalar.activation(hi, src, ACT.Copy).then_inc(s_vh, 1)
                        continue
                    if n % 2:
                        continue
                    act.wait_ge(s_pv, v0 + (n + 1))
                    if n:
                        act.wait_ge(s_pe, v0 + n)
                    nc.scalar.activation(*v_copy(kind, n, t0, w), ACT.Copy).then_inc(s_pe, 1)

            def na(b, g):
                n0 = b * (G0 * H0 * NT) + g * (H0 * NT)
                with act.Fori(0, H0 // 2) as hp:
                    m0 = n0 + hp * (2 * NT)

                    def copy(n):
                        nb = NA_TILES[n % NT][4]
                        act.wait_ge(n_tp, m0 + (n + 1))
                        nc.scalar.activation(PT[0:BAND, n % 2, 0:nb * P], TP[0:BAND, n % 2, 0:nb * P],
                                             ACT.Copy).then_inc(n_ev, 1)

                    for n in range(2 * NT):
                        w = NA_TILES[n % NT][4] * BAND
                        act.wait_ge(n_nm, m0 + (n + 1))
                        p = Pb[:, (n % 4) * 512:(n % 4) * 512 + w]
                        nc.scalar.activation(p, p, ACT.Exp, bias=nmax[:, n % RING:n % RING + 1],
                                             accum_out=rsum[:, n % RING, 0:1]).then_inc(n_ex, 1)
                        if n:
                            copy(n - 1)
                    copy(2 * NT - 1)

            def selfa(b, g):
                gi = b * G0 + g
                n0 = gi * (UNITS * PAIRS)

                def copy(u):
                    act.wait_ge(f_pv, n0 + (CREDIT + (u + 1) * PAIRS))
                    if u >= 2:
                        act.wait_ge(f_am, gi * ITEMS + (RING_AT["out", u - 2, None] + 1))
                    nc.scalar.activation(UC[:, u % 2, :], OU[u % 2], ACT.Copy).then_inc(f_uc, 1)

                for n in range(UNITS * PAIRS):
                    act.wait_ge(f_st, n0 + (n + 1))
                    act.wait_ge(f_pv, n0 + (CREDIT + n - 2))
                    src = ST[:, n % 2, :, 0:CH]
                    for dst, made in ((Pb[:, (n % 3) * 2 * CH:(n % 3 + 1) * 2 * CH], f_ex),
                                      (PHI[:, n % 3, :], f_eh)):
                        nc.scalar.activation(dst.rearrange("p (k n) -> p k n", k=2), src, ACT.Exp)\
                            .then_inc(made, 1)
                    if n % PAIRS == 2 and n > PAIRS:
                        copy(n // PAIRS - 1)
                copy(UNITS - 1)

            def causal(b, g):
                gi = b * G1 + g
                k0, t0 = gi * NK, gi * TILES1

                def exps(n, c):
                    at, w = CHUNK_AT[n, c], L1_CHUNKS[n % NT][c][1]
                    if c == 0:
                        act.wait_ge(c_nm, t0 + (n + 1))
                    act.wait_ge(c_tp, k0 + (CREDIT + at - BANKS + 1))
                    p = slice((at % BANKS) * 512, (at % BANKS) * 512 + w)
                    nc.scalar.activation(Pb[:, p], SC[:, p], ACT.Exp, bias=nmax[:, n % RING:n % RING + 1])\
                        .then_inc(c_ex, 1)

                def copy(n, c):
                    at, w = CHUNK_AT[n, c], -(-L1_CHUNKS[n % NT][c][1] // P) * P
                    act.wait_ge(c_tp, k0 + (CREDIT + at + 1))
                    act.wait_ge(c_pv, k0 + (CREDIT + at - 1))
                    nc.scalar.activation(PT[:, at % 2, 0:w], TP[:, at % 2, 0:w], ACT.Copy).then_inc(c_ev, 1)

                for kind, n, c in ORDER1["act"]:
                    {"exp": exps, "copy": copy}[kind](n, c)

            def outp(b, layer):
                n0 = b * (2 * NCH) + layer * NCH
                for c in range(NCH):
                    for t in range(3):
                        n = 3 * c + t
                        act.wait_ge(s_op, n0 * 3 + (n + 1))
                        if t == 0 and c >= 2:
                            act.wait_ge(s_om, n0 * KC + KC * (c - 1))
                        src = TP[:, n % 2, :].rearrange("p (k n) -> p k n", k=KC)
                        dst = yT[:, c % 2, :, t * P:(t + 1) * P]
                        if layer == 0:
                            for k in range(KC):
                                d_, s_ = dst[:, k, :], src[:, k, :]
                                if k < G0:
                                    d_ = yT[:, c % 2, k, :].rearrange("p (r w c) -> p w r c", w=CW, c=QW)[:, t]
                                    s_ = s_.rearrange("p (r c) -> p r c", c=QW)
                                ins = nc.scalar.activation(d_, s_, ACT.Identity, bias=bqkv[:, k, 2:3])
                            ins.then_inc(s_oy, 1)
                        else:
                            nc.scalar.activation(dst, src, ACT.Copy).then_inc(s_oy, 1)

            def final(b):
                for t in range(0, NT, 2):
                    act.wait_ge(s_ft, b * NT + (t + 1))
                    if t:
                        act.wait_ge(s_fe, b * NT + t)
                    nc.scalar.activation(YT[:, t, :], TP[:, t % 2, :], ACT.Copy).then_inc(s_fe, 1)

            run_phases(act, setup, load, norm, proj, na, selfa, causal, outp, final)

        @block.vector
        def _(dve):
            def setup():
                nc.vector.memset(epst[:, :], EPS)
                nc.vector.memset(YT[:, 3, :], 0.0)
                nc.vector.memset(YT[:, 15, :], 0.0)
                nc.vector.memset(XN.ap(), 0.0).then_inc(s_set, 1)
                dve.wait_ge(s_const, 16 * 10)
                n = a["relp"].shape[1]
                nc.vector.tensor_copy(YT[0:8, 14, n:2 * HW - 1],
                                      YT[0:8, 14, n - 1:n].to_broadcast([8, 2 * HW - 1 - n])).then_inc(s_set, 1)
                nc.vector.tensor_scalar(bqkv[:, :, 0], bqkv[:, :, 0], SCALE0, None, ALU.mult)
                nc.vector.tensor_copy(qoh.ap(), YT[:, 0, 0:3 * P].rearrange("p (n q) -> p n q", n=3))
                for n in range(2):
                    dve.wait_ge(s_setp, 4 * (n + 1))
                    for i in range(4):
                        ins = nc.vector.tensor_copy(YT[:, 4 + 4 * n + i, 0:TTW], SC[:, i * 512:i * 512 + TTW])
                    ins.then_inc(s_set, 1)
                dve.wait_ge(s_dram, 16 * (3 + 8 + 10))
                ts = YT[:, 3, 0:8 * NU].rearrange("p (h n) -> p h n", h=8)
                ps = YT[:, 15, 0:8 * HW].rearrange("p (h n) -> p h n", h=8)
                mask = YT[:, 2, 0:NU].rearrange("p (o n) -> p o n", o=1).to_broadcast([P, 8, NU])
                nc.vector.tensor_tensor(ts, ts, mask, ALU.add).then_inc(s_vd, 1)
                dve.wait_ge(s_vd, 1)
                n = 1
                for dst, src, width in ((PS, ps, HW), (TS, ts, NU)):
                    part = QL[:, 0:8 * width].rearrange("p (h n) -> p h n", h=8)
                    nc.vector.tensor_copy(part, src).then_inc(s_vd, 1)
                    dve.wait_ge(s_vd, n + 1)
                    nc.vector.tensor_copy(dst[0:64], part[0:64].bitcast(F32))
                    nc.vector.tensor_tensor(dst[64:P], src[64:P], part[64:P].bitcast(F32), ALU.subtract)\
                        .then_inc(s_vd, 1)
                    dve.wait_ge(s_vd, n + 2)
                    n += 2

            def load(b):
                def chunk(c):
                    for k in range(KC):
                        nc.vector.bn_stats(st[:, k, c, :], XN[:, k, c * CH:(c + 1) * CH]).then_inc(s_ls, 1)

                for t in range(1, NT, 2):
                    dve.wait_ge(s_xt, b * NT + (t + 1))
                    dve.wait_ge(s_xe, b * NT + (CREDIT + t))
                    nc.vector.tensor_copy(XN[:, :, t * P:(t + 1) * P],
                                          TP[:, t % 2, :].rearrange("p (k n) -> p k n", k=KC)).then_inc(s_xe, 1)
                    if t % 6 == 5:
                        chunk(t // 3 - 1)
                        dve.wait_ge(s_xe, b * NT + (CREDIT + t + 1))
                        chunk(t // 3)

            def norm(b, layer):
                d0 = b * 2 + layer
                s0 = b * (3 * KC) + layer * KC
                for k in range(KC if layer else 0):
                    for c in range(NCH):
                        ins = nc.vector.bn_stats(st[:, k, c, :], XN[:, k, c * CH:(c + 1) * CH])
                    ins.then_inc(s_bn, 1)
                if layer:
                    hold(dve, s_bn, s0 + KC)
                    s0 = s0 + KC
                else:
                    hold(dve, s_ls, b * (NCH * KC) + NCH * KC)
                for k in range(KC):
                    nc.vector.bn_aggr(mv[:, k, :], st[:, k, :, :]).then_inc(s_bn, 1)
                hold(dve, s_bn, s0 + KC)
                dve.engine_nop().then_inc(s_st, 1)
                dve.wait_ge(s_gp, d0 * 2 + 1)
                nc.vector.tensor_copy(gm[:, :], SC[:, 0:KC]).then_inc(s_st, 1)
                dve.wait_ge(s_st, d0 * 6 + 2)
                nc.vector.tensor_tensor(dv[:, :], mv[:, :, 0], gm[:, :], ALU.subtract).then_inc(s_st, 1)
                dve.wait_ge(s_st, d0 * 6 + 3)
                nc.vector.tensor_tensor(sd[:, :], dv[:, :], dv[:, :], ALU.mult).then_inc(s_sqr, 1)
                dve.wait_ge(s_sqr, d0 + 1)
                nc.vector.tensor_tensor(dv[:, :], sd[:, :], mv[:, :, 1], ALU.add).then_inc(s_st, 1)
                dve.wait_ge(s_gp, d0 * 2 + 2)
                nc.vector.tensor_copy(dv[:, :], SC[:, 512:512 + KC]).then_inc(s_st, 1)
                dve.wait_ge(s_sq, d0 + 1)
                nc.vector.reciprocal(rstd[:, :], sd[:, :]).then_inc(s_st, 1)
                dve.wait_ge(s_st, d0 * 6 + 6)
                dve.wait_ge(s_save, b * SAVES + (SAVES if layer else 3 * 16))
                for k in range(KC):
                    nc.vector.tensor_scalar(XN[:, k, :], XN[:, k, :], gm[:, k:k + 1], rstd[:, k:k + 1],
                                            ALU.subtract, ALU.mult)

            def proj(kind, b, g):
                gi = group_index(kind, b, g)
                if kind == "causal":
                    bias_operand(nc.vector, g, 0)
                for n in range(2 * NCH):
                    c, m = n // 2, 1 - n % 2
                    dve.wait_ge(s_hi, gi * (2 * NCH) + (n + 1))
                    src = SC[:, (n % 3) * 512:(n % 3) * 512 + CH]
                    hi = (QH, KH)[m][:, c * CH:(c + 1) * CH]
                    lo = (QL, KL)[m][:, c * CH:(c + 1) * CH]
                    if kind == "na" and m == 0:
                        src = src.rearrange("p (r w c) -> p w r c", w=CW, c=QW)
                        hi = hi.rearrange("p (w r c) -> p w r c", w=CW, c=QW)
                        lo = lo.rearrange("p (w r c) -> p w r c", w=CW, c=QW)
                    if kind == "causal":
                        ins = nc.vector.tensor_tensor(lo, src, hi.bitcast(F32), ALU.subtract)
                    else:
                        parts = [(lo, src, hi)] if kind != "na" or m else [
                            (lo[:, w], src[:, w], hi[:, w]) for w in range(CW)]
                        for lo_, src_, hi_ in parts:
                            ins = nc.vector.scalar_tensor_tensor(
                                out=lo_, in0=src_, scalar=bsel[:, m:m + 1], in1=hi_.bitcast(F32),
                                op0=ALU.add, op1=ALU.subtract)
                    ins.then_inc(s_lo, 1)
                v0 = gi * NV
                for n, (t0, w) in enumerate(V_BANKS):
                    if kind == "self":
                        dve.wait_ge(s_vh, (b * G0 + g) * NV + (n + 1))
                        hi, lo, src = v_split(n, t0, w)
                        nc.vector.tensor_tensor(lo, src, hi.bitcast(F32), ALU.subtract).then_inc(s_pe, 1)
                        continue
                    if n % 2 == 0:
                        continue
                    dve.wait_ge(s_pv, v0 + (n + 1))
                    dve.wait_ge(s_pe, v0 + n)
                    nc.vector.tensor_copy(*v_copy(kind, n, t0, w)).then_inc(s_pe, 1)

            def na(b, g):
                n0 = b * (G0 * H0 * NT) + g * (H0 * NT)
                with dve.Fori(0, H0 // 2) as hp:
                    m0 = n0 + hp * (2 * NT)
                    k0 = (b * (G0 * H0) + g * H0 + hp * 2) * NTAB

                    def norm_out(n):
                        e, t = n % RING, NA_TILES[n % NT][0]
                        dve.wait_ge(n_pv, m0 + (n + 1))
                        nc.vector.reciprocal(rden[:, e:e + 1], rsum[:, e, 0:1]).then_inc(n_rd, 1)
                        dve.wait_ge(n_rd, m0 + (n + 1))
                        head = hp * (2 * D0) + (n // NT) * D0
                        nc.vector.tensor_scalar(
                            YT[:, t, bass.ds(g * P + head, D0)], OV_NA[n % 2][:, bass.ds(head, D0)],
                            rden[:, e:e + 1], None, ALU.mult).then_inc(n_nr, 1)

                    for n in range(2 * NT):
                        t, cw, cls, lo, nb = NA_TILES[n % NT]
                        tb = (n // NT) * NTAB + NA_TABLE_OF[n % NT]
                        if n >= RING:
                            norm_out(n - RING)
                        dve.wait_ge(n_sc, m0 + (n + 1))
                        hold(dve, n_tab, k0 + (tb + 1))
                        w = nb * BAND
                        nc.vector.tensor_tensor_reduce(
                            out=Pb[:, (n % 4) * 512:(n % 4) * 512 + w].rearrange("p (r c) -> p r c", c=BW),
                            in0=SC[:, (n % RING) * 512:(n % RING) * 512 + w].rearrange("p (r c) -> p r c", c=BW),
                            in1=tab[:, tb % TAB_RING, 0:nb * BR, :], scale=1.0, scalar=-3e38,
                            op0=ALU.add, op1=ALU.max, accum_out=cmax[:, n % 2:n % 2 + 1]).then_inc(n_ad, 1)
                        dve.wait_ge(n_ad, m0 + (CREDIT + n + 1))
                        nc.vector.tensor_scalar(nmax[:, n % RING:n % RING + 1], cmax[:, n % 2:n % 2 + 1], -1.0, None,
                                                ALU.mult).then_inc(n_nm, 1)
                    for n in range(2 * NT - RING, 2 * NT):
                        norm_out(n)

            def selfa(b, g):
                gi = b * G0 + g
                u0 = gi * UNITS
                nc.vector.memset(MM.ap().bitcast(F32), 0.0)

                i0 = gi * ITEMS

                def item(kind, u, n):
                    at = RING_AT[kind, u, n]
                    bank = AM[at % 2]
                    dve.wait_ge(f_am, i0 + (at + 1))
                    if kind == "row":
                        q0 = (u % 3) * CH + n * P
                        nc.vector.tensor_copy(QS[3 * D0:4 * D0, 0, q0:q0 + P], bank[0:D0, 0:P]).then_inc(f_cm, 1)
                    elif kind == "out":
                        j, c = u // NCH, u % NCH
                        tiles = bank[:, 0:CH].rearrange("p (t n) -> p t n", n=P)
                        nc.vector.reciprocal(urec[:, :], tiles[:, :, VW - 1])
                        nc.vector.tensor_reduce(un.ap(), tiles[:, :, 0:2 * D0].rearrange(
                            "p t (h n) -> p t n h", h=2), AX.X, ALU.add).then_inc(f_cm, 1)
                        dve.wait_ge(f_cm, i0 + (CREDIT + at + 1))
                        scale = urec[:, :].rearrange("p (t o) -> p t o", o=1).to_broadcast([P, UT, D0])
                        nc.vector.tensor_tensor(
                            YT[:, c * UT:(c + 1) * UT, bass.ds((G0 + g) * P + j * D0, D0)], un.ap(), scale,
                            ALU.mult).then_inc(f_nr, 1)
                    else:
                        c = n % NC0
                        nc.vector.tensor_reduce(cmax[:, c:c + 1], bank[:, 0:SELF_CHUNKS[c][1]],
                                                AX.X, ALU.max).then_inc(f_cm, 1)
                        if c == NC0 - 1:
                            e, t = (u * UT + n // NC0) % 2, (u0 + u) * UT + (n // NC0 + 1)
                            dve.wait_ge(f_cm, i0 + (CREDIT + at + 1))
                            for dst in (um[:, e:e + 1], MM[:, e, 0:1]):
                                nc.vector.tensor_reduce(dst, cmax[:, 0:NC0], AX.X, ALU.max, negate=True)\
                                    .then_inc(f_um, 1)
                            dve.wait_ge(f_um, 2 * t)
                            nc.vector.tensor_tensor(MM[:, e, 1:2], um[:, e:e + 1], MM[:, e, 0:1].bitcast(F32),
                                                    ALU.subtract).then_inc(f_ml, 1)

                def low(n):
                    dve.wait_ge(f_eh, u0 * PAIRS + (CREDIT + n + 1))
                    nc.vector.tensor_tensor(PLO[:, n % 3, 0:LD], Pb[:, (n % 3) * 2 * CH:(n % 3) * 2 * CH + LD],
                                            PHI[:, n % 3, 0:LD].bitcast(F32), ALU.subtract).then_inc(f_ld, 1)

                for it in AHEAD:
                    item(*it)
                for n in range(UNITS * PAIRS):
                    items = beside(n // PAIRS, n % PAIRS)
                    for it in items[:1]:
                        item(*it)
                    if n >= 1:
                        low(n - 1)
                    for it in items[1:]:
                        item(*it)
                low(UNITS * PAIRS - 1)
                item("out", UNITS - 1, None)

            def causal(b, g):
                gi = b * G1 + g
                k0, t0 = gi * NK, gi * TILES1
                def maximum(n, c):
                    chunks, at = len(L1_CHUNKS[n % NT]), CHUNK_AT[n, c]
                    dve.wait_ge(c_sc, k0 + (at + 1))
                    o, m = (at % BANKS) * 512, n % 2 * NC0
                    nc.vector.tensor_reduce(cmax[:, m + c:m + c + 1], SC[:, o:o + L1_CHUNKS[n % NT][c][1]], AX.X,
                                            ALU.max).then_inc(c_cm, 1)
                    if c == chunks - 1:
                        dve.wait_ge(c_cm, k0 + (at + 1))
                        nc.vector.tensor_reduce(nmax[:, n % RING:n % RING + 1], cmax[:, m:m + chunks], AX.X, ALU.max,
                                                negate=True).then_inc(c_nm, 1)

                def out_of(n):
                    e, j = n % 2, n // NT
                    last = CHUNK_AT[n, len(L1_CHUNKS[n % NT]) - 1]
                    dve.wait_ge(c_pv, k0 + (CREDIT + last + 1))
                    nc.vector.reciprocal(rden[:, e:e + 1], OV[:, P:P + 1]).then_inc(c_rd, 1)
                    dve.wait_ge(c_rd, t0 + (n + 1))
                    nc.vector.tensor_scalar(YT[:, n % NT, bass.ds(g * P + j * D1, D1)], OV[:, j * D1:(j + 1) * D1],
                                            rden[:, e:e + 1], None, ALU.mult).then_inc(c_nr, 1)

                for kind, *step in ORDER1["dve"]:
                    {"maximum": maximum, "out": out_of}[kind](*step)

            def outp(b, layer):
                n0 = b * (2 * NCH * KC) + layer * NCH * KC
                for c in range(NCH):
                    for m in range(KC):
                        n = c * KC + m
                        dve.wait_ge(s_om, n0 + (n + 1))
                        dve.wait_ge(s_or[n % 2], n0 * 8 + 16 * (n // 2 + 1))
                        dst = XN[:, m, :].rearrange("p (c r) -> p r c", r=HW)[:, c * QR:(c + 1) * QR, :]
                        src = SC[:, (n % 4) * 512:(n % 4) * 512 + CH].rearrange("p (r c) -> p r c", c=HW)
                        add = res[:, n % 2, :].rearrange("p (r c) -> p r c", c=HW)
                        if layer == 0:
                            nc.vector.scalar_tensor_tensor(out=dst, in0=src, scalar=bproj[:, m:m + 1], in1=add,
                                                           op0=ALU.add, op1=ALU.add).then_inc(s_oa, 1)
                        else:
                            nc.vector.tensor_tensor(dst, src, add, ALU.add).then_inc(s_oa, 1)

            def final(b):
                for t in range(1, NT, 2):
                    dve.wait_ge(s_ft, b * NT + (t + 1))
                    dve.wait_ge(s_fe, b * NT + t)
                    nc.vector.tensor_copy(YT[:, t, :], TP[:, t % 2, :]).then_inc(s_fe, 1)

            run_phases(dve, setup, load, norm, proj, na, selfa, causal, outp, final)

        @block.gpsimd
        def _(pool):
            def proj(kind, b, g):
                gi = group_index(kind, b, g)
                hold(pool, s_w, gi * 16 + 16)
                q = Wg[:, :, 0:P]
                scale = SCALE1 if kind == "causal" else SCALE0
                nc.gpsimd.tensor_scalar(q, q, scale, None, ALU.mult).then_inc(s_ws, 1)
                o0 = b * (3 * G0 + G1) + (g * 3 if kind == "self" else g + 3 * G0)
                if kind == "causal":
                    hold(pool, s_ws, gi + 1)
                    nc.gpsimd.memset(VC[:, :, P:V1W], 1.0).then_inc(s_one, 1)
                if kind == "self":
                    hold(pool, s_ws, gi + 1)
                    nc.gpsimd.memset(VX[:, :, :, 2 * D0:VW].bitcast(F32), 1.0).then_inc(s_one, 1)
                    for slot in range(2):
                        hold(pool, s_one, o0 + (slot + 1))
                        nc.gpsimd.memset(KST[3 * D0:4 * D0, slot, :].bitcast(F32), 1.0).then_inc(s_one, 1)

            def na(b, g):
                h0 = b * (G0 * H0) + g * H0
                n0 = b * (G0 * H0 * NT) + g * (H0 * NT)
                for j in range(H0):
                    hold(pool, n_tt[j % 2], (b * G0 + g) * (H0 // 2 * 16) + (j // 2 + 1) * 16)
                    for x, (cw, cls, nb, n) in enumerate(NA_TABLES):
                        r0 = BR if cls == 0 else 0
                        c0 = 6 - (QW * cw - COL0[cw])
                        k = j * NTAB + x
                        nr = nb * BR
                        if k:
                            hold(pool, n_tab, h0 * NTAB + k)
                        rows = rowm[:, cls, 0:nr].rearrange("p (r o) -> p r o", o=1).to_broadcast([P, nr, BW])
                        nc.gpsimd.tensor_tensor(tmpt[:, 0:nr, 0:BW], TT[:, j % 2, r0:r0 + nr, c0:c0 + BW],
                                                rows, ALU.add).then_inc(n_tmp, 1)
                        hold(pool, n_tmp, h0 * NTAB + (k + 1))
                        if k >= TAB_RING:
                            kk = k - TAB_RING + 1
                            done = (kk // NTAB) * NT + NA_TABLES[kk % NTAB][3]
                            hold(pool, n_ad, n0 + (CREDIT + done))
                        cols = colm[:, cw:cw + 1, :].to_broadcast([P, nr, BW])
                        nc.gpsimd.tensor_tensor(tab[:, k % TAB_RING, 0:nr, :], tmpt[:, 0:nr, 0:BW], cols,
                                                ALU.add).then_inc(n_tab, 1)

            def causal(b, g):
                for i in range(H1):
                    hold(pool, s_stk[i], stk_base("causal", b, g) + STK_C)
                bias_operand(nc.gpsimd, g, 1)

            def selfa(b, g):
                n0 = (b * G0 + g) * (UNITS * PAIRS)
                for n in range(UNITS * PAIRS):
                    hold(pool, f_eh, n0 + (CREDIT + n + 1))
                    o = (n % 3) * 2 * CH
                    nc.gpsimd.tensor_tensor(PLO[:, n % 3, LD:2 * CH], Pb[:, o + LD:o + 2 * CH],
                                            PHI[:, n % 3, LD:2 * CH].bitcast(F32), ALU.subtract)\
                        .then_inc(f_lp, 1)

            run_phases(pool, nothing, nothing, nothing, proj, na, selfa, causal, nothing, nothing)


def constants():
    f = np.float32
    c = {"ident": np.eye(P, dtype=f), "rev": np.eye(P, dtype=f)[::-1].copy(),
         "avg": np.kron(np.eye(P // 16, dtype=f), np.full((16, 16), 1 / 16, f))}
    qoh = np.zeros((P, 3, P), f)
    for phase in range(3):
        for p in range(P):
            tok = P * phase + p
            r = tok // HW - P * phase // HW
            for base in (0, 64):
                qoh[base + HW - 1 - tok % HW, phase, p] = 1
                qoh[base + HW + 3 - r, phase, p] = 1
    c["qoh"] = qoh.reshape(P, 3 * P)
    tmask = np.zeros((P, NU), f)
    for r in range(4):
        for base in (0, 64):
            tmask[base + HW + 3 - r, HW - 1 + r + 1:] = -BIG
    c["tmask"] = tmask

    def outside(q, key):
        first = min(max(q - KS // 2, 0), HW - KS)
        return not first <= key < first + KS

    rowm, colm = np.zeros((P, 3, 16), f), np.zeros((P, 3, BW), f)
    for p in range(P):
        for cls, (q0, w0) in enumerate(((0, 0), (QR, QR - BR), (HW - QR, HW - QR - BR))):
            for k in range(16):
                rowm[p, cls, k] = -BIG if outside(q0 + p // QW, w0 + k) else 0
        for cw in range(CW):
            for k in range(BW):
                colm[p, cw, k] = -BIG if outside(QW * cw + p % QW, COL0[cw] + k) else 0
    c["rowm"], c["colm"] = rowm, colm
    return c


def kernel(**inputs):
    import concourse.bacc as bacc
    from concourse.bass_utils import run_bass_kernel_spmd

    arr = {k: np.asarray(v) for k, v in inputs.items()}
    x = arr["x"].reshape(B, T, C)
    wqkv = arr["L0_conv_W_qkv"].reshape(KC, P, 2, 3, 2, P)
    w0 = wqkv.transpose(2, 4, 1, 0, 3, 5).reshape(2 * G0, P, KC, 3 * P)
    w1 = np.stack([arr["L1_conv_Wq"], arr["L1_conv_Wk"], arr["L1_conv_Wv"]]).reshape(3, KC, P, G1, P)
    w1 = w1.transpose(3, 2, 1, 0, 4).reshape(G1, P, KC, 3 * P)
    wo = np.stack([arr["L0_conv_W_proj"], arr["L1_conv_Wo"]]).reshape(2, KC, P, C).transpose(0, 2, 1, 3)
    bqkv = arr["L0_conv_b_qkv"].reshape(2, 3, 2, P).transpose(3, 0, 2, 1).reshape(P, 2 * G0, 3)
    given = {"x": x, "wgrp": np.concatenate([w0, w1, w0[:1]]), "wo": wo, "bqkv": bqkv,
             "bproj": arr["L0_conv_b_proj"].reshape(KC, P).T, "rpb": arr["L0_conv_rpb"],
             "relt": arr["L1_conv_rel_pos_bias"].T, "relp": arr["L1_conv_particle_rel_pos_bias"].T,
             **constants()}
    given = {k: np.ascontiguousarray(v) for k, v in given.items()}
    nc = bacc.Bacc("TRN2", target_bir_lowering=False, num_devices=1)
    a = {k: nc.dram_tensor(f"in_{k}", v.shape, F32, kind="ExternalInput").ap() for k, v in given.items()}
    a["out"] = nc.dram_tensor("out", (B, T, C), F32, kind="ExternalOutput").ap()
    build(nc, a)
    r = run_bass_kernel_spmd(nc, [{f"in_{k}": v for k, v in given.items()}], core_ids=[0])
    return np.asarray(r.results[0]["out"]).reshape(B, HW, HW, C)
```
